# Optimizing a Trainium2 kernel written in Bass

```python
import numpy as np
import jax
import jax.numpy as jnp

def _softmax(x, axis=-1):
    return jax.nn.softmax(x, axis=axis)

def _gelu(x):
    return jax.nn.gelu(x, approximate=True)

def _silu(x):
    return jax.nn.silu(x)

def _sigmoid(x):
    return jax.nn.sigmoid(x)

def _layernorm(x, axis=-1, eps=1e-05):
    m = jnp.mean(x, axis=axis, keepdims=True)
    v = jnp.var(x, axis=axis, keepdims=True)
    return (x - m) / jnp.sqrt(v + eps)

def _scatter_add(tgt, idx, src, axis=0):
    return tgt.at[idx].add(src)

def _segment_sum(src, seg, n):
    return jax.ops.segment_sum(src, seg, n)
kernel_name = 'mk_xattn_ffn_d4_seqx_r4_9c0a28'

def setup_inputs(seed: int=0):
    np.random.seed(seed)
    _w = jnp.asarray

    def _rec_inputs():
        import jax
        import jax.numpy as jnp
        _rk = jax.random.key(seed)
        x = -0.0003929 + 0.9999 * jax.random.normal(jax.random.fold_in(_rk, 1), (2, 1024, 256), jnp.float32)
        _lenS = 1024 - jax.random.randint(jax.random.fold_in(_rk, 7), (2,), 0, max(1, 1024 // 4) + 1, jnp.int32)
        _lenS2 = 77 - jax.random.randint(jax.random.fold_in(_rk, 8), (2,), 0, max(1, 77 // 4) + 1, jnp.int32)
        _ctx_512P = jax.random.normal(jax.random.fold_in(_rk, 11), (2, 16, 128), jnp.float32)
        _ctx_512c = jax.random.dirichlet(jax.random.fold_in(_rk, 511), 0.3 * jnp.ones((16,), jnp.float32), (2, 77))
        _ctx_512t = jnp.einsum('bsk,bkd->bsd', _ctx_512c, _ctx_512P)
        _ctx_512t = _ctx_512t * jax.lax.rsqrt(jnp.mean(jnp.square(_ctx_512t)) + 1e-12) * 0.953939
        ctx_512 = -1.39393e-06 + 0.999914 * (_ctx_512t + 0.3 * jax.random.normal(jax.random.fold_in(_rk, 611), (2, 77, 128), jnp.float32))
        return (x, ctx_512)
    x, ctx_512 = _rec_inputs()

    def _L0_xattn_setup():
        import jax, jax.numpy as jnp
        import numpy as np
        HEADS = 16
        D_MODEL = 256
        IMG_MODEL = 128
        D_K = D_MODEL // HEADS
        key = jax.random.key(seed)
        ks = jax.random.split(key, 12)
        B, LQ, LKV = (8, 512, 256)
        s_dm = 1.0 / np.sqrt(D_MODEL)
        s_im = 1.0 / np.sqrt(IMG_MODEL)
        return {'q': jax.random.normal(ks[0], (B, LQ, D_MODEL), jnp.float32), 'k': jax.random.normal(ks[1], (B, LKV, IMG_MODEL), jnp.float32), 'v': jax.random.normal(ks[2], (B, LKV, IMG_MODEL), jnp.float32), 'Wq': jax.random.normal(ks[3], (D_MODEL, D_MODEL), jnp.float32) * s_dm, 'bq': jnp.zeros((D_MODEL,), jnp.float32), 'Wk': jax.random.normal(ks[4], (IMG_MODEL, D_MODEL), jnp.float32) * s_im, 'bk': jnp.zeros((D_MODEL,), jnp.float32), 'Wv': jax.random.normal(ks[5], (IMG_MODEL, D_MODEL), jnp.float32) * s_im, 'bv': jnp.zeros((D_MODEL,), jnp.float32), 'Wo': jax.random.normal(ks[6], (D_MODEL, D_MODEL), jnp.float32) * s_dm, 'bo': jnp.zeros((D_MODEL,), jnp.float32)}
    _L0_xattn_all = _L0_xattn_setup()
    _L0_xattn_in = {k: v for k, v in _L0_xattn_all.items() if k in ('Wq', 'bq', 'Wk', 'bk', 'Wv', 'bv', 'Wo', 'bo')}
    del _L0_xattn_all

    def _L0_ffn_setup():
        import jax, jax.numpy as jnp
        import numpy as np
        NUM_EXPERTS = 8
        HIDDEN = 256
        INTER = 256
        BATCH = 2
        SEQ = 256
        TOP_K = 2
        SWIGLU_ALPHA = 1.702
        LIMIT = 7.0

        def _grouped_mm(x, w, expert_ids):
            onehot = jax.nn.one_hot(expert_ids, w.shape[0], dtype=x.dtype)
            y_all = jnp.einsum('tk,ekn->etn', x, w)
            return jnp.einsum('te,etn->tn', onehot, y_all)

        def _gpt_oss_swiglu(x):
            gate = jnp.minimum(x[..., ::2], LIMIT)
            up = jnp.clip(x[..., 1::2], -LIMIT, LIMIT)
            glu = gate * jax.nn.sigmoid(gate * SWIGLU_ALPHA)
            return (up + 1.0) * glu
        key = jax.random.key(seed)
        ks = jax.random.split(key, 7)
        hidden_states = jax.random.normal(ks[0], (BATCH, SEQ, HIDDEN), jnp.float32)
        router_indices = jax.random.randint(ks[1], (BATCH * SEQ, TOP_K), 0, NUM_EXPERTS)
        routing_weights = jax.nn.softmax(jax.random.normal(ks[2], (BATCH * SEQ, NUM_EXPERTS), jnp.float32), axis=-1)
        scale = 0.02
        gate_up_proj = jax.random.normal(ks[3], (NUM_EXPERTS, HIDDEN, 2 * INTER), jnp.float32) * scale
        gate_up_proj_bias = jax.random.normal(ks[4], (NUM_EXPERTS, 2 * INTER), jnp.float32) * scale
        down_proj = jax.random.normal(ks[5], (NUM_EXPERTS, INTER, HIDDEN), jnp.float32) * scale
        down_proj_bias = jax.random.normal(ks[6], (NUM_EXPERTS, HIDDEN), jnp.float32) * scale
        return {'hidden_states': hidden_states, 'router_indices': router_indices, 'routing_weights': routing_weights, 'gate_up_proj': gate_up_proj, 'gate_up_proj_bias': gate_up_proj_bias, 'down_proj': down_proj, 'down_proj_bias': down_proj_bias}
    _L0_ffn_all = _L0_ffn_setup()
    _L0_ffn_in = {k: v for k, v in _L0_ffn_all.items() if k in ('router_indices', 'routing_weights', 'gate_up_proj', 'gate_up_proj_bias', 'down_proj', 'down_proj_bias')}
    del _L0_ffn_all

    def _L1_xattn_setup():
        import jax, jax.numpy as jnp
        import numpy as np
        H, D, C1, C2, S, M, B, W = (16, 32, 256, 128, 512, 128, 2, 4)

        def _ln(x, g, b):
            m = jnp.mean(x, -1, keepdims=True)
            v = jnp.var(x, -1, keepdims=True)
            return (x - m) * jax.lax.rsqrt(v + 1e-05) * g + b

        def _mha(x, y, wq, wk, wv, li1_w, li1_b, lnx_g, lnx_b, lny_g, lny_b, ln3_g, ln3_b, li2_w, li2_b, li3_w, li3_b, causal):
            xn = _ln(x, lnx_g, lnx_b)
            yn = _ln(y, lny_g, lny_b)
            q = jnp.einsum('bsc,hcd->bhsd', xn, wq)
            k = jnp.einsum('btc,hcd->bhtd', yn, wk)
            v = jnp.einsum('btc,hcd->bhtd', yn, wv)
            a = jax.nn.softmax(jnp.einsum('bhsd,bhtd->bhst', q, k) * D ** (-0.5), axis=-1)
            if causal:
                s, t = (a.shape[-2], a.shape[-1])
                mask = (jnp.arange(t)[None, :] > jnp.arange(s)[:, None]).astype(a.dtype)
                a = a * mask
            o = jnp.einsum('bhst,bhtd->bhsd', a, v)
            o = o.transpose(0, 2, 1, 3).reshape(x.shape[0], x.shape[1], H * D)
            x_out = x + o @ li1_w + li1_b
            h = jax.nn.gelu(_ln(x_out, ln3_g, ln3_b) @ li2_w + li2_b, approximate=False)
            return x_out + h @ li3_w + li3_b
        key = jax.random.key(seed)
        ks = iter(jax.random.split(key, 64))

        def w(shape, scale=0.02):
            return jax.random.normal(next(ks), shape, jnp.float32) * scale
        inp = {'xx': jax.random.normal(next(ks), (B, S, C1), jnp.float32), 'ee': jax.random.normal(next(ks), (B, M, C2), jnp.float32), 'ln1_g': jnp.ones(C1, jnp.float32), 'ln1_b': jnp.zeros(C1, jnp.float32), 'ln2_g': jnp.ones(C1, jnp.float32), 'ln2_b': jnp.zeros(C1, jnp.float32)}
        for pfx, cy in (('a1', C1), ('a2', C2)):
            inp[pfx + '_wq'] = w((H, C1, D))
            inp[pfx + '_wk'] = w((H, cy, D))
            inp[pfx + '_wv'] = w((H, cy, D))
            inp[pfx + '_li1_w'] = w((H * D, C1))
            inp[pfx + '_li1_b'] = jnp.zeros(C1, jnp.float32)
            inp[pfx + '_lnx_g'] = jnp.ones(C1, jnp.float32)
            inp[pfx + '_lnx_b'] = jnp.zeros(C1, jnp.float32)
            inp[pfx + '_lny_g'] = jnp.ones(cy, jnp.float32)
            inp[pfx + '_lny_b'] = jnp.zeros(cy, jnp.float32)
            inp[pfx + '_ln3_g'] = jnp.ones(C1, jnp.float32)
            inp[pfx + '_ln3_b'] = jnp.zeros(C1, jnp.float32)
            inp[pfx + '_li2_w'] = w((C1, C1 * W))
            inp[pfx + '_li2_b'] = jnp.zeros(C1 * W, jnp.float32)
            inp[pfx + '_li3_w'] = w((C1 * W, C1))
            inp[pfx + '_li3_b'] = jnp.zeros(C1, jnp.float32)
        inp['training'] = 0
        return inp
    _L1_xattn_all = _L1_xattn_setup()
    _L1_xattn_in = {k: v for k, v in _L1_xattn_all.items() if k in ('ln1_g', 'ln1_b', 'ln2_g', 'ln2_b', 'a1_wq', 'a1_wk', 'a1_wv', 'a1_li1_w', 'a1_li1_b', 'a1_lnx_g', 'a1_lnx_b', 'a1_lny_g', 'a1_lny_b', 'a1_ln3_g', 'a1_ln3_b', 'a1_li2_w', 'a1_li2_b', 'a1_li3_w', 'a1_li3_b', 'a2_wq', 'a2_wk', 'a2_wv', 'a2_li1_w', 'a2_li1_b', 'a2_lnx_g', 'a2_lnx_b', 'a2_lny_g', 'a2_lny_b', 'a2_ln3_g', 'a2_ln3_b', 'a2_li2_w', 'a2_li2_b', 'a2_li3_w', 'a2_li3_b')}
    del _L1_xattn_all

    def _L1_ffn_setup():
        import jax, jax.numpy as jnp
        import numpy as np
        import math
        N_EXP = 8
        TOP_K = 2
        CAPACITY_FACTOR = 1.25

        def _capacity(num_tokens):
            cap = math.floor(TOP_K * CAPACITY_FACTOR * num_tokens / N_EXP)
            cap += cap % 2
            return int(cap)
        key = jax.random.key(seed)
        k1, k2, k3, k4 = jax.random.split(key, 4)
        B, C, d = (4, 256, 256)
        x = jax.random.normal(k1, (B, C, d), dtype=jnp.float32)
        w_g = jax.random.normal(k2, (d, N_EXP), dtype=jnp.float32) * 0.02
        c_fc = jax.random.normal(k3, (N_EXP, d, 4 * d), dtype=jnp.float32) * 0.02
        c_proj = jax.random.normal(k4, (N_EXP, 4 * d, d), dtype=jnp.float32) * 0.02
        return {'x': x, 'w_g': w_g, 'c_fc': c_fc, 'c_proj': c_proj}
    _L1_ffn_all = _L1_ffn_setup()
    _L1_ffn_in = {k: v for k, v in _L1_ffn_all.items() if k in ('w_g', 'c_fc', 'c_proj')}
    del _L1_ffn_all

    def _L2_xattn_setup():
        import jax, jax.numpy as jnp
        import numpy as np
        DIM = 256
        LATENT_DIM = 128
        NUM_HEADS = 16
        HEAD_DIM = DIM // NUM_HEADS
        SCALE = HEAD_DIM ** (-0.5)
        key = jax.random.key(seed)
        k1, k2, k3, k4, k5 = jax.random.split(key, 5)
        B, xN, zN = (2, 512, 512)
        x = jax.random.normal(k1, (B, xN, DIM), dtype=jnp.float32)
        z = jax.random.normal(k2, (B, zN, LATENT_DIM), dtype=jnp.float32)
        Wq = jax.random.normal(k3, (DIM, DIM), dtype=jnp.float32) * DIM ** (-0.5)
        Wkv = jax.random.normal(k4, (2 * DIM, LATENT_DIM), dtype=jnp.float32) * LATENT_DIM ** (-0.5)
        Wo = jax.random.normal(k5, (DIM, DIM), dtype=jnp.float32) * DIM ** (-0.5)
        return {'x': x, 'z': z, 'Wq': Wq, 'Wkv': Wkv, 'Wo': Wo}
    _L2_xattn_all = _L2_xattn_setup()
    _L2_xattn_in = {k: v for k, v in _L2_xattn_all.items() if k in ('Wq', 'Wkv', 'Wo')}
    del _L2_xattn_all

    def _L2_ffn_setup():
        import jax, jax.numpy as jnp
        import numpy as np
        DIM = 256
        DEPTH = 2
        HEADS = 8
        DIM_HEAD = 64
        WINDOW = 128
        INNER = HEADS * DIM_HEAD
        HID = int(DIM * 4 * 2 / 3)
        B, N = (2, 2048)
        QK_SCALE = 8.0

        def shift_token(t):
            t1, t2 = jnp.split(t, 2, axis=-1)
            t2 = jnp.pad(t2, ((0, 0), (1, 0), (0, 0)))[:, :-1]
            return jnp.concatenate([t1, t2], axis=-1)

        def l2norm(t):
            return t / jnp.clip(jnp.linalg.norm(t, axis=-1, keepdims=True), 1e-12)

        def rotate_half(x):
            x1, x2 = jnp.split(x, 2, axis=-1)
            return jnp.concatenate([-x2, x1], axis=-1)

        def rotary_xpos(q, k):
            n = q.shape[-2]
            half_idx = jnp.arange(0, DIM_HEAD, 2, dtype=jnp.float32)
            inv_freq = 1.0 / 10000.0 ** (half_idx / DIM_HEAD)
            t = jnp.arange(n, dtype=jnp.float32)
            freqs = t[:, None] * inv_freq[None, :]
            freqs = jnp.concatenate([freqs, freqs], axis=-1)
            base = (half_idx + 0.4 * DIM_HEAD) / (1.4 * DIM_HEAD)
            power = (t - n // 2) / float(WINDOW // 2)
            scale = base[None, :] ** power[:, None]
            scale = jnp.concatenate([scale, scale], axis=-1)
            cos, sin = (jnp.cos(freqs), jnp.sin(freqs))
            q = q * cos * scale + rotate_half(q) * sin * scale
            k = k * cos / scale + rotate_half(k) * sin / scale
            return (q, k)

        def local_attention(q, k, v):
            b, h, n, d = q.shape
            w = n // WINDOW
            bq = q.reshape(b, h, w, WINDOW, d) * QK_SCALE
            bk = k.reshape(b, h, w, WINDOW, d)
            bv = v.reshape(b, h, w, WINDOW, d)

            def look_around(t):
                p = jnp.pad(t, ((0, 0), (0, 0), (1, 0), (0, 0), (0, 0)))
                return jnp.concatenate([p[:, :, :w], p[:, :, 1:]], axis=3)
            bk, bv = (look_around(bk), look_around(bv))
            bt = jnp.arange(n).reshape(w, WINDOW)
            btp = jnp.pad(bt, ((1, 0), (0, 0)), constant_values=-1)
            btk = jnp.concatenate([btp[:w], btp[1:]], axis=1)
            sim = jnp.einsum('bhwid,bhwjd->bhwij', bq, bk)
            i = bt[:, :, None]
            j = btk[:, None, :]
            mask = (i < j) | (i > j + WINDOW) | (j == -1)
            sim = jnp.where(mask, -jnp.finfo(sim.dtype).max, sim)
            attn = jax.nn.softmax(sim, axis=-1)
            out = jnp.einsum('bhwij,bhwjd->bhwid', attn, bv)
            return out.reshape(b, h, n, d)

        def _layer(x, wqkv, qs, ksc, wo, lg, lb, w1, b1, w2, b2):
            b, n, _ = x.shape
            h = shift_token(x)
            qkv = h @ wqkv
            q, k, v = jnp.split(qkv, 3, axis=-1)
            to_heads = lambda t: t.reshape(b, n, HEADS, DIM_HEAD).transpose(0, 2, 1, 3)
            q, k, v = (to_heads(q), to_heads(k), to_heads(v))
            q = l2norm(q) * qs
            k = l2norm(k) * ksc
            q, k = rotary_xpos(q, k)
            o = local_attention(q, k, v)
            o = o.transpose(0, 2, 1, 3).reshape(b, n, INNER)
            x = x + o @ wo
            h = shift_token(x)
            mu = h.mean(-1, keepdims=True)
            var = h.var(-1, keepdims=True)
            h = (h - mu) / jnp.sqrt(var + 1e-05) * lg + lb
            h = h @ w1 + b1
            a, g = jnp.split(h, 2, axis=-1)
            h = a * jax.nn.gelu(g, approximate=False)
            x = x + h @ w2 + b2
            return x
        key = jax.random.key(seed)
        ks = jax.random.split(key, 6)
        return {'x': jax.random.normal(ks[0], (B, N, DIM), jnp.float32), 'wqkv': jax.random.normal(ks[1], (DEPTH, DIM, 3 * INNER), jnp.float32) * 0.02, 'q_scale': jnp.ones((DEPTH, DIM_HEAD), jnp.float32), 'k_scale': jnp.ones((DEPTH, DIM_HEAD), jnp.float32), 'wo': jax.random.normal(ks[2], (DEPTH, INNER, DIM), jnp.float32) * 0.02, 'ln_g': jnp.ones((DEPTH, DIM), jnp.float32), 'ln_b': jnp.zeros((DEPTH, DIM), jnp.float32), 'w1': jax.random.normal(ks[3], (DEPTH, DIM, 2 * HID), jnp.float32) * 0.02, 'b1': jnp.zeros((DEPTH, 2 * HID), jnp.float32), 'w2': jax.random.normal(ks[4], (DEPTH, HID, DIM), jnp.float32) * 0.02, 'b2': jnp.zeros((DEPTH, DIM), jnp.float32)}
    _L2_ffn_all = _L2_ffn_setup()
    _L2_ffn_in = {k: v for k, v in _L2_ffn_all.items() if k in ('wqkv', 'q_scale', 'k_scale', 'wo', 'ln_g', 'ln_b', 'w1', 'b1', 'w2', 'b2')}
    del _L2_ffn_all

    def _L3_xattn_setup():
        import jax, jax.numpy as jnp
        import numpy as np
        B, LQ, LK = (8, 512, 512)
        QD, KD, VD = (256, 128, 128)
        key = jax.random.key(seed)
        ks = jax.random.split(key, 9)
        s = 0.02
        return {'query': jax.random.normal(ks[0], (B, LQ, QD), jnp.float32), 'key': jax.random.normal(ks[1], (B, LK, KD), jnp.float32), 'value': jax.random.normal(ks[2], (B, LK, VD), jnp.float32), 'Wq': jax.random.normal(ks[3], (QD, QD), jnp.float32) * s, 'bq': jnp.zeros((QD,), jnp.float32), 'Wk': jax.random.normal(ks[4], (KD, QD), jnp.float32) * s, 'bk': jnp.zeros((QD,), jnp.float32), 'Wv': jax.random.normal(ks[5], (VD, QD), jnp.float32) * s, 'bv': jnp.zeros((QD,), jnp.float32)}
    _L3_xattn_all = _L3_xattn_setup()
    _L3_xattn_in = {k: v for k, v in _L3_xattn_all.items() if k in ('Wq', 'bq', 'Wk', 'bk', 'Wv', 'bv')}
    del _L3_xattn_all

    def _L3_ffn_setup():
        import jax, jax.numpy as jnp
        import numpy as np
        key = jax.random.key(seed)
        ks = jax.random.split(key, 5)
        B, Sq, M, E, H = (4, 512, 256, 8, 1024)
        x = jax.random.normal(ks[0], (B, Sq, M), dtype=jnp.float32)
        wg = jax.random.normal(ks[1], (M, E), dtype=jnp.float32) * (1.0 / np.sqrt(M))
        w1 = jax.random.normal(ks[2], (E, M, H), dtype=jnp.float32) * (1.0 / np.sqrt(M))
        b1 = jnp.zeros((E, H), dtype=jnp.float32)
        w2 = jax.random.normal(ks[3], (E, H, M), dtype=jnp.float32) * (1.0 / np.sqrt(H))
        b2 = jnp.zeros((E, M), dtype=jnp.float32)
        return {'x': x, 'wg': wg, 'w1': w1, 'b1': b1, 'w2': w2, 'b2': b2}
    _L3_ffn_all = _L3_ffn_setup()
    _L3_ffn_in = {k: v for k, v in _L3_ffn_all.items() if k in ('wg', 'w1', 'b1', 'w2', 'b2')}
    del _L3_ffn_all
    return {'x': x, 'ctx_512': ctx_512, 'L0_xattn_Wq': _L0_xattn_in['Wq'], 'L0_xattn_bq': _L0_xattn_in['bq'], 'L0_xattn_Wk': _L0_xattn_in['Wk'], 'L0_xattn_bk': _L0_xattn_in['bk'], 'L0_xattn_Wv': _L0_xattn_in['Wv'], 'L0_xattn_bv': _L0_xattn_in['bv'], 'L0_xattn_Wo': _L0_xattn_in['Wo'], 'L0_xattn_bo': _L0_xattn_in['bo'], 'L0_ffn_router_indices': _L0_ffn_in['router_indices'], 'L0_ffn_routing_weights': _L0_ffn_in['routing_weights'], 'L0_ffn_gate_up_proj': _L0_ffn_in['gate_up_proj'], 'L0_ffn_gate_up_proj_bias': _L0_ffn_in['gate_up_proj_bias'], 'L0_ffn_down_proj': _L0_ffn_in['down_proj'], 'L0_ffn_down_proj_bias': _L0_ffn_in['down_proj_bias'], 'L1_xattn_ln1_g': _L1_xattn_in['ln1_g'], 'L1_xattn_ln1_b': _L1_xattn_in['ln1_b'], 'L1_xattn_ln2_g': _L1_xattn_in['ln2_g'], 'L1_xattn_ln2_b': _L1_xattn_in['ln2_b'], 'L1_xattn_a1_wq': _L1_xattn_in['a1_wq'], 'L1_xattn_a1_wk': _L1_xattn_in['a1_wk'], 'L1_xattn_a1_wv': _L1_xattn_in['a1_wv'], 'L1_xattn_a1_li1_w': _L1_xattn_in['a1_li1_w'], 'L1_xattn_a1_li1_b': _L1_xattn_in['a1_li1_b'], 'L1_xattn_a1_lnx_g': _L1_xattn_in['a1_lnx_g'], 'L1_xattn_a1_lnx_b': _L1_xattn_in['a1_lnx_b'], 'L1_xattn_a1_lny_g': _L1_xattn_in['a1_lny_g'], 'L1_xattn_a1_lny_b': _L1_xattn_in['a1_lny_b'], 'L1_xattn_a1_ln3_g': _L1_xattn_in['a1_ln3_g'], 'L1_xattn_a1_ln3_b': _L1_xattn_in['a1_ln3_b'], 'L1_xattn_a1_li2_w': _L1_xattn_in['a1_li2_w'], 'L1_xattn_a1_li2_b': _L1_xattn_in['a1_li2_b'], 'L1_xattn_a1_li3_w': _L1_xattn_in['a1_li3_w'], 'L1_xattn_a1_li3_b': _L1_xattn_in['a1_li3_b'], 'L1_xattn_a2_wq': _L1_xattn_in['a2_wq'], 'L1_xattn_a2_wk': _L1_xattn_in['a2_wk'], 'L1_xattn_a2_wv': _L1_xattn_in['a2_wv'], 'L1_xattn_a2_li1_w': _L1_xattn_in['a2_li1_w'], 'L1_xattn_a2_li1_b': _L1_xattn_in['a2_li1_b'], 'L1_xattn_a2_lnx_g': _L1_xattn_in['a2_lnx_g'], 'L1_xattn_a2_lnx_b': _L1_xattn_in['a2_lnx_b'], 'L1_xattn_a2_lny_g': _L1_xattn_in['a2_lny_g'], 'L1_xattn_a2_lny_b': _L1_xattn_in['a2_lny_b'], 'L1_xattn_a2_ln3_g': _L1_xattn_in['a2_ln3_g'], 'L1_xattn_a2_ln3_b': _L1_xattn_in['a2_ln3_b'], 'L1_xattn_a2_li2_w': _L1_xattn_in['a2_li2_w'], 'L1_xattn_a2_li2_b': _L1_xattn_in['a2_li2_b'], 'L1_xattn_a2_li3_w': _L1_xattn_in['a2_li3_w'], 'L1_xattn_a2_li3_b': _L1_xattn_in['a2_li3_b'], 'L1_ffn_w_g': _L1_ffn_in['w_g'], 'L1_ffn_c_fc': _L1_ffn_in['c_fc'], 'L1_ffn_c_proj': _L1_ffn_in['c_proj'], 'L2_xattn_Wq': _L2_xattn_in['Wq'], 'L2_xattn_Wkv': _L2_xattn_in['Wkv'], 'L2_xattn_Wo': _L2_xattn_in['Wo'], 'L2_ffn_wqkv': _L2_ffn_in['wqkv'], 'L2_ffn_q_scale': _L2_ffn_in['q_scale'], 'L2_ffn_k_scale': _L2_ffn_in['k_scale'], 'L2_ffn_wo': _L2_ffn_in['wo'], 'L2_ffn_ln_g': _L2_ffn_in['ln_g'], 'L2_ffn_ln_b': _L2_ffn_in['ln_b'], 'L2_ffn_w1': _L2_ffn_in['w1'], 'L2_ffn_b1': _L2_ffn_in['b1'], 'L2_ffn_w2': _L2_ffn_in['w2'], 'L2_ffn_b2': _L2_ffn_in['b2'], 'L3_xattn_Wq': _L3_xattn_in['Wq'], 'L3_xattn_bq': _L3_xattn_in['bq'], 'L3_xattn_Wk': _L3_xattn_in['Wk'], 'L3_xattn_bk': _L3_xattn_in['bk'], 'L3_xattn_Wv': _L3_xattn_in['Wv'], 'L3_xattn_bv': _L3_xattn_in['bv'], 'L3_ffn_wg': _L3_ffn_in['wg'], 'L3_ffn_w1': _L3_ffn_in['w1'], 'L3_ffn_b1': _L3_ffn_in['b1'], 'L3_ffn_w2': _L3_ffn_in['w2'], 'L3_ffn_b2': _L3_ffn_in['b2']}

def reference(x, ctx_512, L0_xattn_Wq, L0_xattn_bq, L0_xattn_Wk, L0_xattn_bk, L0_xattn_Wv, L0_xattn_bv, L0_xattn_Wo, L0_xattn_bo, L0_ffn_router_indices, L0_ffn_routing_weights, L0_ffn_gate_up_proj, L0_ffn_gate_up_proj_bias, L0_ffn_down_proj, L0_ffn_down_proj_bias, L1_xattn_ln1_g, L1_xattn_ln1_b, L1_xattn_ln2_g, L1_xattn_ln2_b, L1_xattn_a1_wq, L1_xattn_a1_wk, L1_xattn_a1_wv, L1_xattn_a1_li1_w, L1_xattn_a1_li1_b, L1_xattn_a1_lnx_g, L1_xattn_a1_lnx_b, L1_xattn_a1_lny_g, L1_xattn_a1_lny_b, L1_xattn_a1_ln3_g, L1_xattn_a1_ln3_b, L1_xattn_a1_li2_w, L1_xattn_a1_li2_b, L1_xattn_a1_li3_w, L1_xattn_a1_li3_b, L1_xattn_a2_wq, L1_xattn_a2_wk, L1_xattn_a2_wv, L1_xattn_a2_li1_w, L1_xattn_a2_li1_b, L1_xattn_a2_lnx_g, L1_xattn_a2_lnx_b, L1_xattn_a2_lny_g, L1_xattn_a2_lny_b, L1_xattn_a2_ln3_g, L1_xattn_a2_ln3_b, L1_xattn_a2_li2_w, L1_xattn_a2_li2_b, L1_xattn_a2_li3_w, L1_xattn_a2_li3_b, L1_ffn_w_g, L1_ffn_c_fc, L1_ffn_c_proj, L2_xattn_Wq, L2_xattn_Wkv, L2_xattn_Wo, L2_ffn_wqkv, L2_ffn_q_scale, L2_ffn_k_scale, L2_ffn_wo, L2_ffn_ln_g, L2_ffn_ln_b, L2_ffn_w1, L2_ffn_b1, L2_ffn_w2, L2_ffn_b2, L3_xattn_Wq, L3_xattn_bq, L3_xattn_Wk, L3_xattn_bk, L3_xattn_Wv, L3_xattn_bv, L3_ffn_wg, L3_ffn_w1, L3_ffn_b1, L3_ffn_w2, L3_ffn_b2):
    import jax
    import jax.numpy as jnp

    def _L0_xattn_ref(q, k, v, Wq, bq, Wk, bk, Wv, bv, Wo, bo):
        import jax, jax.numpy as jnp
        import numpy as np
        HEADS = 16
        D_MODEL = 256
        IMG_MODEL = 128
        D_K = D_MODEL // HEADS
        B, LQ, _ = q.shape
        LKV = k.shape[1]
        qh = (q @ Wq + bq).reshape(B, LQ, HEADS, D_K).transpose(0, 2, 1, 3)
        kh = (k @ Wk + bk).reshape(B, LKV, HEADS, D_K).transpose(0, 2, 1, 3)
        vh = (v @ Wv + bv).reshape(B, LKV, HEADS, D_K).transpose(0, 2, 1, 3)
        scale = 1.0 / np.sqrt(D_K)
        scores = jnp.einsum('bhqd,bhkd->bhqk', qh, kh) * scale
        attn = jax.nn.softmax(scores, axis=-1)
        out = jnp.einsum('bhqk,bhkd->bhqd', attn, vh)
        concat = out.transpose(0, 2, 1, 3).reshape(B, LQ, D_MODEL)
        return concat @ Wo + bo

    def _L0_ffn_ref(hidden_states, router_indices, routing_weights, gate_up_proj, gate_up_proj_bias, down_proj, down_proj_bias):
        import jax, jax.numpy as jnp
        import numpy as np
        NUM_EXPERTS = 8
        HIDDEN = 256
        INTER = 256
        BATCH = 2
        SEQ = 256
        TOP_K = 2
        SWIGLU_ALPHA = 1.702
        LIMIT = 7.0

        def _grouped_mm(x, w, expert_ids):
            onehot = jax.nn.one_hot(expert_ids, w.shape[0], dtype=x.dtype)
            y_all = jnp.einsum('tk,ekn->etn', x, w)
            return jnp.einsum('te,etn->tn', onehot, y_all)

        def _gpt_oss_swiglu(x):
            gate = jnp.minimum(x[..., ::2], LIMIT)
            up = jnp.clip(x[..., 1::2], -LIMIT, LIMIT)
            glu = gate * jax.nn.sigmoid(gate * SWIGLU_ALPHA)
            return (up + 1.0) * glu
        B = hidden_states.shape[0]
        H = hidden_states.shape[-1]
        x = hidden_states.reshape(-1, H)
        M = x.shape[0]
        top_k = router_indices.shape[1]
        num_experts = gate_up_proj.shape[0]
        topk_weights = jnp.take_along_axis(routing_weights, router_indices, axis=1)
        flat_experts = router_indices.reshape(-1)
        sort_idx = jnp.argsort(flat_experts)
        sorted_pos = sort_idx // top_k
        expert_sorted = flat_experts[sort_idx]
        grouped = x[sorted_pos]
        gate_up = _grouped_mm(grouped, gate_up_proj, expert_sorted)
        gate_up = gate_up + gate_up_proj_bias[expert_sorted]
        inter = _gpt_oss_swiglu(gate_up)
        down = _grouped_mm(inter, down_proj, expert_sorted)
        down = down + down_proj_bias[expert_sorted]
        down = down * topk_weights.reshape(-1)[sort_idx][:, None]
        out = jnp.zeros((M, H), x.dtype).at[sorted_pos].add(down)
        return out.reshape(B, -1, H)

    def _L1_xattn_ref(xx, ee, ln1_g, ln1_b, ln2_g, ln2_b, a1_wq, a1_wk, a1_wv, a1_li1_w, a1_li1_b, a1_lnx_g, a1_lnx_b, a1_lny_g, a1_lny_b, a1_ln3_g, a1_ln3_b, a1_li2_w, a1_li2_b, a1_li3_w, a1_li3_b, a2_wq, a2_wk, a2_wv, a2_li1_w, a2_li1_b, a2_lnx_g, a2_lnx_b, a2_lny_g, a2_lny_b, a2_ln3_g, a2_ln3_b, a2_li2_w, a2_li2_b, a2_li3_w, a2_li3_b, training):
        import jax, jax.numpy as jnp
        import numpy as np
        H, D, C1, C2, S, M, B, W = (16, 32, 256, 128, 512, 128, 2, 4)

        def _ln(x, g, b):
            m = jnp.mean(x, -1, keepdims=True)
            v = jnp.var(x, -1, keepdims=True)
            return (x - m) * jax.lax.rsqrt(v + 1e-05) * g + b

        def _mha(x, y, wq, wk, wv, li1_w, li1_b, lnx_g, lnx_b, lny_g, lny_b, ln3_g, ln3_b, li2_w, li2_b, li3_w, li3_b, causal):
            xn = _ln(x, lnx_g, lnx_b)
            yn = _ln(y, lny_g, lny_b)
            q = jnp.einsum('bsc,hcd->bhsd', xn, wq)
            k = jnp.einsum('btc,hcd->bhtd', yn, wk)
            v = jnp.einsum('btc,hcd->bhtd', yn, wv)
            a = jax.nn.softmax(jnp.einsum('bhsd,bhtd->bhst', q, k) * D ** (-0.5), axis=-1)
            if causal:
                s, t = (a.shape[-2], a.shape[-1])
                mask = (jnp.arange(t)[None, :] > jnp.arange(s)[:, None]).astype(a.dtype)
                a = a * mask
            o = jnp.einsum('bhst,bhtd->bhsd', a, v)
            o = o.transpose(0, 2, 1, 3).reshape(x.shape[0], x.shape[1], H * D)
            x_out = x + o @ li1_w + li1_b
            h = jax.nn.gelu(_ln(x_out, ln3_g, ln3_b) @ li2_w + li2_b, approximate=False)
            return x_out + h @ li3_w + li3_b
        x = _ln(xx, ln1_g, ln1_b)
        x = x + _mha(x, x, a1_wq, a1_wk, a1_wv, a1_li1_w, a1_li1_b, a1_lnx_g, a1_lnx_b, a1_lny_g, a1_lny_b, a1_ln3_g, a1_ln3_b, a1_li2_w, a1_li2_b, a1_li3_w, a1_li3_b, causal=True)
        x = _ln(x, ln2_g, ln2_b)
        return x + _mha(x, ee, a2_wq, a2_wk, a2_wv, a2_li1_w, a2_li1_b, a2_lnx_g, a2_lnx_b, a2_lny_g, a2_lny_b, a2_ln3_g, a2_ln3_b, a2_li2_w, a2_li2_b, a2_li3_w, a2_li3_b, causal=False)

    def _L1_ffn_ref(x, w_g, c_fc, c_proj):
        import jax, jax.numpy as jnp
        import numpy as np
        import math
        N_EXP = 8
        TOP_K = 2
        CAPACITY_FACTOR = 1.25

        def _capacity(num_tokens):
            cap = math.floor(TOP_K * CAPACITY_FACTOR * num_tokens / N_EXP)
            cap += cap % 2
            return int(cap)
        B, C, d = x.shape
        T = B * C
        cap = _capacity(T)
        xt = x.reshape(T, d)
        logits = xt @ w_g
        top_v, top_i = jax.lax.top_k(logits, TOP_K)
        full = jnp.full_like(logits, -jnp.inf)
        full = full.at[jnp.arange(T)[:, None], top_i].set(top_v)
        probs = jax.nn.softmax(full, axis=-1)
        exp_mask = jax.nn.one_hot(top_i, N_EXP, dtype=jnp.int32)
        exp_mask = jnp.transpose(exp_mask, (1, 0, 2))
        exp_rank = jnp.cumsum(exp_mask.reshape(TOP_K * T, N_EXP), axis=0) - 1
        exp_rank = exp_rank.reshape(TOP_K, T, N_EXP)
        exp_mask = exp_mask * (exp_rank < cap).astype(jnp.int32)
        exp_rank = jnp.sum(exp_mask * exp_rank, axis=-1)
        exp_weights = exp_mask.astype(x.dtype) * probs[None]
        rank_oh = jax.nn.one_hot(exp_rank, cap, dtype=x.dtype)
        cb_weight = jnp.einsum('kte,ktc->tec', exp_weights, rank_oh)
        sec_mask = (cb_weight != 0).astype(x.dtype)
        exp_batches = jnp.einsum('tec,td->ecd', sec_mask, xt)
        h = jax.nn.gelu(jnp.einsum('ecd,edf->ecf', exp_batches, c_fc), approximate=False)
        exp_out = jnp.einsum('ecf,efd->ecd', h, c_proj)
        out = cb_weight.reshape(T, N_EXP * cap) @ exp_out.reshape(N_EXP * cap, d)
        return out.reshape(B, C, d)

    def _L2_xattn_ref(x, z, Wq, Wkv, Wo):
        import jax, jax.numpy as jnp
        import numpy as np
        DIM = 256
        LATENT_DIM = 128
        NUM_HEADS = 16
        HEAD_DIM = DIM // NUM_HEADS
        SCALE = HEAD_DIM ** (-0.5)
        B, xN, _ = x.shape
        _, zN, _ = z.shape
        Q = (x @ Wq.T).reshape(B, xN, NUM_HEADS, HEAD_DIM)
        KV = (z @ Wkv.T).reshape(B, zN, 2, NUM_HEADS, HEAD_DIM)
        K = KV[:, :, 0]
        V = KV[:, :, 1]
        attn = jnp.einsum('bqhd,bkhd->bhqk', Q, K) * SCALE
        attn = jax.nn.softmax(attn, axis=-1)
        O = jnp.einsum('bhqk,bkhd->bqhd', attn, V).reshape(B, xN, DIM)
        return O @ Wo.T

    def _L2_ffn_ref(x, wqkv, q_scale, k_scale, wo, ln_g, ln_b, w1, b1, w2, b2):
        import jax, jax.numpy as jnp
        import numpy as np
        DIM = 256
        DEPTH = 2
        HEADS = 8
        DIM_HEAD = 64
        WINDOW = 128
        INNER = HEADS * DIM_HEAD
        HID = int(DIM * 4 * 2 / 3)
        B, N = (2, 2048)
        QK_SCALE = 8.0

        def shift_token(t):
            t1, t2 = jnp.split(t, 2, axis=-1)
            t2 = jnp.pad(t2, ((0, 0), (1, 0), (0, 0)))[:, :-1]
            return jnp.concatenate([t1, t2], axis=-1)

        def l2norm(t):
            return t / jnp.clip(jnp.linalg.norm(t, axis=-1, keepdims=True), 1e-12)

        def rotate_half(x):
            x1, x2 = jnp.split(x, 2, axis=-1)
            return jnp.concatenate([-x2, x1], axis=-1)

        def rotary_xpos(q, k):
            n = q.shape[-2]
            half_idx = jnp.arange(0, DIM_HEAD, 2, dtype=jnp.float32)
            inv_freq = 1.0 / 10000.0 ** (half_idx / DIM_HEAD)
            t = jnp.arange(n, dtype=jnp.float32)
            freqs = t[:, None] * inv_freq[None, :]
            freqs = jnp.concatenate([freqs, freqs], axis=-1)
            base = (half_idx + 0.4 * DIM_HEAD) / (1.4 * DIM_HEAD)
            power = (t - n // 2) / float(WINDOW // 2)
            scale = base[None, :] ** power[:, None]
            scale = jnp.concatenate([scale, scale], axis=-1)
            cos, sin = (jnp.cos(freqs), jnp.sin(freqs))
            q = q * cos * scale + rotate_half(q) * sin * scale
            k = k * cos / scale + rotate_half(k) * sin / scale
            return (q, k)

        def local_attention(q, k, v):
            b, h, n, d = q.shape
            w = n // WINDOW
            bq = q.reshape(b, h, w, WINDOW, d) * QK_SCALE
            bk = k.reshape(b, h, w, WINDOW, d)
            bv = v.reshape(b, h, w, WINDOW, d)

            def look_around(t):
                p = jnp.pad(t, ((0, 0), (0, 0), (1, 0), (0, 0), (0, 0)))
                return jnp.concatenate([p[:, :, :w], p[:, :, 1:]], axis=3)
            bk, bv = (look_around(bk), look_around(bv))
            bt = jnp.arange(n).reshape(w, WINDOW)
            btp = jnp.pad(bt, ((1, 0), (0, 0)), constant_values=-1)
            btk = jnp.concatenate([btp[:w], btp[1:]], axis=1)
            sim = jnp.einsum('bhwid,bhwjd->bhwij', bq, bk)
            i = bt[:, :, None]
            j = btk[:, None, :]
            mask = (i < j) | (i > j + WINDOW) | (j == -1)
            sim = jnp.where(mask, -jnp.finfo(sim.dtype).max, sim)
            attn = jax.nn.softmax(sim, axis=-1)
            out = jnp.einsum('bhwij,bhwjd->bhwid', attn, bv)
            return out.reshape(b, h, n, d)

        def _layer(x, wqkv, qs, ksc, wo, lg, lb, w1, b1, w2, b2):
            b, n, _ = x.shape
            h = shift_token(x)
            qkv = h @ wqkv
            q, k, v = jnp.split(qkv, 3, axis=-1)
            to_heads = lambda t: t.reshape(b, n, HEADS, DIM_HEAD).transpose(0, 2, 1, 3)
            q, k, v = (to_heads(q), to_heads(k), to_heads(v))
            q = l2norm(q) * qs
            k = l2norm(k) * ksc
            q, k = rotary_xpos(q, k)
            o = local_attention(q, k, v)
            o = o.transpose(0, 2, 1, 3).reshape(b, n, INNER)
            x = x + o @ wo
            h = shift_token(x)
            mu = h.mean(-1, keepdims=True)
            var = h.var(-1, keepdims=True)
            h = (h - mu) / jnp.sqrt(var + 1e-05) * lg + lb
            h = h @ w1 + b1
            a, g = jnp.split(h, 2, axis=-1)
            h = a * jax.nn.gelu(g, approximate=False)
            x = x + h @ w2 + b2
            return x
        for l in range(DEPTH):
            x = _layer(x, wqkv[l], q_scale[l], k_scale[l], wo[l], ln_g[l], ln_b[l], w1[l], b1[l], w2[l], b2[l])
        return x

    def _L3_xattn_ref(query, key, value, Wq, bq, Wk, bk, Wv, bv):
        import jax, jax.numpy as jnp
        import numpy as np
        B, LQ, LK = (8, 512, 512)
        QD, KD, VD = (256, 128, 128)
        q = jnp.einsum('bld,de->ble', query, Wq) + bq
        k = jnp.einsum('bld,de->ble', key, Wk) + bk
        v = jnp.einsum('bld,de->ble', value, Wv) + bv
        scores = jnp.einsum('bqe,bke->bqk', q, k)
        attn = jax.nn.softmax(scores, axis=-1)
        out = jnp.einsum('bqk,bke->bqe', attn, v)
        return out

    def _L3_ffn_ref(x, wg, w1, b1, w2, b2):
        import jax, jax.numpy as jnp
        import numpy as np
        B, Sq, M = x.shape
        E = wg.shape[1]
        S = B * Sq
        C = S // E
        xt = x.reshape(S, M)
        gates = jax.nn.softmax(xt @ wg, axis=-1)
        expert_idx = jnp.argmax(gates, axis=-1)
        mask1 = jax.nn.one_hot(expert_idx, E, dtype=xt.dtype)
        locations = jnp.cumsum(mask1, axis=0) - 1.0
        pos = jnp.sum(locations * mask1, axis=1).astype(jnp.int32)
        keep = (pos < C).astype(xt.dtype)
        gate_val = jnp.sum(gates * mask1, axis=1) * keep
        slot = expert_idx.astype(jnp.int32) * C + jnp.clip(pos, 0, C - 1)
        disp = jnp.zeros((E * C, M), dtype=xt.dtype).at[slot].add(xt * keep[:, None])
        disp = disp.reshape(E, C, M)
        h = jax.nn.relu(jnp.einsum('ecm,emh->ech', disp, w1) + b1[:, None, :])
        eo = jnp.einsum('ech,ehm->ecm', h, w2) + b2[:, None, :]
        out = eo.reshape(E * C, M)[slot] * gate_val[:, None]
        return out.reshape(B, Sq, M)
    x = x + _L0_xattn_ref(_layernorm(x, axis=-1), ctx_512, ctx_512, L0_xattn_Wq, L0_xattn_bq, L0_xattn_Wk, L0_xattn_bk, L0_xattn_Wv, L0_xattn_bv, L0_xattn_Wo, L0_xattn_bo)
    x = x + _L0_ffn_ref(_layernorm(x, axis=-1), L0_ffn_router_indices, L0_ffn_routing_weights, L0_ffn_gate_up_proj, L0_ffn_gate_up_proj_bias, L0_ffn_down_proj, L0_ffn_down_proj_bias)
    x = x + _L1_xattn_ref(_layernorm(x, axis=-1), ctx_512, L1_xattn_ln1_g, L1_xattn_ln1_b, L1_xattn_ln2_g, L1_xattn_ln2_b, L1_xattn_a1_wq, L1_xattn_a1_wk, L1_xattn_a1_wv, L1_xattn_a1_li1_w, L1_xattn_a1_li1_b, L1_xattn_a1_lnx_g, L1_xattn_a1_lnx_b, L1_xattn_a1_lny_g, L1_xattn_a1_lny_b, L1_xattn_a1_ln3_g, L1_xattn_a1_ln3_b, L1_xattn_a1_li2_w, L1_xattn_a1_li2_b, L1_xattn_a1_li3_w, L1_xattn_a1_li3_b, L1_xattn_a2_wq, L1_xattn_a2_wk, L1_xattn_a2_wv, L1_xattn_a2_li1_w, L1_xattn_a2_li1_b, L1_xattn_a2_lnx_g, L1_xattn_a2_lnx_b, L1_xattn_a2_lny_g, L1_xattn_a2_lny_b, L1_xattn_a2_ln3_g, L1_xattn_a2_ln3_b, L1_xattn_a2_li2_w, L1_xattn_a2_li2_b, L1_xattn_a2_li3_w, L1_xattn_a2_li3_b, 0)
    x = x + _L1_ffn_ref(_layernorm(x, axis=-1), L1_ffn_w_g, L1_ffn_c_fc, L1_ffn_c_proj)
    x = x + _L2_xattn_ref(_layernorm(x, axis=-1), ctx_512, L2_xattn_Wq, L2_xattn_Wkv, L2_xattn_Wo)
    x = x + _L2_ffn_ref(_layernorm(x, axis=-1), L2_ffn_wqkv, L2_ffn_q_scale, L2_ffn_k_scale, L2_ffn_wo, L2_ffn_ln_g, L2_ffn_ln_b, L2_ffn_w1, L2_ffn_b1, L2_ffn_w2, L2_ffn_b2)
    x = x + _L3_xattn_ref(_layernorm(x, axis=-1), ctx_512, ctx_512, L3_xattn_Wq, L3_xattn_bq, L3_xattn_Wk, L3_xattn_bk, L3_xattn_Wv, L3_xattn_bv)
    x = x + _L3_ffn_ref(_layernorm(x, axis=-1), L3_ffn_wg, L3_ffn_w1, L3_ffn_b1, L3_ffn_w2, L3_ffn_b2)
    return x

_drawn_inputs = setup_inputs


def setup_inputs(seed=0):
    import zlib

    import numpy as np

    out = dict(_drawn_inputs(seed))
    spreads = {'L0_xattn_bq': (0.0, 0.33),
     'L0_xattn_bk': (0.0, 2.0),
     'L0_xattn_bv': (0.0, 0.1),
     'L0_xattn_bo': (0.0, 0.1),
     'L1_xattn_ln1_g': (1.0, 0.2),
     'L1_xattn_ln1_b': (0.0, 0.1),
     'L1_xattn_ln2_g': (1.0, 0.2),
     'L1_xattn_ln2_b': (0.0, 0.1),
     'L1_xattn_a1_li1_b': (0.0, 0.272),
     'L1_xattn_a1_lnx_g': (1.0, 0.6),
     'L1_xattn_a1_lnx_b': (0.0, 0.8),
     'L1_xattn_a1_lny_g': (1.0, 0.6),
     'L1_xattn_a1_lny_b': (0.0, 0.8),
     'L1_xattn_a1_ln3_g': (1.0, 0.6),
     'L1_xattn_a1_ln3_b': (0.0, 0.8),
     'L1_xattn_a1_li2_b': (0.0, 0.643),
     'L1_xattn_a1_li3_b': (0.0, 0.284),
     'L1_xattn_a2_li1_b': (0.0, 0.1),
     'L1_xattn_a2_lnx_g': (1.0, 0.6),
     'L1_xattn_a2_lnx_b': (0.0, 0.8),
     'L1_xattn_a2_lny_g': (1.0, 0.6),
     'L1_xattn_a2_lny_b': (0.0, 0.8),
     'L1_xattn_a2_ln3_g': (1.0, 0.6),
     'L1_xattn_a2_ln3_b': (0.0, 2.0),
     'L1_xattn_a2_li2_b': (0.0, 0.65),
     'L1_xattn_a2_li3_b': (0.0, 0.306),
     'L2_ffn_q_scale': (1.0, 0.6),
     'L2_ffn_k_scale': (1.0, 0.6),
     'L2_ffn_ln_g': (1.0, 0.6),
     'L2_ffn_ln_b': (0.0, 0.8),
     'L2_ffn_b1': (0.0, 0.8),
     'L2_ffn_b2': (0.0, 0.8),
     'L3_xattn_bq': (0.0, 2.0),
     'L3_xattn_bk': (0.0, 2.0),
     'L3_xattn_bv': (0.0, 1.654),
     'L3_ffn_b1': (0.0, 2.0),
     'L3_ffn_b2': (0.0, 2.0)}
    factors = {'L0_ffn_routing_weights': 8.0,
     'L0_ffn_gate_up_proj': 7.648,
     'L0_ffn_gate_up_proj_bias': 8.0,
     'L0_ffn_down_proj': 8.0,
     'L0_ffn_down_proj_bias': 32.455,
     'L1_xattn_a1_wq': 8.0,
     'L1_xattn_a1_wk': 8.0,
     'L1_xattn_a1_wv': 3.835,
     'L1_xattn_a1_li1_w': 3.856,
     'L1_xattn_a2_wq': 8.0,
     'L1_xattn_a2_wk': 8.0,
     'L1_xattn_a2_wv': 3.128,
     'L1_xattn_a2_li1_w': 3.17,
     'L2_ffn_w1': 4.62,
     'L2_ffn_w2': 4.525,
     'L3_xattn_Wq': 19.96,
     'L3_xattn_Wk': 13.628,
     'L1_ffn_w_g': 3.134,
     'L1_ffn_c_fc': 2.791,
     'L1_ffn_c_proj': 2.744,
     'L3_xattn_Wv': 4.42,
     'L3_ffn_wg': 3.2,
     'L3_ffn_w1': 5.809,
     'L3_ffn_w2': 4.01}
    for name, (base, spread) in spreads.items():
        noise = np.random.default_rng([zlib.crc32(name.encode()), seed]).standard_normal(out[name].shape)
        drawn = base * np.exp(spread * noise) if base else spread * noise
        out[name] = jnp.asarray(drawn.astype(out[name].dtype))
    for name, factor in factors.items():
        out[name] = (out[name] * factor).astype(out[name].dtype)
    return out
```

```python
from contextlib import ExitStack, contextmanager

import numpy as np
import concourse.bass as bass
from concourse import mybir

F32 = mybir.dt.float32
BF16 = mybir.dt.bfloat16
I32 = mybir.dt.int32
U32 = mybir.dt.uint32
ALU = mybir.AluOpType
ACT = mybir.ActivationFunctionType
AX = mybir.AxisListType

P = 128
BATCH = 2
SEQ = 1024
TOK = BATCH * SEQ
T = TOK // P
TB = SEQ // P
D = 256
KD = D // P
CTX = 77
CP = 80
IMG = 128
GT = 4
G = T // GT
GN = GT * P
EPS = 1e-5
NEG = -1e30


@contextmanager
def stage(nc, *names):
    with ExitStack() as held:
        sems = [held.enter_context(nc.semaphore(n)) for n in names]
        with nc.Block() as block:
            yield (block, *sems)
        with nc.Block() as clearing:
            @clearing.sync
            def _(sp):
                for s in sems:
                    sp.sem_clear(s)


def tiles(nc, held):
    def make(name, shape, dt=F32):
        return held.enter_context(nc.sbuf_tensor(f"{name}_{nc.next_id()}", shape, dt))
    return make


class Chain:

    def __init__(self, eng, sem, base=0):
        self.eng, self.sem, self.base, self.n = eng, sem, base, 0

    def __call__(self, ins):
        self.n += 1
        ins.then_inc(self.sem, 1)
        self.eng.wait_ge(self.sem, self.base + self.n)



def build_constants(nc, k, cols_dram, ctx_dram, x_dram):
    with stage(nc, "x_loaded", "vectors_loaded", "ctx_loaded", "pool_step", "ctx_turned", "ctx_copied", "ones_set") as (
            block, x_loaded, vectors_loaded, ctx_loaded, pool_step, ctx_turned, ctx_copied, ones_set):
        @block.sync
        def _(sp):
            sp.dma_start(k.x[:, :, :], x_dram.rearrange("b (t p) d -> p (b t) d", p=P)).then_inc(x_loaded, 16)
            sp.dma_start(k.ctx[0:CTX, :, :], ctx_dram.rearrange("b s d -> s b d")).then_inc(ctx_loaded, 16)
            sp.dma_start(k.cols[:, :], cols_dram).then_inc(vectors_loaded, 16)
            sp.wait_ge(x_loaded, 16)
            sp.wait_ge(vectors_loaded, 16)

        @block.gpsimd
        def _(pool):
            step = Chain(pool, pool_step)
            step(pool.memset(k.ident[:, :], 0.0))
            step(pool.affine_select(out=k.ident[:, :], in_=k.ident[:, :], compare_op=ALU.not_equal, fill=1.0,
                                    base=0, pattern=[[-1, P]], channel_multiplier=1))
            step(pool.memset(k.upper[:, :], 1.0))
            step(pool.affine_select(out=k.upper[:, :], in_=k.upper[:, :], compare_op=ALU.is_gt, fill=0.0,
                                    base=0, pattern=[[1, P]], channel_multiplier=-1))
            for mask, d in ((k.hm16, 16), (k.hm32, 32)):
                n = P // d
                step(pool.memset(mask[:, :], 1.0))
                step(pool.affine_select(out=mask[:, :], in_=mask[:, :], compare_op=ALU.is_ge, fill=0.0,
                                        base=0, pattern=[[-d, n]], channel_multiplier=1))
                step(pool.affine_select(out=mask[:, :], in_=mask[:, :], compare_op=ALU.is_ge, fill=0.0,
                                        base=d - 1, pattern=[[d, n]], channel_multiplier=-1))
            for j in range(5):
                h0 = heads_of_block(j)[0]
                vm = k.vmask[:, j, :]
                step(pool.memset(vm, 1.0))
                step(pool.affine_select(out=vm, in_=vm, compare_op=ALU.is_ge, fill=0.0, base=P * j - CP * h0,
                                        pattern=[[-CP, 3]], channel_multiplier=1))
                step(pool.affine_select(out=vm, in_=vm, compare_op=ALU.is_ge, fill=0.0, base=CP * h0 + CP - 1 - P * j,
                                        pattern=[[CP, 3]], channel_multiplier=-1))
            step(pool.iota(k.eidx[:, :], pattern=[[1, 8]], base=0, channel_multiplier=0,
                           allow_small_or_imprecise_dtypes=True))

        @block.tensor
        def _(pe):
            pe.wait_ge(ctx_loaded, 16)
            pe.wait_ge(pool_step, 2)
            for b in range(BATCH):
                pe.transpose(k.ps[:, b, 0:CTX], k.ctx[0:CTX, b, :], k.ident[0:CTX, 0:CTX]).then_inc(ctx_turned, 1)

        @block.vector
        def _(dve):
            dve.memset(k.ones[:, :], 1.0).then_inc(ones_set, 1)
            for b in range(BATCH):
                dve.wait_ge(ctx_turned, b + 1)
                dve.tensor_copy(k.ctxT[:, b, :], k.ps[:, b, 0:CTX]).then_inc(ctx_copied, 1)



def reciprocal_root(dve, step, rstd, var, root, tmp):
    step(dve.reciprocal(rstd, root))
    step(dve.tensor_tensor(tmp, rstd, rstd, ALU.mult))
    step(dve.tensor_tensor(tmp, tmp, var, ALU.mult))
    step(dve.tensor_scalar(tmp, tmp, -0.5, 1.5, ALU.mult, ALU.add))
    step(dve.tensor_tensor(rstd, rstd, tmp, ALU.mult))


def ln_stats(nc, k, src, mean, rstd, n=T, rows=P):
    width = src.shape[2]
    with ExitStack() as held:
        stats = tiles(nc, held)("stats", [P, n, 6])
        tmp = tiles(nc, held)("tmp", [P, 5, n])
        with stage(nc, "stats_done", "var_ready", "root_ready", "dve_step") as (
                block, stats_done, var_ready, root_ready, dve_step):
            r = slice(0, rows)
            var, root, dif, sq, nw = (tmp[r, j, :] for j in range(5))

            @block.vector
            def _(dve):
                if n > 4:
                    with dve.Fori(0, n) as t:
                        dve.bn_stats(stats[r, t, :], src[r, t, :]).then_inc(stats_done, 1)
                else:
                    for t in range(n):
                        dve.bn_stats(stats[r, t, :], src[r, t, :]).then_inc(stats_done, 1)
                dve.wait_ge(stats_done, n)
                step = Chain(dve, dve_step)
                even, odd = stats[r, :, 1], stats[r, :, 4]
                dve.tensor_tensor(mean[r, :], even, odd, ALU.add)
                dve.tensor_tensor(dif, even, odd, ALU.subtract)
                step(dve.tensor_tensor(var, stats[r, :, 2], stats[r, :, 5], ALU.add))
                dve.tensor_scalar(mean[r, :], mean[r, :], 0.5, None, ALU.mult)
                dve.tensor_tensor(sq, dif, dif, ALU.mult)
                step(dve.tensor_scalar(var, var, 1.0 / width, EPS, ALU.mult, ALU.add))
                dve.scalar_tensor_tensor(out=var, in0=sq, scalar=0.25, in1=var,
                                         op0=ALU.mult, op1=ALU.add).then_inc(var_ready, 1)
                dve.wait_ge(root_ready, 1)
                reciprocal_root(dve, step, rstd[r, :], var, root, nw)

            @block.scalar
            def _(act):
                act.wait_ge(var_ready, 1)
                act.activation(root, var, ACT.Sqrt).then_inc(root_ready, 1)



def normalise_group(dve, g, xn, src, mean, rstd, turned, normed):
    for u in range(GT):
        if u == 0:
            dve.wait_ge(turned, g * GT)
        t = g * GT + u
        if mean is None:
            dve.tensor_copy(xn[:, u, :], src[:, t, :]).then_inc(normed, 1)
        else:
            dve.tensor_scalar(xn[:, u, :], src[:, t, :], mean[:, bass.ds(t, 1)], rstd[:, bass.ds(t, 1)],
                              ALU.subtract, ALU.mult).then_inc(normed, 1)


def turn_group(pe, g, k, xn, psT, normed, turned, copied, copies):
    for u in range(GT):
        if u == 0:
            pe.wait_ge(copied, g * 2 * copies)
        pe.wait_ge(normed, g * GT + (u + 1))
        for c in range(KD):
            m = pe.transpose(psT[:, u // 2, (u % 2 * KD + c) * P:(u % 2 * KD + c + 1) * P],
                             xn[:, u, c * P:(c + 1) * P], k.ident[:, :])
        m.then_inc(turned, 1)


def copy_group(act, g, xT, psT, gains, turned, copied, xT_read, reads):
    for q in range(2):
        if q == 0:
            act.wait_ge(xT_read, g * reads)
        act.wait_ge(turned, g * GT + (2 * q + 2))
        turned_pair = psT[:, q, :].rearrange("p (u c n) -> p c u n", c=KD, n=P)
        for dst, gain in zip(xT, gains):
            out = dst[:, :, q * 2 * P:(q + 1) * 2 * P].rearrange("p c (u n) -> p c u n", n=P)
            if gain is None:
                act.activation(out, turned_pair, ACT.Copy).then_inc(copied, 1)
            else:
                for c in range(KD):
                    m = act.activation(out[:, c], turned_pair[:, c], ACT.Identity,
                                       scale=gain[0][:, c:c + 1], bias=gain[1][:, c:c + 1])
                m.then_inc(copied, 1)



def ffn(nc, k, src, acc, w1, w2, gain, b1, b2row, glu=False):
    F = w2.shape[0]
    blocks = [(f, min(P, F - f)) for f in range(0, F, P)]
    NB = len(blocks)
    full = F // P
    with ExitStack() as held:
        sb = tiles(nc, held)
        w1s = sb("w1s", [P, KD, w1.shape[1]])
        w2s = sb("w2s", [P, NB, D])
        b2s = sb("b2s", [1, D])
        xn = sb("xn", [P, GT, D])
        xT = sb("xT", [P, KD, GN])
        hT = sb("hT", [P, NB, GN])
        gl = sb("gl", [P, 2, GN]) if glu else None
        mean = sb("mean", [P, T])
        rstd = sb("rstd", [P, T])
        ln_stats(nc, k, src, mean, rstd)
        psT = k.ps[:, 0:2, :]
        NH = 4 if glu else 3
        psH = [k.ps[:, 2 + j, :] for j in range(NH)]
        psY = [k.ps[:, 6 + j, 0:D] for j in range(2)]
        with stage(nc, "w1_loaded", "w2_loaded", "normed", "turned", "copied", "h_ready", "h_done", "gate_done",
                   "y_ready", "y_added") as (
                block, w1_loaded, w2_loaded, normed, turned, copied, h_ready, h_done, gate_done, y_ready, y_added):
            @block.sync
            def _(sp):
                sp.dma_start(w1s[:, :, :], w1.rearrange("(c p) f -> p c f", p=P)).then_inc(w1_loaded, 16)
                sp.dma_start(w2s[:, 0:full, :],
                             w2[0:full * P, :].rearrange("(c p) f -> p c f", p=P)).then_inc(w2_loaded, 16)
                if full < NB:
                    sp.dma_start(w2s[0:F - full * P, full, :], w2[full * P:F, :]).then_inc(w2_loaded, 16)
                sp.dma_start(b2s[:, :], b2row).then_inc(w2_loaded, 16)
            w2_all = 16 * (3 if full < NB else 2)

            @block.tensor
            def _(pe):
                with pe.Fori(0, G) as g:
                    turn_group(pe, g, k, xn, psT, normed, turned, copied, 1)
                    pe.wait_ge(w1_loaded, 16)
                    pe.wait_ge(copied, (g + 1) * 2)
                    if not glu:
                        for j, (f, m) in enumerate(blocks):
                            pe.wait_ge(h_done, g * NB + max(j - NH + 1, 0))
                            for c in range(KD):
                                mm = pe.matmul(psH[j % NH][0:m, :], w1s[:, c, f:f + m], xT[:, c, :],
                                               start=(c == 0), stop=(c == KD - 1))
                            mm.then_inc(h_ready, 1)
                    else:
                        for j, (f, m) in enumerate(blocks):
                            pe.wait_ge(h_done, g * NB + max(j - 1, 0))
                            for half in (1, 0):
                                for c in range(KD):
                                    mm = pe.matmul(psH[2 * (j % 2) + half][0:m, :],
                                                   w1s[:, c, half * F + f:half * F + f + m], xT[:, c, :],
                                                   start=(c == 0), stop=(c == KD - 1))
                                mm.then_inc(h_ready, 1)
                    pe.wait_ge(w2_loaded, w2_all)
                    for u in range(GT):
                        pe.wait_ge(y_added, g * GT + max(u - 1, 0))
                        pe.matmul(psY[u % 2], k.ones[0:1, 0:P], b2s[:, :], start=True, stop=False)
                        if u == 0:
                            pe.wait_ge(h_done, (g + 1) * NB)
                        for j, (f, m) in enumerate(blocks):
                            mm = pe.matmul(psY[u % 2], hT[0:m, j, u * P:(u + 1) * P], w2s[0:m, j, :],
                                           start=False, stop=(j == NB - 1))
                        mm.then_inc(y_ready, 1)

            @block.scalar
            def _(act):
                with act.Fori(0, G) as g:
                    hidden = 2 * NB if glu else NB
                    copy_group(act, g, [xT], psT, [gain], turned, copied, h_ready, hidden)
                    for j, (f, m) in enumerate(blocks):
                        if not glu:
                            if j == 0:
                                act.wait_ge(y_ready, g * GT)
                            act.wait_ge(h_ready, g * NB + (j + 1))
                            act.activation(hT[0:m, j, :], psH[j % NH][0:m, :], ACT.Gelu,
                                           bias=b1[0:m, j:j + 1]).then_inc(h_done, 1)
                        else:
                            act.wait_ge(h_ready, g * 2 * NB + (2 * j + 1))
                            act.wait_ge(h_done, g * NB + max(j - 1, 0))
                            act.activation(gl[0:m, j % 2, :], psH[2 * (j % 2) + 1][0:m, :], ACT.Gelu,
                                           bias=b1[0:m, NB + j:NB + j + 1]).then_inc(gate_done, 1)

            @block.vector
            def _(dve):
                with dve.Fori(0, G) as g:
                    normalise_group(dve, g, xn, src, mean, rstd, turned, normed)
                    if glu:
                        for j, (f, m) in enumerate(blocks):
                            if j == 0:
                                dve.wait_ge(y_ready, g * GT)
                            dve.wait_ge(h_ready, g * 2 * NB + (2 * j + 2))
                            dve.wait_ge(gate_done, g * NB + (j + 1))
                            dve.scalar_tensor_tensor(out=hT[0:m, j, :], in0=psH[2 * (j % 2)][0:m, :],
                                                     scalar=b1[0:m, j:j + 1], in1=gl[0:m, j % 2, :],
                                                     op0=ALU.add, op1=ALU.mult).then_inc(h_done, 1)
                    for u in range(GT):
                        t = g * GT + u
                        dve.wait_ge(y_ready, g * GT + (u + 1))
                        dve.tensor_tensor(acc[:, t, :], psY[u % 2], acc[:, t, :], ALU.add).then_inc(y_added, 1)



def project(nc, k, src, mean, rstd, gains, turned_jobs, row_jobs, loads, dst_of=None):
    with ExitStack() as held:
        sb = tiles(nc, held)
        xn = sb("xn", [P, GT, D])
        xT = [sb(f"xT{j}", [P, KD, GN]) for j in range(len(gains))]
        psT = k.ps[:, 0:2, :]
        NC = len(gains)
        blocks = [(w, a, dst, bias, scale, f) for w, a, dst, bias, scale in turned_jobs
                  for f in range(w.shape[2] // P)]
        rows = [(w, a, dst, u, f) for w, a, dst in row_jobs for u in range(GT) for f in range(w.shape[2] // 512)]
        NF, NR = len(blocks), len(rows)
        RING = 3
        with stage(nc, "w_loaded", "normed", "turned", "copied", "feat_ready", "feat_out", "row_ready", "row_out",
                   "products_done") as (
                block, w_loaded, normed, turned, copied, feat_ready, feat_out, row_ready, row_out, products_done):
            @block.sync
            def _(sp):
                for dst, weights in loads:
                    sp.dma_start(dst, weights).then_inc(w_loaded, 16)

            @block.tensor
            def _(pe):
                with pe.Fori(0, G) as g:
                    turn_group(pe, g, k, xn, psT, normed, turned, copied, NC)
                    pe.wait_ge(w_loaded, 16 * len(loads))
                    pe.wait_ge(copied, (g + 1) * 2 * NC)
                    for j, (w, a, dst, bias, scale, f) in enumerate(blocks):
                        pe.wait_ge(feat_out, g * NF + max(j - RING + 1, 0))
                        for c in range(KD):
                            mm = pe.matmul(k.ps[:, 2 + j % RING, :], w[:, c, f * P:(f + 1) * P], xT[a][:, c, :],
                                           start=(c == 0), stop=(c == KD - 1))
                        mm.then_inc(feat_ready, 1)
                    for j, (w, a, dst, u, f) in enumerate(rows):
                        pe.wait_ge(row_out, g * NR + max(j - RING + 1, 0))
                        for c in range(KD):
                            mm = pe.matmul(k.ps[:, 5 + j % RING, :], xT[a][:, c, u * P:(u + 1) * P],
                                           w[:, c, f * 512:(f + 1) * 512], start=(c == 0), stop=(c == KD - 1))
                        mm.then_inc(row_ready, 1)

            @block.scalar
            def _(act):
                with act.Fori(0, G) as g:
                    last, n = (row_ready, NR) if NR else (feat_ready, NF)
                    copy_group(act, g, xT, psT, gains, turned, copied, last, n)
                    for j, (w, a, dst, u, f) in enumerate(rows):
                        act.wait_ge(row_ready, g * NR + (j + 1))
                        act.activation(dst[:, 4 * f:4 * f + 4, bass.ds(g * GT + u, 1), :].rearrange("p a t n -> p (a t) n"),
                                       k.ps[:, 5 + j % RING, :].rearrange("p (a n) -> p a n", a=4),
                                       ACT.Copy).then_inc(row_out, 1)

            @block.vector
            def _(dve):
                with dve.Fori(0, G) as g:
                    normalise_group(dve, g, xn, src, mean, rstd, turned, normed)
                    for j, (w, a, dst, bias, scale, f) in enumerate(blocks):
                        dve.wait_ge(feat_ready, g * NF + (j + 1))
                        dve.tensor_scalar(dst[:, f, bass.ds(g * GN, GN)], k.ps[:, 2 + j % RING, :],
                                          0.0 if bias is None else bias[:, f:f + 1], scale,
                                          ALU.add, ALU.mult).then_inc(feat_out, 1)



def heads_of_block(j):
    return P * j // CP, (P * j + P - 1) // CP


def cross_attention(nc, k, d, srcT, QT, O, wk, wv, bk, bvrow, scale):
    NQ = 16 * d // P
    HB = P // d
    hm = k.hm16 if d == 16 else k.hm32
    W = d + 1
    with ExitStack() as held:
        sb = tiles(nc, held)
        Kbd = sb("Kbd", [P, BATCH, 16, CTX])
        Vfirst = sb("Vfirst", [P, BATCH, 2, 8 * W])
        Vbd = sb("Vbd", [P, BATCH, 10, 3 * W])
        with ExitStack() as prep:
            sb2 = tiles(nc, prep)
            wks = sb2("wks", [P, 16 * d])
            wvs = sb2("wvs", [P, 16 * d])
            bvs = sb2("bvs", [1, 16 * d])
            rep = sb2("rep", [P, BATCH, 8, CP])
            with stage(nc, "wk_loaded", "wv_loaded", "zeroed", "rep_made", "k_ready", "k_out", "v_ready", "v_out") as (
                    block, wk_loaded, wv_loaded, zeroed, rep_made, k_ready, k_out, v_ready, v_out):
                @block.sync
                def _(sp):
                    sp.dma_start(wks[:, :], wk).then_inc(wk_loaded, 16)
                    sp.dma_start(wvs[:, :], wv).then_inc(wv_loaded, 16)
                    if bvrow is not None:
                        sp.dma_start(bvs[:, :], bvrow).then_inc(wv_loaded, 16)

                @block.gpsimd
                def _(pool):
                    pool.memset(rep[:, :, :, :], 0.0).then_inc(zeroed, 1)
                    pool.memset(Vfirst[:, :, :, :], 0.0).then_inc(zeroed, 1)
                    pool.wait_ge(zeroed, 1)
                    for b in range(BATCH):
                        pool.tensor_copy(rep[:, b, :, 0:CTX],
                                         srcT[:, b, :].unsqueeze(1).to_broadcast([P, 8, CTX])).then_inc(rep_made, 1)

                @block.tensor
                def _(pe):
                    pe.wait_ge(wk_loaded, 16)
                    n = 0
                    for b in range(BATCH):
                        for q in range(NQ):
                            if n >= 4:
                                pe.wait_ge(k_out, n - 3)
                            pe.matmul(k.ps[:, n % 4, 0:CTX], wks[:, q * P:(q + 1) * P], srcT[:, b, :],
                                      start=True, stop=True).then_inc(k_ready, 1)
                            n += 1
                    pe.wait_ge(wv_loaded, 32 if bvrow is not None else 16)
                    pe.wait_ge(rep_made, BATCH)
                    n = 0
                    for b in range(BATCH):
                        flat = rep[:, b, :, :].rearrange("p h c -> p (h c)")
                        for j in range(10):
                            h0, h1 = heads_of_block(j)
                            cols = slice(h0 * d, (h1 + 1) * d)
                            if n >= 4:
                                pe.wait_ge(v_out, n - 3)
                            out = k.ps[:, 4 + n % 4, 0:(h1 - h0 + 1) * d]
                            mm = pe.matmul(out, flat[:, j % 5 * P:(j % 5 + 1) * P], wvs[:, cols],
                                           start=True, stop=(bvrow is None))
                            if bvrow is not None:
                                mm = pe.matmul(out, k.ones[0:1, 0:P], bvs[:, cols], start=False, stop=True)
                            mm.then_inc(v_ready, 1)
                            n += 1

                @block.vector
                def _(dve):
                    n = 0
                    for b in range(BATCH):
                        for q in range(NQ):
                            dve.wait_ge(k_ready, n + 1)
                            for h in range(HB):
                                m = dve.tensor_scalar(Kbd[:, b, q * HB + h, :], k.ps[:, n % 4, 0:CTX],
                                                      0.0 if bk is None else bk[:, q:q + 1], hm[:, h:h + 1],
                                                      ALU.add, ALU.mult)
                            m.then_inc(k_out, 1)
                            n += 1
                    dve.wait_ge(zeroed, 2)
                    n = 0
                    for b in range(BATCH):
                        for j in range(10):
                            h0, h1 = heads_of_block(j)
                            nh = h1 - h0 + 1
                            dst = Vfirst[:, b, j // 5, 0:nh * W] if j % 5 == 0 else Vbd[:, b, j, 0:nh * W]
                            dst = dst.rearrange("p (h w) -> p h w", w=W)
                            dve.wait_ge(v_ready, n + 1)
                            mask = k.vmask[:, j % 5, 0:nh].unsqueeze(2)
                            dve.tensor_copy(dst[:, :, d:W], mask)
                            dve.tensor_tensor(dst[:, :, 0:d],
                                              k.ps[:, 4 + n % 4, 0:nh * d].rearrange("p (h w) -> p h w", w=d),
                                              mask.to_broadcast([P, nh, d]), ALU.mult).then_inc(v_out, 1)
                            n += 1

        qs = sb("qs", [P, 2, NQ, P])
        neg = sb("neg", [P, 2, 8])
        sd = sb("sd", [P, 2, 8, CTX])
        pr = sb("pr", [P, 2, 8, CP])
        pT = sb("pT", [P, 2, 5, P])
        rsum = sb("rsum", [P, 2, 8])
        score_view = lambda c: k.ps[:, 2 * (c % 2):2 * (c % 2) + 2, 0:4 * CTX].rearrange("p b (h n) -> p b h n", n=CTX)
        psPT = k.ps[:, 4:6, :]
        IT = 4
        with stage(nc, "pads_zeroed", "q_staged", "s_ready", "shifted", "exp_done", "pt_ready", "pt_copied",
                   "o_ready", "o_done", "max_done", "inverse_done") as (
                block, pads_zeroed, q_staged, s_ready, shifted, exp_done, pt_ready, pt_copied, o_ready, o_done,
                max_done, inverse_done):
            @block.gpsimd
            def _(pool):
                pool.memset(pr[:, :, :, :], 0.0).then_inc(pads_zeroed, 1)
                with pool.Fori(0, T // 2) as i:
                    pool.wait_ge(s_ready, i * IT)
                    for u in range(2):
                        pool.tensor_copy(qs[:, u, :, :], QT[:, :, bass.ds((2 * i + u) * P, P)]).then_inc(q_staged, 1)

            @block.tensor
            def _(pe):
                def scores(b, it, c):
                    u, half = c // 2, c % 2
                    pe.wait_ge(q_staged, it * 2 + (u + 1))
                    pe.wait_ge(shifted, it * IT + max(c - 1, 0))
                    for j in range(2):
                        h = 8 * half + 4 * j
                        mm = pe.matmul(k.ps[:, 2 * (c % 2) + j, 0:4 * CTX], qs[:, u, h // HB, :],
                                       Kbd[:, b, h:h + 4, :].rearrange("p a h n -> p (a h n)"), start=True, stop=True)
                    mm.then_inc(s_ready, 1)

                def turn(it, c):
                    pe.wait_ge(exp_done, it * IT + (c + 1))
                    pe.wait_ge(pt_copied, it * IT + c)
                    flat = pr[:, c % 2, :, :].rearrange("p h n -> p (h n)")
                    for j in range(5):
                        mm = pe.transpose(psPT[:, j // 4, j % 4 * P:(j % 4 + 1) * P], flat[:, j * P:(j + 1) * P],
                                          k.ident[:, :])
                    mm.then_inc(pt_ready, 1)

                def values(b, it, c):
                    half = c % 2
                    pe.wait_ge(pt_copied, it * IT + (c + 1))
                    pe.wait_ge(o_done, it * IT + max(c - 1, 0))
                    for j in range(5):
                        h0, h1 = heads_of_block(5 * half + j)
                        if j == 0:
                            out, v = k.ps[:, 6 + c % 2, 0:8 * W], Vfirst[:, b, half, :]
                        else:
                            out = k.ps[:, 6 + c % 2, (h0 - 8 * half) * W:(h1 + 1 - 8 * half) * W]
                            v = Vbd[:, b, 5 * half + j, 0:(h1 - h0 + 1) * W]
                        mm = pe.matmul(out, pT[:, c % 2, j, :], v.rearrange("p a n -> p (a n)"),
                                       start=(j == 0), stop=(j == 4))
                    mm.then_inc(o_ready, 1)

                with pe.Fori(0, BATCH) as bb:
                    with pe.Fori(0, TB // 2) as i:
                        it = bb * (TB // 2) + i
                        b = bass.ds(bb, 1)
                        scores(b, it, 0)
                        scores(b, it, 1)
                        turn(it, 0)
                        scores(b, it, 2)
                        values(b, it, 0)
                        turn(it, 1)
                        scores(b, it, 3)
                        values(b, it, 1)
                        for c in (2, 3):
                            turn(it, c)
                            values(b, it, c)

            @block.scalar
            def _(act):
                def probs(it, c):
                    act.wait_ge(shifted, it * IT + (c + 1))
                    act.wait_ge(pt_ready, it * IT + max(c - 1, 0))
                    act.activation(pr[:, c % 2, :, 0:CTX], sd[:, c % 2, :, :], ACT.Exp,
                                   scale=scale).then_inc(exp_done, 1)

                def copy_pt(it, c):
                    act.wait_ge(pt_ready, it * IT + (c + 1))
                    act.wait_ge(o_ready, it * IT + max(c - 1, 0))
                    act.activation(pT[:, c % 2, :, :].rearrange("p a n -> p (a n)"),
                                   psPT.rearrange("p a n -> p (a n)")[:, 0:5 * P], ACT.Copy).then_inc(pt_copied, 1)

                act.wait_ge(pads_zeroed, 1)
                with act.Fori(0, T // 2) as it:
                    probs(it, 0)
                    probs(it, 1)
                    copy_pt(it, 0)
                    probs(it, 2)
                    copy_pt(it, 1)
                    probs(it, 3)
                    copy_pt(it, 2)
                    copy_pt(it, 3)

            @block.vector
            def _(dve):
                def shift(it, c):
                    dve.wait_ge(s_ready, it * IT + (c + 1))
                    dve.wait_ge(exp_done, it * IT + max(c - 1, 0))
                    m = neg[:, c % 2, :].rearrange("p (b h) -> p b h", b=2)
                    dve.tensor_reduce(m, score_view(c), AX.X, ALU.max).then_inc(max_done, 1)
                    dve.wait_ge(max_done, it * IT + (c + 1))
                    dve.tensor_tensor(sd[:, c % 2, :, :].rearrange("p (b h) n -> p b h n", b=2), score_view(c),
                                      m.unsqueeze(3).to_broadcast([P, 2, 4, CTX]), ALU.subtract).then_inc(shifted, 1)

                def normal(it, c):
                    u, half = c // 2, c % 2
                    dve.wait_ge(o_ready, it * IT + (c + 1))
                    o = k.ps[:, 6 + c % 2, 0:8 * W].rearrange("p (h w) -> p h w", w=W)
                    dve.reciprocal(rsum[:, c % 2, :], o[:, :, d]).then_inc(inverse_done, 1)
                    dve.wait_ge(inverse_done, it * IT + (c + 1))
                    dve.tensor_tensor(
                        O[:, half * NQ // 2:(half + 1) * NQ // 2, bass.ds(2 * it + u, 1), :].rearrange(
                            "p a t (h w) -> p (a t) h w", w=d),
                        o[:, :, 0:d].rearrange("p (a h) w -> p a h w", h=HB),
                        rsum[:, c % 2, :].rearrange("p (a h) -> p a h", h=HB).unsqueeze(3).to_broadcast(
                            [P, NQ // 2, HB, d]), ALU.mult).then_inc(o_done, 1)

                with dve.Fori(0, T // 2) as it:
                    shift(it, 0)
                    shift(it, 1)
                    shift(it, 2)
                    normal(it, 0)
                    shift(it, 3)
                    for c in (1, 2, 3):
                        normal(it, c)



def out_project(nc, k, O, w, brow, add_to, also=None):
    NB = w.shape[0] // P
    with ExitStack() as held:
        sb = tiles(nc, held)
        ws = sb("ws", [P, NB, D])
        bs = sb("bs", [1, D])
        ot = sb("ot", [P, 2, NB * P])
        OT = sb("OT", [P, 2, NB * P])
        with stage(nc, "w_loaded", "o_staged", "turned", "copied", "y_ready", "y_added", "summed") as (
                block, w_loaded, o_staged, turned, copied, y_ready, y_added, summed):
            @block.sync
            def _(sp):
                sp.dma_start(ws[:, :, :], w.rearrange("(c p) f -> p c f", p=P)).then_inc(w_loaded, 16)
                if brow is not None:
                    sp.dma_start(bs[:, :], brow).then_inc(w_loaded, 16)

            @block.gpsimd
            def _(pool):
                with pool.Fori(0, T // 2) as i:
                    pool.wait_ge(turned, 2 * i)
                    for u in range(2):
                        pool.tensor_copy(ot[:, u, :].rearrange("p (a n) -> p a n", n=P),
                                         O[:, :, bass.ds(2 * i + u, 1), :].rearrange("p a t n -> p (a t) n")
                                         ).then_inc(o_staged, 1)

            @block.tensor
            def _(pe):
                pe.wait_ge(w_loaded, 32 if brow is not None else 16)
                with pe.Fori(0, T // 2) as i:
                    for u in range(2):
                        pe.wait_ge(o_staged, 2 * i + (u + 1))
                        pe.wait_ge(copied, 2 * i)
                        for c in range(NB):
                            mm = pe.transpose(k.ps[:, u, c * P:(c + 1) * P], ot[:, u, c * P:(c + 1) * P], k.ident[:, :])
                        mm.then_inc(turned, 1)
                    for u in range(2):
                        pe.wait_ge(copied, 2 * i + (u + 1))
                        pe.wait_ge(y_added, 2 * i)
                        if brow is not None:
                            pe.matmul(k.ps[:, 2 + u, 0:D], k.ones[0:1, 0:P], bs[:, :], start=True, stop=False)
                        for c in range(NB):
                            mm = pe.matmul(k.ps[:, 2 + u, 0:D], OT[:, u, c * P:(c + 1) * P], ws[:, c, :],
                                           start=(c == 0 and brow is None), stop=(c == NB - 1))
                        mm.then_inc(y_ready, 1)

            @block.scalar
            def _(act):
                with act.Fori(0, T // 2) as i:
                    act.wait_ge(y_ready, 2 * i)
                    for u in range(2):
                        act.wait_ge(turned, 2 * i + (u + 1))
                        act.activation(OT[:, u, :], k.ps[:, u, 0:NB * P], ACT.Copy).then_inc(copied, 1)

            @block.vector
            def _(dve):
                with dve.Fori(0, T // 2) as i:
                    for u in range(2):
                        t = 2 * i + u
                        dve.wait_ge(y_ready, 2 * i + (u + 1))
                        if also is None:
                            dve.tensor_tensor(add_to[:, t, :], k.ps[:, 2 + u, 0:D], add_to[:, t, :],
                                              ALU.add).then_inc(y_added, 1)
                        else:
                            dve.scalar_tensor_tensor(out=also[:, t, :], in0=add_to[:, t, :], scalar=2.0,
                                                     in1=k.ps[:, 2 + u, 0:D], op0=ALU.mult, op1=ALU.add).then_inc(summed, 1)
                            dve.wait_ge(summed, 2 * i + (u + 1))
                            dve.tensor_tensor(add_to[:, t, :], k.ps[:, 2 + u, 0:D], add_to[:, t, :],
                                              ALU.add).then_inc(y_added, 1)


def normalise_context(nc, k, gain, yT):
    with ExitStack() as held:
        sb = tiles(nc, held)
        mean, rstd = sb("cmean", [P, BATCH]), sb("crstd", [P, BATCH])
        cn = sb("cn", [P, BATCH, IMG])
        ln_stats(nc, k, k.ctx, mean, rstd, n=BATCH, rows=CTX)
        with stage(nc, "normed", "turned") as (block, normed, turned):
            @block.vector
            def _(dve):
                for b in range(BATCH):
                    dve.tensor_scalar(cn[0:CTX, b, :], k.ctx[0:CTX, b, :], mean[0:CTX, b:b + 1], rstd[0:CTX, b:b + 1],
                                      ALU.subtract, ALU.mult).then_inc(normed, 1)

            @block.tensor
            def _(pe):
                for b in range(BATCH):
                    pe.wait_ge(normed, b + 1)
                    pe.transpose(k.ps[:, b, 0:CTX], cn[0:CTX, b, :], k.ident[0:CTX, 0:CTX]).then_inc(turned, 1)

            @block.scalar
            def _(act):
                for b in range(BATCH):
                    act.wait_ge(turned, b + 1)
                    act.activation(yT[:, b, :], k.ps[:, b, 0:CTX], ACT.Identity, scale=gain[0], bias=gain[1])



def turned_weights(w):
    return w.rearrange("(c p) f -> p c f", p=P)


def row_of(v):
    return v.rearrange("(a n) -> a n", a=1)


def cross_layer(nc, k, d, src, add_to, also, wq, bq, wk, bk, wv, bvrow, wo, borow, gain, ctxT):
    W = 16 * d
    with ExitStack() as outer:
        O = tiles(nc, outer)("O", [P, W // P, T, P])
        with ExitStack() as held:
            sb = tiles(nc, held)
            QT = sb("QT", [P, W // P, TOK])
            with ExitStack() as front:
                mean = tiles(nc, front)("mean", [P, T])
                rstd = tiles(nc, front)("rstd", [P, T])
                wqs = tiles(nc, front)("wqs", [P, KD, W])
                ln_stats(nc, k, src, mean, rstd)
                project(nc, k, src, mean, rstd, [gain], [(wqs, 0, QT, bq, 1.0)], [],
                        [(wqs[:, :, :], turned_weights(wq))])
            cross_attention(nc, k, d, ctxT, QT, O, wk, wv, bk, bvrow, float(d) ** -0.5)
        out_project(nc, k, O, wo, borow, add_to, also)


def layer0_attention(nc, k, a):
    cross_layer(nc, k, 16, k.x, k.x, None, a["L0_xattn_Wq"], k.col("L0_xattn_bq"), a["L0_xattn_Wk"],
                k.col("L0_xattn_bk"), a["L0_xattn_Wv"], row_of(a["L0_xattn_bv"]), a["L0_xattn_Wo"],
                row_of(a["L0_xattn_bo"]), None, k.ctxT)


def layer2_attention(nc, k, a):
    cross_layer(nc, k, 16, k.x, k.x, None, a["L2_xattn_Wq"], None, a["L2_xattn_Wk"],
                None, a["L2_xattn_Wv"], None, a["L2_xattn_Wo"], None, None, k.ctxT)



SH = 32
HG = P // SH


def self_attention(nc, k, QT, KT, V, O, qz):
    QB = TB
    NB = BATCH * (16 // HG)
    QT = QT[:, :, :].rearrange("p a n -> p (a n)")
    KT = KT[:, :, :].rearrange("p a n -> p (a n)")
    V = V[:, :, :, :].rearrange("p a t n -> p (a t n)")
    O = O[:, :, :, :].rearrange("p a t n -> p (a t n)")
    UNITS = [(h, q) for h in range(HG) for q in range(QB)]
    NU = len(UNITS)
    with ExitStack() as held:
        sb = tiles(nc, held)
        pr = sb("pr", [P, 2, SEQ])
        pT = sb("pT", [P, 2, SEQ])
        neg = sb("neg", [P, 2])
        rs = sb("rs", [P, 4])
        inv = sb("inv", [P, 2])
        with stage(nc, "zeroed", "q_staged", "s_ready", "max_done", "exp_done", "masked", "pt_ready",
                   "pt_copied", "o_ready", "inverse_done", "o_done") as (
                block, zeroed, q_staged, s_ready, max_done, exp_done, masked, pt_ready,
                pt_copied, o_ready, inverse_done, o_done):
            @block.gpsimd
            def _(pool):
                def stage_q(it, h, scored):
                    if scored is not None:
                        pool.wait_ge(s_ready, scored)
                    r = slice(SH * h, SH * (h + 1))
                    pool.tensor_copy(qz[r, h, :], QT[r, bass.ds(it * SEQ, SEQ)]).then_inc(q_staged, 1)
                    pool.wait_ge(q_staged, it * HG + (h + 1))

                def masks(it, stage_next):
                    for n, (h, q) in enumerate(UNITS):
                        pool.wait_ge(exp_done, it * NU + (n + 1))
                        own = pr[:, n % 2, q * P:(q + 1) * P]
                        pool.tensor_tensor(own, own, k.upper[:, :], ALU.mult).then_inc(masked, 1)
                        if stage_next and n >= QB + 1 and n % QB == 1:
                            pool.wait_ge(masked, it * NU + (n + 1))
                            stage_q(it + 1, h - 1, it * NU + QB * h)
                    if stage_next:
                        pool.wait_ge(masked, it * NU + NU)
                        stage_q(it + 1, HG - 1, it * NU + NU)

                pool.memset(qz[:, :, :], 0.0).then_inc(zeroed, 1)
                pool.wait_ge(zeroed, 1)
                for h in range(HG):
                    stage_q(0, h, None)
                with pool.Fori(0, NB - 1) as it:
                    masks(it, True)
                masks(NB - 1, False)

            @block.tensor
            def _(pe):
                def scores(it, n):
                    h, q = UNITS[n]
                    if q == 0:
                        pe.wait_ge(q_staged, it * HG + (h + 1))
                    pe.wait_ge(exp_done, it * NU + max(n - 1, 0))
                    for j in range(2):
                        mm = pe.matmul(k.ps[:, 2 * (n % 2) + j, :], qz[:, h, q * P:(q + 1) * P],
                                       KT[:, bass.ds(it * SEQ + j * 512, 512)], start=True, stop=True)
                    mm.then_inc(s_ready, 1)

                def turn(it, n):
                    q = UNITS[n][1]
                    pe.wait_ge(masked, it * NU + (n + 1))
                    pe.wait_ge(pt_copied, it * NU + n)
                    for c in range(q, QB):
                        mm = pe.transpose(k.ps[:, 4 + (c - q) // 4, (c - q) % 4 * P:((c - q) % 4 + 1) * P],
                                          pr[:, n % 2, c * P:(c + 1) * P], k.ident[:, :])
                    mm.then_inc(pt_ready, 1)

                def values(it, n):
                    h, q = UNITS[n]
                    pe.wait_ge(pt_copied, it * NU + (n + 1))
                    pe.wait_ge(o_done, it * NU + max(n - 1, 0))
                    for c in range(q, QB):
                        mm = pe.matmul(k.ps[:, 6 + n % 2, 0:SH], pT[:, n % 2, (c - q) * P:(c - q + 1) * P],
                                       V[:, bass.ds((it * QB + c) * P + h * SH, SH)], start=(c == q), stop=(c == QB - 1))
                    mm.then_inc(o_ready, 1)

                with pe.Fori(0, NB) as it:
                    scores(it, 0)
                    for n in range(NU):
                        if n + 1 < NU:
                            scores(it, n + 1)
                        turn(it, n)
                        if n:
                            values(it, n - 1)
                    values(it, NU - 1)

            def copy_pt(eng, it, n):
                w = (QB - UNITS[n][1]) * P
                eng.wait_ge(pt_ready, it * NU + (n + 1))
                eng.wait_ge(o_ready, it * NU + max(n - 1, 0))
                src = k.ps[:, 4:6, :].rearrange("p a n -> p (a n)")[:, 0:w]
                if eng is nc.scalar:
                    eng.activation(pT[:, n % 2, 0:w], src, ACT.Copy).then_inc(pt_copied, 1)
                else:
                    eng.tensor_copy(pT[:, n % 2, 0:w], src).then_inc(pt_copied, 1)

            @block.scalar
            def _(act):
                def exps(it, n):
                    act.wait_ge(max_done, it * NU + (n + 1))
                    act.wait_ge(pt_ready, it * NU + max(n - 1, 0))
                    act.wait_ge(o_done, it * NU + max(n - 3, 0))
                    act.activation(pr[:, n % 2, :], k.ps[:, 2 * (n % 2):2 * (n % 2) + 2, :].rearrange("p a n -> p (a n)"),
                                   ACT.Exp, bias=neg[:, n % 2:n % 2 + 1],
                                   accum_out=rs[:, n % 4:n % 4 + 1]).then_inc(exp_done, 1)

                with act.Fori(0, NB) as it:
                    exps(it, 0)
                    for n in range(NU):
                        if n + 1 < NU:
                            exps(it, n + 1)
                        if n % 2:
                            copy_pt(act, it, n)

            @block.vector
            def _(dve):
                def maxima(it, n):
                    dve.wait_ge(s_ready, it * NU + (n + 1))
                    dve.tensor_reduce(neg[:, n % 2:n % 2 + 1], k.ps[:, 2 * (n % 2):2 * (n % 2) + 2, :], AX.XY,
                                      ALU.max, negate=True).then_inc(max_done, 1)

                def normal(it, n):
                    h, q = UNITS[n]
                    dve.wait_ge(o_ready, it * NU + (n + 1))
                    dve.reciprocal(inv[:, n % 2:n % 2 + 1], rs[:, n % 4:n % 4 + 1]).then_inc(inverse_done, 1)
                    dve.wait_ge(inverse_done, it * NU + (n + 1))
                    dve.tensor_scalar(O[:, bass.ds((it * QB + q) * P + h * SH, SH)], k.ps[:, 6 + n % 2, 0:SH], inv[:, n % 2:n % 2 + 1], None,
                        ALU.mult).then_inc(o_done, 1)

                with dve.Fori(0, NB) as it:
                    maxima(it, 0)
                    for n in range(NU):
                        if n + 1 < NU:
                            maxima(it, n + 1)
                        if n % 2 == 0:
                            copy_pt(dve, it, n)
                        if n:
                            normal(it, n - 1)
                    normal(it, NU - 1)


def layer1_attention(nc, k, a):
    with ExitStack() as held:
        sb = tiles(nc, held)
        y = sb("y_rows", [P, T, D])
        base = sb("base_rows", [P, T, D])
        layer_norm_rows(nc, k, k.x, y, None)
        layer_norm_rows(nc, k, y, y, ("L1_xattn_ln1_g", "L1_xattn_ln1_b"), a)
        A = "L1_xattn_a1_"
        with ExitStack() as outer:
            O = tiles(nc, outer)("O", [P, 4, T, P])
            with ExitStack() as inner:
                sb2 = tiles(nc, inner)
                QT, KT, V = sb2("QT", [P, 4, TOK]), sb2("KT", [P, 4, TOK]), sb2("V", [P, 4, T, P])
                with ExitStack() as front:
                    sb3 = tiles(nc, front)
                    mean, rstd = sb3("mean", [P, T]), sb3("rstd", [P, T])
                    ws = [sb3(f"w{n}", [P, KD, 512]) for n in "qkv"]
                    ln_stats(nc, k, y, mean, rstd)
                    project(nc, k, y, mean, rstd,
                            [(k.col(A + "lnx_g"), k.col(A + "lnx_b")), (k.col(A + "lny_g"), k.col(A + "lny_b"))],
                            [(ws[0], 0, QT, None, float(SH) ** -0.5), (ws[1], 1, KT, None, 1.0)], [(ws[2], 1, V)],
                            [(w[:, :, :], turned_weights(a[A + n])) for w, n in zip(ws, ("wq", "wk", "wv"))])
                self_attention(nc, k, QT, KT, V, O, base[:, :, :].rearrange("p (h t) d -> p h (t d)", h=HG))
            out_project(nc, k, O, a[A + "li1_w"], row_of(a[A + "li1_b"]), y, base)
        ffn(nc, k, y, base, a[A + "li2_w"], a[A + "li3_w"], (k.col(A + "ln3_g"), k.col(A + "ln3_b")),
            k.col(A + "li2_b"), row_of(a[A + "li3_b"]))
        layer_norm_rows(nc, k, base, y, ("L1_xattn_ln2_g", "L1_xattn_ln2_b"), a)
        A = "L1_xattn_a2_"
        yT = sb("yT", [P, BATCH, CTX])
        normalise_context(nc, k, (k.col(A + "lny_g"), k.col(A + "lny_b")), yT)
        cross_layer(nc, k, 32, y, y, base, a[A + "wq"], None, a[A + "wk"], None, a[A + "wv"], None,
                    a[A + "li1_w"], row_of(a[A + "li1_b"]), (k.col(A + "lnx_g"), k.col(A + "lnx_b")), yT)
        ffn(nc, k, y, base, a[A + "li2_w"], a[A + "li3_w"], (k.col(A + "ln3_g"), k.col(A + "ln3_b")),
            k.col(A + "li2_b"), row_of(a[A + "li3_b"]))
        add_rows(nc, k, base)


def add_rows(nc, k, rows):
    with stage(nc) as (block,):
        @block.vector
        def _(dve):
            dve.tensor_tensor(k.x[:, :, :], k.x[:, :, :], rows[:, :, :], ALU.add)


def layer_norm_rows(nc, k, src, dst, gain, a=None):
    with ExitStack() as held:
        sb = tiles(nc, held)
        mean, rstd = sb("mean", [P, T]), sb("rstd", [P, T])
        gb = sb("gb", [P, 2, D])
        ln_stats(nc, k, src, mean, rstd)
        with stage(nc, "gain_loaded", "normed", "scaled") as (block, gain_loaded, normed, scaled):
            @block.sync
            def _(sp):
                if gain is not None:
                    for j, n in enumerate(gain):
                        sp.dma_start(gb[:, j, :], row_of(a[n]).to_broadcast([P, D])).then_inc(gain_loaded, 16)

            @block.vector
            def _(dve):
                with dve.Fori(0, T) as t:
                    dve.tensor_scalar(dst[:, t, :], src[:, t, :], mean[:, bass.ds(t, 1)], rstd[:, bass.ds(t, 1)],
                                      ALU.subtract, ALU.mult).then_inc(normed, 1)
                if gain is not None:
                    dve.wait_ge(gain_loaded, 32)
                    dve.wait_ge(normed, T)
                    dve.tensor_tensor(dst[:, :, :], dst[:, :, :], gb[:, 0:1, :].to_broadcast([P, T, D]),
                                      ALU.mult).then_inc(scaled, 1)
                    dve.wait_ge(scaled, 1)
                    dve.tensor_tensor(dst[:, :, :], dst[:, :, :], gb[:, 1:2, :].to_broadcast([P, T, D]), ALU.add)



def layer3_attention(nc, k, a):
    with ExitStack() as held:
        sb = tiles(nc, held)
        QT = sb("QT", [P, KD, TOK])
        KT = sb("KT", [P, KD, BATCH, CTX])
        V = sb("V", [P, BATCH, D])
        with ExitStack() as front:
            sb2 = tiles(nc, front)
            mean, rstd = sb2("mean", [P, T]), sb2("rstd", [P, T])
            wqs, wks, wvs, bvs = sb2("wqs", [P, KD, D]), sb2("wks", [P, D]), sb2("wvs", [P, D]), sb2("bvs", [1, D])
            ln_stats(nc, k, k.x, mean, rstd)
            project(nc, k, k.x, mean, rstd, [None], [(wqs, 0, QT, k.col("L3_xattn_bq"), 1.0)], [],
                    [(wqs[:, :, :], turned_weights(a["L3_xattn_Wq"]))])
            with stage(nc, "wk_loaded", "wv_loaded", "k_ready", "v_ready") as (
                    block, wk_loaded, wv_loaded, k_ready, v_ready):
                @block.sync
                def _(sp):
                    sp.dma_start(wks[:, :], a["L3_xattn_Wk"]).then_inc(wk_loaded, 16)
                    sp.dma_start(wvs[:, :], a["L3_xattn_Wv"]).then_inc(wv_loaded, 16)
                    sp.dma_start(bvs[:, :], row_of(a["L3_xattn_bv"])).then_inc(wv_loaded, 16)

                @block.tensor
                def _(pe):
                    pe.wait_ge(wk_loaded, 16)
                    for b in range(BATCH):
                        for c in range(KD):
                            pe.matmul(k.ps[:, KD * b + c, 0:CTX], wks[:, c * P:(c + 1) * P], k.ctxT[:, b, :],
                                      start=True, stop=True).then_inc(k_ready, 1)
                    pe.wait_ge(wv_loaded, 32)
                    for b in range(BATCH):
                        pe.matmul(k.ps[0:CTX, 4 + b, 0:D], k.ctxT[:, b, :], wvs[:, :], start=True, stop=False)
                        pe.matmul(k.ps[0:CTX, 4 + b, 0:D], k.ones[0:1, 0:CTX], bvs[:, :], start=False,
                                  stop=True).then_inc(v_ready, 1)

                @block.vector
                def _(dve):
                    bk = k.col("L3_xattn_bk")
                    for b in range(BATCH):
                        for c in range(KD):
                            dve.wait_ge(k_ready, KD * b + c + 1)
                            dve.tensor_scalar(KT[:, c, b, :], k.ps[:, KD * b + c, 0:CTX], bk[:, c:c + 1], None, ALU.add)
                    for b in range(BATCH):
                        dve.wait_ge(v_ready, b + 1)
                        dve.tensor_copy(V[0:CTX, b, :], k.ps[0:CTX, 4 + b, 0:D])

        qs = sb("qs", [P, 2, KD, P])
        pr = sb("pr", [P, 2, CTX])
        pT = sb("pT", [P, 2, P])
        neg, rs, inv = sb("neg", [P, 2]), sb("rs", [P, 2]), sb("inv", [P, 2])
        with stage(nc, "q_staged", "s_ready", "max_done", "exp_done", "pt_ready", "pt_copied", "o_ready",
                   "inverse_done", "o_done") as (
                block, q_staged, s_ready, max_done, exp_done, pt_ready, pt_copied, o_ready, inverse_done, o_done):
            @block.gpsimd
            def _(pool):
                with pool.Fori(0, T // 2) as i:
                    pool.wait_ge(s_ready, 2 * i)
                    for u in range(2):
                        pool.tensor_copy(qs[:, u, :, :], QT[:, :, bass.ds((2 * i + u) * P, P)]).then_inc(q_staged, 1)

            @block.tensor
            def _(pe):
                with pe.Fori(0, BATCH) as b:
                    with pe.Fori(0, TB // 2) as j:
                        i = b * (TB // 2) + j
                        for u in range(2):
                            pe.wait_ge(q_staged, 2 * i + (u + 1))
                            pe.wait_ge(exp_done, 2 * i)
                            for c in range(KD):
                                mm = pe.matmul(k.ps[:, u, 0:CTX], qs[:, u, c, :], KT[:, c, bass.ds(b, 1), :].rearrange(
                                    "p a n -> p (a n)"), start=(c == 0), stop=(c == KD - 1))
                            mm.then_inc(s_ready, 1)
                        for u in range(2):
                            pe.wait_ge(exp_done, 2 * i + (u + 1))
                            pe.wait_ge(pt_copied, 2 * i)
                            pe.transpose(k.ps[0:CTX, 2 + u, 0:P], pr[:, u, :], k.ident[:, :]).then_inc(pt_ready, 1)
                        for u in range(2):
                            pe.wait_ge(pt_copied, 2 * i + (u + 1))
                            pe.wait_ge(o_done, 2 * i)
                            pe.matmul(k.ps[:, 4 + u, 0:D], pT[0:CTX, u, :], V[0:CTX, bass.ds(b, 1), :].rearrange(
                                "p a n -> p (a n)"), start=True, stop=True).then_inc(o_ready, 1)

            @block.scalar
            def _(act):
                with act.Fori(0, T // 2) as i:
                    for u in range(2):
                        act.wait_ge(max_done, 2 * i + (u + 1))
                        act.wait_ge(o_done, 2 * i)
                        act.activation(pr[:, u, :], k.ps[:, u, 0:CTX], ACT.Exp, bias=neg[:, u:u + 1],
                                       accum_out=rs[:, u:u + 1]).then_inc(exp_done, 1)
                    for u in range(2):
                        act.wait_ge(pt_ready, 2 * i + (u + 1))
                        act.activation(pT[0:CTX, u, :], k.ps[0:CTX, 2 + u, 0:P], ACT.Copy).then_inc(pt_copied, 1)

            @block.vector
            def _(dve):
                with dve.Fori(0, T // 2) as i:
                    for u in range(2):
                        dve.wait_ge(s_ready, 2 * i + (u + 1))
                        dve.tensor_reduce(neg[:, u:u + 1], k.ps[:, u, 0:CTX], AX.X, ALU.max,
                                          negate=True).then_inc(max_done, 1)
                    for u in range(2):
                        dve.wait_ge(o_ready, 2 * i + (u + 1))
                        dve.reciprocal(inv[:, u:u + 1], rs[:, u:u + 1]).then_inc(inverse_done, 1)
                        dve.wait_ge(inverse_done, 2 * i + (u + 1))
                        row = k.x[:, 2 * i + u, :]
                        dve.scalar_tensor_tensor(out=row, in0=k.ps[:, 4 + u, 0:D], scalar=inv[:, u:u + 1], in1=row,
                                                 op0=ALU.mult, op1=ALU.add).then_inc(o_done, 1)



LH = 8
LD = 64
LW = LH * LD


def shift_rows(nc, k, x, h):
    H = D // 2
    with stage(nc, "zeroed", "moved", "copied") as (block, zeroed, moved, copied):
        @block.vector
        def _(dve):
            for b in range(BATCH):
                dve.memset(h[0:1, b * TB, H:D], 0.0).then_inc(zeroed, 1)
            dve.tensor_copy(h[:, :, 0:H], x[:, :, 0:H]).then_inc(copied, 1)

        @block.sync
        def _(sp):
            sp.dma_start(h[1:P, :, H:D], x[0:P - 1, :, H:D]).then_inc(moved, 16)
            for b in range(BATCH):
                sp.dma_start(h[0:1, b * TB + 1:(b + 1) * TB, H:D],
                             x[P - 1:P, b * TB:(b + 1) * TB - 1, H:D]).then_inc(moved, 16)
            sp.wait_ge(moved, 16 * (1 + BATCH))


def local_qkv(nc, k, a, layer, h, ws, bb, QT, KT, V):
    with ExitStack() as held:
        sb = tiles(nc, held)
        cosT = sb("cosT", [P, TB, 2, LD])
        sinT = sb("sinT", [P, TB, 2, LD])
        qks = sb("qks", [P, 2, LD])
        qkw = sb("qkw", [P, 2, LD])
        with stage(nc, "tables_loaded", "scaled") as (block, tables_loaded, scaled):
            @block.sync
            def _(sp):
                sp.dma_start(cosT[:, :, :, :], a["rotary_cos"]).then_inc(tables_loaded, 16)
                sp.dma_start(sinT[:, :, :, :], a["rotary_sin"]).then_inc(tables_loaded, 16)
                for j, n in enumerate(("L2_ffn_q_scale", "L2_ffn_k_scale")):
                    v = a[n][layer:layer + 1, :]
                    sp.dma_start(qks[:, j, :], v.to_broadcast([P, LD])).then_inc(tables_loaded, 16)
                    for m in range(2):
                        sp.dma_start(qkw[:, j, m * LD // 2:(m + 1) * LD // 2],
                                     v[:, (1 - m) * LD // 2:(2 - m) * LD // 2].to_broadcast([P, LD // 2])
                                     ).then_inc(tables_loaded, 16)
                sp.wait_ge(tables_loaded, 16 * 8)

            @block.vector
            def _(dve):
                dve.wait_ge(tables_loaded, 16 * 8)
                for tab, sc in ((cosT, qks), (sinT, qkw)):
                    dve.tensor_tensor(tab[:, :, :, :], tab[:, :, :, :],
                                      sc[:, :, :].unsqueeze(1).to_broadcast([P, TB, 2, LD]), ALU.mult)

        xn = sb("xn", [P, GT, D])
        xT = sb("xT", [P, KD, GN])
        sq = sb("sq", [P, 2 * LH, LD])
        ab = sb("ab", [P, 2, 2 * LH, LD])
        qk = sb("qk", [P, 2, 2, LW])
        ss = sb("ss", [P, 2 * LH])
        root = sb("root", [P, 2 * LH])
        rn = sb("rn", [P, 2, 2 * LH])
        psT = k.ps[:, 0:2, :]
        CH = 6
        heads = lambda ap: ap.rearrange("p b (h w) -> p b h w", w=LD)
        with stage(nc, "w_loaded", "normed", "turned", "copied", "qk_ready", "qk_out", "v_ready", "v_out", "squared", "products",
                   "summed", "ss_ready", "root_ready", "chain", "rotated", "qkt_ready", "qkt_out") as (
                block, w_loaded, normed, turned, copied, qk_ready, qk_out, v_ready, v_out, squared, products,
                summed, ss_ready, root_ready, chain, rotated, qkt_ready, qkt_out):
            @block.sync
            def _(sp):
                sp.dma_start(ws[:, :, :], turned_weights(a["L2_ffn_wqkv"][layer])).then_inc(w_loaded, 16)

            @block.tensor
            def _(pe):
                def turn_qk(g, u):
                    for j in range(2):
                        pe.wait_ge(rotated, g * GT + (u + 1))
                        pe.wait_ge(qkt_out, g * 2 * GT + (2 * u + j))
                        flat = ab[:, u % 2, :, :].rearrange("p h w -> p (h w)")
                        for c in range(4):
                            mm = pe.transpose(k.ps[:, 7, c * P:(c + 1) * P],
                                              flat[:, (4 * j + c) * P:(4 * j + c + 1) * P], k.ident[:, :])
                        mm.then_inc(qkt_ready, 1)

                with pe.Fori(0, G) as g:
                    turn_group(pe, g, k, xn, psT, normed, turned, copied, 1)
                    pe.wait_ge(w_loaded, 16)
                    pe.wait_ge(copied, (g + 1) * 2)
                    for u in range(GT):
                        pe.wait_ge(qk_out, g * GT + max(u - 1, 0))
                        for j in range(3):
                            if j == 2:
                                pe.wait_ge(v_out, g * GT + u)
                            out = k.ps[:, 6, :] if j == 2 else k.ps[:, 2 + 2 * (u % 2) + j, :]
                            for c in range(KD):
                                mm = pe.matmul(out, xT[:, c, u * P:(u + 1) * P], ws[:, c, j * LW:(j + 1) * LW],
                                               start=(c == 0), stop=(c == KD - 1))
                            if j:
                                mm.then_inc(qk_ready if j == 1 else v_ready, 1)
                        if u:
                            turn_qk(g, u - 1)
                    turn_qk(g, GT - 1)

            @block.scalar
            def _(act):
                def copy_qk(g, u):
                    for j, dst in enumerate((QT, KT)):
                        act.wait_ge(qkt_ready, g * 2 * GT + (2 * u + j + 1))
                        at = (g * GT + u + 1) * P
                        act.activation(dst[:, :, bass.ds(at, P)], k.ps[:, 7, :].rearrange("p (c n) -> p c n", c=4),
                                       ACT.Copy).then_inc(qkt_out, 1)

                with act.Fori(0, G) as g:
                    copy_group(act, g, [xT], psT, [None], turned, copied, v_ready, GT)
                    for u in range(GT):
                        act.wait_ge(qk_ready, g * GT + (u + 1))
                        act.wait_ge(products, g * GT + max(u - 1, 0))
                        act.activation(qk[:, u % 2, :, :], k.ps[:, 2 + 2 * (u % 2):4 + 2 * (u % 2), :],
                                       ACT.Copy).then_inc(qk_out, 1)
                        act.wait_ge(qk_out, g * GT + (u + 1))
                        act.wait_ge(ss_ready, g * GT + u)
                        act.activation(sq[:, :, :].rearrange("p h w -> p (h w)"),
                                       qk[:, u % 2, :, :].rearrange("p b n -> p (b n)"), ACT.Square).then_inc(squared, 1)
                        act.wait_ge(v_ready, g * GT + (u + 1))
                        act.activation(V[:, :, bass.ds(g * GT + u + 1, 1), :].rearrange("p a t n -> p (a t) n"),
                                       k.ps[:, 6, :].rearrange("p (a n) -> p a n", a=4), ACT.Copy).then_inc(v_out, 1)
                        act.wait_ge(ss_ready, g * GT + (u + 1))
                        act.activation(root[:, :], ss[:, :], ACT.Sqrt).then_inc(root_ready, 1)
                        if u:
                            copy_qk(g, u - 1)
                    copy_qk(g, GT - 1)

            @block.vector
            def _(dve):
                with dve.Fori(0, BATCH) as b:
                    for gg in range(G // BATCH):
                        g = b * (G // BATCH) + gg
                        normalise_group(dve, g, xn, h, None, None, turned, normed)
                        for u in range(GT):
                            i = gg * GT + u
                            A, B = ab[:, u % 2, :, :], bb[:, :, :]
                            two = lambda ap: ap.rearrange("p (b h) w -> p b h w", b=2)
                            H = LD // 2
                            dve.wait_ge(qk_out, g * GT + (u + 1))
                            dve.wait_ge(qkt_ready, g * 2 * GT + max(2 * (u - 1), 0))
                            dve.wait_ge(summed, g * GT + u)
                            dve.tensor_tensor(two(A), heads(qk[:, u % 2, :, :]),
                                              cosT[:, i, :, :].unsqueeze(2).to_broadcast([P, 2, LH, LD]), ALU.mult)
                            for m in range(2):
                                ins = dve.tensor_tensor(
                                    two(B)[:, :, :, m * H:(m + 1) * H], heads(qk[:, u % 2, :, :])[:, :, :, (1 - m) * H:(2 - m) * H],
                                    sinT[:, i, :, m * H:(m + 1) * H].unsqueeze(2).to_broadcast([P, 2, LH, H]), ALU.mult)
                            ins.then_inc(products, 1)
                            dve.wait_ge(squared, g * GT + (u + 1))
                            dve.wait_ge(root_ready, g * GT + u)
                            dve.tensor_reduce(ss[:, :], sq[:, :, :], AX.X, ALU.add).then_inc(ss_ready, 1)
                            dve.wait_ge(root_ready, g * GT + (u + 1))
                            step = Chain(dve, chain, (g * GT + u) * CH)
                            r0, r1 = rn[:, 0, :], rn[:, 1, :]
                            step(dve.tensor_scalar(root[:, :], root[:, :], 1e-12, None, ALU.max))
                            step(dve.reciprocal(r0, root[:, :]))
                            step(dve.tensor_tensor(r0, r0, ss[:, :], ALU.mult))
                            step(dve.tensor_tensor(r0, r0, root[:, :], ALU.add))
                            step(dve.tensor_scalar(r0, r0, 0.5, 1e-12, ALU.mult, ALU.max))
                            step(dve.reciprocal(r1, r0))
                            assert step.n == CH
                            dve.wait_ge(summed, g * GT + (u + 1))
                            dve.tensor_tensor(A, A, r1.unsqueeze(2).to_broadcast([P, 2 * LH, LD]),
                                              ALU.mult).then_inc(rotated, 1)

            @block.gpsimd
            def _(pool):
                with pool.Fori(0, G) as g:
                    for u in range(GT):
                        pool.wait_ge(products, g * GT + (u + 1))
                        A, B = ab[:, u % 2, :, :], bb[:, :, :]
                        pool.tensor_tensor(A, A, B, ALU.add).then_inc(summed, 1)


def local_attention(nc, k, QT, KT, V, O):
    HB = P // LD
    with ExitStack() as held:
        sb = tiles(nc, held)
        mask = sb("mask", [P, TB, 2, 2 * P], BF16)
        ident16 = sb("ident16", [P, P], BF16)
        qz = sb("qz", [P, 2, 4, HB, P])
        pr = sb("pr", [P, 2, 4, 2 * P])
        pT = sb("pT", [P, 2, 8, P])
        neg, rs, inv = sb("neg", [P, 2, 4]), sb("rs", [P, 4, 4]), sb("inv", [P, 2, 4])
        with stage(nc, "pool_step") as (block, pool_step):
            @block.gpsimd
            def _(pool):
                step = Chain(pool, pool_step)
                step(pool.memset(mask[:, :, :, :], 0.0))
                for j in range(2):
                    m = mask[:, :, j, 0:P]
                    step(pool.affine_select(out=m, in_=m, compare_op=ALU.is_ge, fill=NEG, base=0,
                                            pattern=[[0, TB], [1, P]], channel_multiplier=-1))
                    m = mask[:, :, j, P:2 * P]
                    step(pool.affine_select(out=m, in_=m, compare_op=ALU.is_ge, fill=NEG, base=0,
                                            pattern=[[0, TB], [-1, P]], channel_multiplier=1))
                    step(pool.memset(mask[:, 0, j, 0:P], NEG))
                step(pool.tensor_copy(ident16[:, :], k.ident[:, :]))
                pool.memset(qz[:, :, :, :, :], 0.0)
        N4 = 4
        with stage(nc, "q_staged", "s_ready", "max_done", "exp_done", "pt_ready", "pt_copied", "o_ready",
                   "inverse_done", "o_done") as (
                block, q_staged, s_ready, max_done, exp_done, pt_ready, pt_copied, o_ready, inverse_done, o_done):
            @block.gpsimd
            def _(pool):
                with pool.Fori(0, T // 2) as i:
                    for u in range(2):
                        pool.wait_ge(s_ready, i * N4)
                        for e in range(HB):
                            r = slice(e * LD, (e + 1) * LD)
                            pool.tensor_copy(qz[r, u, :, e, :], QT[r, :, bass.ds((2 * i + u + 1) * P, P)]
                                             ).then_inc(q_staged, 1)
                            pool.wait_ge(q_staged, 2 * HB * i + (HB * u + e + 1))

            @block.tensor
            def _(pe):
                def scores(b, j, i, c):
                    u, half = c // 2, c % 2
                    pe.wait_ge(q_staged, 2 * HB * i + HB * (u + 1))
                    pe.wait_ge(exp_done, i * N4 + max(c - 1, 0))
                    for m in range(2):
                        bank = k.ps[:, 2 * (c % 2) + m, :]
                        pe.matmul(bank, ident16[:, :], mask[:, bass.ds(2 * j + u, 1), :, :].rearrange(
                            "p a b n -> p (a b n)"), start=True, stop=False)
                        for e in range(HB):
                            blk = 2 * half + m
                            mm = pe.matmul(bank[:, e * 2 * P:(e + 1) * 2 * P], qz[:, u, blk, e, :],
                                           KT[:, blk, bass.ds((2 * i + u) * P, 2 * P)], start=False, stop=(e == 1))
                    mm.then_inc(s_ready, 1)

                def turn(i, c):
                    pe.wait_ge(exp_done, i * N4 + (c + 1))
                    pe.wait_ge(pt_copied, i * N4 + c)
                    flat = pr[:, c % 2, :, :].rearrange("p h n -> p (h n)")
                    for m in range(8):
                        mm = pe.transpose(k.ps[:, 4 + m // 4, m % 4 * P:(m % 4 + 1) * P], flat[:, m * P:(m + 1) * P],
                                          k.ident[:, :])
                    mm.then_inc(pt_ready, 1)

                def values(i, c):
                    u, half = c // 2, c % 2
                    pe.wait_ge(pt_copied, i * N4 + (c + 1))
                    pe.wait_ge(o_done, i * N4 + max(c - 1, 0))
                    for hh in range(4):
                        h = 4 * half + hh
                        for w in range(2):
                            mm = pe.matmul(k.ps[:, 6 + c % 2, hh * LD:(hh + 1) * LD], pT[:, c % 2, 2 * hh + w, :],
                                           V[:, h // HB, bass.ds(2 * i + u + w, 1), h % HB * LD:(h % HB + 1) * LD].rearrange(
                                               "p t n -> p (t n)"), start=(w == 0), stop=(w == 1))
                    mm.then_inc(o_ready, 1)

                with pe.Fori(0, BATCH) as b:
                    with pe.Fori(0, TB // 2) as j:
                        i = b * (TB // 2) + j
                        scores(b, j, i, 0)
                        for c in range(N4):
                            if c + 1 < N4:
                                scores(b, j, i, c + 1)
                            turn(i, c)
                            if c:
                                values(i, c - 1)
                        values(i, N4 - 1)

            def copy_pt(eng, i, c):
                eng.wait_ge(pt_ready, i * N4 + (c + 1))
                eng.wait_ge(o_ready, i * N4 + max(c - 1, 0))
                src = k.ps[:, 4:6, :].rearrange("p a n -> p (a n)")
                dst = pT[:, c % 2, :, :].rearrange("p a n -> p (a n)")
                if eng is nc.scalar:
                    eng.activation(dst, src, ACT.Copy).then_inc(pt_copied, 1)
                else:
                    eng.tensor_copy(dst, src).then_inc(pt_copied, 1)

            @block.scalar
            def _(act):
                def exps(i, c):
                    act.wait_ge(max_done, i * N4 + (c + 1))
                    act.wait_ge(pt_ready, i * N4 + max(c - 1, 0))
                    act.wait_ge(o_done, i * N4 + max(c - 3, 0))
                    for hh in range(4):
                        ins = act.activation(pr[:, c % 2, hh, :], k.ps[:, 2 * (c % 2) + hh // 2,
                                                                     hh % 2 * 2 * P:(hh % 2 + 1) * 2 * P],
                                             ACT.Exp, bias=neg[:, c % 2, hh:hh + 1], accum_out=rs[:, c, hh:hh + 1])
                    ins.then_inc(exp_done, 1)

                with act.Fori(0, T // 2) as i:
                    for c in range(N4):
                        exps(i, c)

            @block.vector
            def _(dve):
                def maxima(i, c):
                    dve.wait_ge(s_ready, i * N4 + (c + 1))
                    dve.tensor_reduce(neg[:, c % 2, :], k.ps[:, 2 * (c % 2):2 * (c % 2) + 2, :].rearrange(
                        "p b (h n) -> p (b h) n", h=2), AX.X, ALU.max, negate=True).then_inc(max_done, 1)

                def normal(i, c):
                    u, half = c // 2, c % 2
                    dve.wait_ge(o_ready, i * N4 + (c + 1))
                    dve.reciprocal(inv[:, c % 2, :], rs[:, c, :]).then_inc(inverse_done, 1)
                    dve.wait_ge(inverse_done, i * N4 + (c + 1))
                    dve.tensor_tensor(
                        O[:, 2 * half:2 * half + 2, bass.ds(2 * i + u, 1), :].rearrange(
                            "p a t (h w) -> p (a t) h w", w=LD),
                        k.ps[:, 6 + c % 2, 0:4 * LD].rearrange("p (a h w) -> p a h w", a=2, w=LD),
                        inv[:, c % 2, :].rearrange("p (a h) -> p a h", a=2).unsqueeze(3).to_broadcast([P, 2, 2, LD]),
                        ALU.mult).then_inc(o_done, 1)

                with dve.Fori(0, T // 2) as i:
                    maxima(i, 0)
                    for c in range(N4):
                        if c + 1 < N4:
                            maxima(i, c + 1)
                        copy_pt(dve, i, c)
                        if c:
                            normal(i, c - 1)
                    normal(i, N4 - 1)


def layer2_ffn(nc, k, a):
    with ExitStack() as held:
        y = tiles(nc, held)("y_rows", [P, T, D])
        layer_norm_rows(nc, k, k.x, y, None)
        for layer in range(2):
            with ExitStack() as outer:
                O = tiles(nc, outer)("O", [P, 4, T, P])
                with ExitStack() as inner:
                    sb = tiles(nc, inner)
                    QT, KT = sb("QT", [P, 4, TOK + P]), sb("KT", [P, 4, TOK + P])
                    V = sb("V", [P, 4, T + 1, P])
                    flat = O[:, :, :, :].rearrange("p a t n -> p (a t n)")
                    h = flat[:, 0:T * D].rearrange("p (t d) -> p t d", d=D)
                    ws = flat[:, T * D:T * D + KD * 3 * LW].rearrange("p (c n) -> p c n", c=KD)
                    bb = flat[:, T * D + KD * 3 * LW:T * D + KD * 3 * LW + 2 * LW].rearrange("p (h w) -> p h w", w=LD)
                    shift_rows(nc, k, y, h)
                    with stage(nc, "zeroed") as (block, zeroed):
                        @block.gpsimd
                        def _(pool):
                            pool.memset(KT[:, :, 0:P], 0.0)
                            pool.memset(V[:, :, 0, :], 0.0)
                    local_qkv(nc, k, a, layer, h, ws, bb, QT, KT, V)
                    local_attention(nc, k, QT, KT, V, O)
                out_project(nc, k, O, a["L2_ffn_wo"][layer], None, y)
            with ExitStack() as inner:
                h = tiles(nc, inner)("h", [P, T, D])
                shift_rows(nc, k, y, h)
                C = f"L2_ffn_{layer}_"
                ffn(nc, k, h, y, a["L2_ffn_w1"][layer], a["L2_ffn_w2"][layer],
                    (k.col(C + "ln_g"), k.col(C + "ln_b")), k.col(C + "b1"), a["L2_ffn_b2"][layer:layer + 1, :], glu=True)
        add_rows(nc, k, y)



E = 8


def layer0_ffn(nc, k, a):
    NT = 4
    NF = 2
    with ExitStack() as held:
        sb = tiles(nc, held)
        mean, rstd = sb("mean", [P, NT]), sb("rstd", [P, NT])
        xn = sb("xn", [P, GT, D])
        xT = sb("xT", [P, KD, GN])
        bias_cols = k.col("L0_ffn_gate_up_proj_bias")
        gu = [sb(f"gu{e}", [P, KD, 4 * P]) for e in range(2)]
        dn = [sb(f"dn{e}", [P, NF, D]) for e in range(2)]
        gate, up, sig = (sb(n, [P, NF, GN]) for n in ("gate", "up", "sig"))
        inter = sb("inter", [P, 2, NF, GN])
        idx, idf = sb("idx", [P, NT, 2], I32), sb("idf", [P, NT, 2])
        rw = sb("rw", [P, NT, E])
        pick = sb("pick", [P, 2, NT, E])
        weight = sb("weight", [P, NT, E])
        weightT = sb("weightT", [E, NT, P])
        bd = sb("bd", [E, D])
        psT = k.ps[:, 0:2, :]
        ln_stats(nc, k, k.x, mean, rstd, n=NT)
        with stage(nc, "loaded", "normed", "turned", "copied", "h_ready", "picked", "weights_turned",
                   "weights_copied", "y_ready") as (
                block, loaded, normed, turned, copied, h_ready, picked, weights_turned, weights_copied, y_ready):
            @block.sync
            def _(sp):
                sp.dma_start(idx[:, :, :], a["L0_ffn_router_indices"].rearrange("(t p) k -> p t k", p=P)
                             ).then_inc(loaded, 16)
                sp.dma_start(rw[:, :, :], a["L0_ffn_routing_weights"].rearrange("(t p) e -> p t e", p=P)
                             ).then_inc(loaded, 16)
                sp.dma_start(bd[:, :], a["L0_ffn_down_proj_bias"]).then_inc(loaded, 16)
                sp.wait_ge(loaded, 48)

            @block.vector
            def _(dve):
                normalise_group(dve, 0, xn, k.x, mean, rstd, turned, normed)
                step = Chain(dve, picked)
                dve.wait_ge(loaded, 48)
                step(dve.tensor_copy(idf[:, :, :], idx[:, :, :]))
                for j in range(2):
                    ins = dve.tensor_tensor(pick[:, j], idf[:, :, j:j + 1].to_broadcast([P, NT, E]),
                                            k.eidx[:, :].unsqueeze(1).to_broadcast([P, NT, E]), ALU.is_equal)
                    step(ins)
                step(dve.tensor_tensor(pick[:, 0], pick[:, 0], pick[:, 1], ALU.add))
                step(dve.tensor_tensor(weight[:, :, :], pick[:, 0], rw[:, :, :], ALU.mult))
                dve.wait_ge(weights_turned, 1)
                dve.tensor_copy(weightT[:, :, :].rearrange("p t n -> p (t n)"), k.ps[0:E, 2, :]).then_inc(weights_copied, 1)
                for t in range(NT):
                    dve.wait_ge(y_ready, t + 1)
                    dve.tensor_tensor(k.x[:, t, :], k.x[:, t, :], k.ps[:, 3 + t, 0:D], ALU.add)

            @block.tensor
            def _(pe):
                turn_group(pe, 0, k, xn, psT, normed, turned, copied, 1)
                pe.wait_ge(picked, 5)
                for t in range(NT):
                    mm = pe.transpose(k.ps[0:E, 2, t * P:(t + 1) * P], weight[:, t, :], k.ident[:, :])
                mm.then_inc(weights_turned, 1)
                pe.wait_ge(weights_copied, 1)
                pe.wait_ge(loaded, 48)
                for t in range(NT):
                    pe.matmul(k.ps[:, 3 + t, 0:D], weightT[:, t, :], bd[:, :], start=True, stop=True).then_inc(y_ready, 1)

            @block.scalar
            def _(act):
                copy_group(act, 0, [xT], psT, [None], turned, copied, h_ready, 1)

        with stage(nc, "first_loaded", "second_loaded", "h_ready", "h_read", "gate_ready", "up_ready", "sig_ready",
                   "prod_ready", "inter_done", "y_ready", "y_added") as (
                block, first_loaded, second_loaded, h_ready, h_read, gate_ready, up_ready, sig_ready,
                prod_ready, inter_done, y_ready, y_added):
            w_loaded = (first_loaded, second_loaded)

            @block.sync
            def _(sp):
                with sp.Fori(0, E // 2) as i:
                    for e in range(2):
                        sp.wait_ge(y_ready, 2 * NT * i)
                        sp.dma_start(gu[e][:, :, :], a["L0_ffn_gate_up_proj"][bass.ds(2 * i + e, 1)].rearrange(
                            "e (c p) f -> p (e c) f", p=P)).then_inc(w_loaded[e], 16)
                        sp.dma_start(dn[e][:, :, :], a["L0_ffn_down_proj"][bass.ds(2 * i + e, 1)].rearrange(
                            "e (c p) f -> p (e c) f", p=P)).then_inc(w_loaded[e], 16)

            @block.tensor
            def _(pe):
                def hidden(i, e):
                    pe.wait_ge(w_loaded[e], 32 * (i + 1))
                    for f in range(NF):
                        pe.wait_ge(h_read, 2 * NF * i + max(NF * e + f - 1, 0))
                        for half in range(2):
                            for c in range(KD):
                                at = (NF * half + f) * P
                                mm = pe.matmul(k.ps[:, 2 * f + half, :], gu[e][:, c, at:at + P], xT[:, c, :],
                                               start=(c == 0), stop=(c == KD - 1))
                        mm.then_inc(h_ready, 1)

                def down(i, e):
                    pe.wait_ge(inter_done, 2 * NF * i + NF * (e + 1))
                    for t in range(NT):
                        pe.wait_ge(y_added, 2 * NT * i + max(NT * e + t - 3, 0))
                        for f in range(NF):
                            mm = pe.matmul(k.ps[:, 4 + t, 0:D], inter[:, e, f, t * P:(t + 1) * P], dn[e][:, f, :],
                                           start=(f == 0), stop=(f == NF - 1))
                        mm.then_inc(y_ready, 1)

                with pe.Fori(0, E // 2) as i:
                    hidden(i, 0)
                    hidden(i, 1)
                    down(i, 0)
                    down(i, 1)

            @block.vector
            def _(dve):
                def gates(i, e):
                    dve.wait_ge(inter_done, 2 * NF * i + NF * e)
                    for f in range(NF):
                        n = 2 * NF * i + NF * e + f
                        col = lambda half: bias_cols[:, bass.ds((2 * i + e) * 4 + NF * half + f, 1)]
                        dve.wait_ge(h_ready, n + 1)
                        dve.tensor_scalar(gate[:, f, :], k.ps[:, 2 * f, :], col(0), 7.0, ALU.add,
                                          ALU.min).then_inc(gate_ready, 1)
                        dve.tensor_scalar(up[:, f, :], k.ps[:, 2 * f + 1, :], col(1), 7.0, ALU.add,
                                          ALU.min).then_inc(h_read, 1)
                        dve.wait_ge(h_read, n + 1)
                        dve.tensor_scalar(up[:, f, :], up[:, f, :], -7.0, 1.0, ALU.max, ALU.add).then_inc(up_ready, 1)
                    for f in range(NF):
                        n = 2 * NF * i + NF * e + f
                        dve.wait_ge(sig_ready, n + 1)
                        dve.wait_ge(prod_ready, n + 1)
                        dve.tensor_tensor(inter[:, e, f, :], up[:, f, :], sig[:, f, :], ALU.mult).then_inc(inter_done, 1)

                with dve.Fori(0, E // 2) as i:
                    gates(i, 0)
                    gates(i, 1)
                    for e in range(2):
                        for t in range(NT):
                            dve.wait_ge(y_ready, 2 * NT * i + (NT * e + t + 1))
                            row = k.x[:, t, :]
                            dve.scalar_tensor_tensor(out=row, in0=k.ps[:, 4 + t, 0:D],
                                                     scalar=weight[:, t, bass.ds(2 * i + e, 1)], in1=row,
                                                     op0=ALU.mult, op1=ALU.add).then_inc(y_added, 1)

            @block.gpsimd
            def _(pool):
                with pool.Fori(0, E // 2) as i:
                    for m in range(2 * NF):
                        pool.wait_ge(up_ready, 2 * NF * i + (m + 1))
                        u = up[:, m % NF, :]
                        pool.tensor_tensor(u, u, gate[:, m % NF, :], ALU.mult).then_inc(prod_ready, 1)

            @block.scalar
            def _(act):
                with act.Fori(0, E // 2) as i:
                    for m in range(2 * NF):
                        act.wait_ge(gate_ready, 2 * NF * i + (m + 1))
                        act.wait_ge(inter_done, 2 * NF * i + max(m - 1, 0))
                        act.activation(sig[:, m % NF, :], gate[:, m % NF, :], ACT.Sigmoid,
                                       scale=1.702).then_inc(sig_ready, 1)



def route(nc, k, rows, wg, cap, top, slots, gather_at, scatter_at, weights):
    with ExitStack() as held:
        sb = tiles(nc, held)
        wgs = sb("wgs", [P, KD, E])
        xn = sb("xn", [P, GT, D])
        xT = sb("xT", [P, KD, GN])
        psT = k.ps[:, 0:2, :]
        with stage(nc, "w_loaded", "normed", "turned", "copied", "logits_ready") as (
                block, w_loaded, normed, turned, copied, logits_ready):
            @block.sync
            def _(sp):
                sp.dma_start(wgs[:, :, :], turned_weights(wg)).then_inc(w_loaded, 16)

            @block.vector
            def _(dve):
                with dve.Fori(0, G) as g:
                    normalise_group(dve, g, xn, rows, None, None, turned, normed)

            @block.scalar
            def _(act):
                with act.Fori(0, G) as g:
                    copy_group(act, g, [xT], psT, [None], turned, copied, logits_ready, GT)

            @block.tensor
            def _(pe):
                pe.wait_ge(w_loaded, 16)
                with pe.Fori(0, G) as g:
                    turn_group(pe, g, k, xn, psT, normed, turned, copied, 1)
                    pe.wait_ge(copied, (g + 1) * 2)
                    for u in range(GT):
                        for c in range(KD):
                            mm = pe.matmul(k.ps[:, 2, bass.ds((g * GT + u) * E, E)], xT[:, c, u * P:(u + 1) * P],
                                           wgs[:, c, :], start=(c == 0), stop=(c == KD - 1))
                        mm.then_inc(logits_ready, 1)

        lg = sb("lg", [P, T, E])
        less = sb("less", [P, T, E])
        cand = sb("cand", [P, T, E])
        oh = sb("oh", [P, top, T, E])
        best, first = sb("best", [P, 2, T]), sb("first", [P, 2, T])
        e8 = sb("e8", [P, E])
        gate = sb("gate", [P, 2, T])
        dif, den = sb("dif", [P, T]), sb("den", [P, T])
        total = sb("total", [P, E])
        all_total = sb("all_total", [P, T, E])
        spare = sb("spare", [P, top, T])
        rank, keep, slot = (sb(n, [P, T]) for n in ("rank", "keep", "slot"))
        wide = lambda v: v.unsqueeze(2).to_broadcast([P, T, E])
        experts = lambda v: v.unsqueeze(1).to_broadcast([P, T, E])
        flat = lambda v: v.rearrange("p t e -> p (t e)")
        with stage(nc, "dve_step", "exp_asked", "exp_done", "chosen", "ranked", "spare_made") as (
                block, dve_step, exp_asked, exp_done, chosen, ranked, spare_made):
            @block.gpsimd
            def _(pool):
                pool.iota(spare[:, :, :], pattern=[[TOK, top], [P, T]], base=slots, channel_multiplier=1,
                          allow_small_or_imprecise_dtypes=True).then_inc(spare_made, 1)

            @block.vector
            def _(dve):
                step = Chain(dve, dve_step)

                def first_best(values, j):
                    step(dve.tensor_reduce(best[:, j, :], values, AX.X, ALU.max))
                    step(dve.tensor_tensor(cand[:, :, :], values, wide(best[:, j, :]), ALU.is_equal))
                    step(dve.tensor_tensor(cand[:, :, :], cand[:, :, :], experts(e8[:, :]), ALU.mult))
                    step(dve.tensor_reduce(first[:, j, :], cand[:, :, :], AX.X, ALU.min))
                    step(dve.tensor_tensor(oh[:, j], experts(e8[:, :]), wide(first[:, j, :]), ALU.is_equal))

                step(dve.tensor_scalar(e8[:, :], k.eidx[:, :], -8.0, None, ALU.add))
                step(dve.tensor_copy(flat(lg[:, :, :]), k.ps[:, 2, 0:T * E]))
                if top == 2:
                    first_best(lg[:, :, :], 0)
                    step(dve.scalar_tensor_tensor(out=less[:, :, :], in0=oh[:, 0], scalar=NEG, in1=lg[:, :, :],
                                                  op0=ALU.mult, op1=ALU.add))
                    first_best(less[:, :, :], 1)
                    dve.tensor_tensor(dif[:, :], best[:, 1, :], best[:, 0, :], ALU.subtract).then_inc(exp_asked, 1)
                    step(dve.tensor_reduce(total[:, :], oh[:, 0].rearrange("p t e -> p e t"), AX.X, ALU.add))
                    dve.tensor_copy(all_total[:, :, :], experts(total[:, :])).then_inc(chosen, 1)
                    dve.wait_ge(exp_done, 1)
                    step(dve.tensor_scalar(den[:, :], gate[:, 1, :], 1.0, None, ALU.add))
                    step(dve.reciprocal(gate[:, 0, :], den[:, :]))
                    step(dve.tensor_tensor(gate[:, 1, :], gate[:, 1, :], gate[:, 0, :], ALU.mult))
                else:
                    step(dve.tensor_reduce(best[:, 0, :], lg[:, :, :], AX.X, ALU.max))
                    dve.tensor_tensor(lg[:, :, :], lg[:, :, :], wide(best[:, 0, :]), ALU.subtract).then_inc(exp_asked, 1)
                    dve.wait_ge(exp_done, 1)
                    step(dve.tensor_reduce(den[:, :], less[:, :, :], AX.X, ALU.add))
                    step(dve.reciprocal(dif[:, :], den[:, :]))
                    step(dve.tensor_tensor(less[:, :, :], less[:, :, :], wide(dif[:, :]), ALU.mult))
                    first_best(less[:, :, :], 0)
                    step(dve.tensor_copy(gate[:, 0, :], best[:, 0, :]))
                    dve.tensor_copy(den[:, :], best[:, 0, :]).then_inc(chosen, 1)
                dve.wait_ge(spare_made, 1)
                for j in range(top):
                    dve.wait_ge(ranked, j + 1)
                    step(dve.tensor_tensor(flat(cand[:, :, :]), k.ps[:, 3 + j, 0:T * E], flat(oh[:, j]), ALU.mult))
                    step(dve.tensor_reduce(rank[:, :], cand[:, :, :], AX.X, ALU.add))
                    step(dve.tensor_scalar(keep[:, :], rank[:, :], float(cap), None, ALU.is_lt))
                    step(dve.tensor_tensor(weights[:, j, :], gate[:, j, :], keep[:, :], ALU.mult))
                    step(dve.tensor_scalar(slot[:, :], first[:, j, :], 8.0, float(cap), ALU.add, ALU.mult))
                    step(dve.tensor_tensor(slot[:, :], slot[:, :], rank[:, :], ALU.add))
                    step(dve.tensor_tensor(slot[:, :], slot[:, :], keep[:, :], ALU.mult))
                    step(dve.tensor_copy(gather_at[:, j, :], slot[:, :]))
                    step(dve.tensor_scalar(keep[:, :], keep[:, :], -1.0, 1.0, ALU.mult, ALU.add))
                    step(dve.tensor_tensor(keep[:, :], keep[:, :], spare[:, j, :], ALU.mult))
                    step(dve.tensor_tensor(slot[:, :], slot[:, :], keep[:, :], ALU.add))
                    step(dve.tensor_copy(scatter_at[:, j, :], slot[:, :]))

            @block.scalar
            def _(act):
                act.wait_ge(exp_asked, 1)
                if top == 2:
                    act.activation(gate[:, 1, :], dif[:, :], ACT.Exp).then_inc(exp_done, 1)
                else:
                    act.activation(less[:, :, :], lg[:, :, :], ACT.Exp).then_inc(exp_done, 1)

            @block.tensor
            def _(pe):
                pe.wait_ge(chosen, 1)
                for j in range(top):
                    mine = flat(oh[:, j])
                    out = k.ps[:, 3 + j, :]
                    pe.matmul(out[:, 0:T * E], k.upper[:, :], mine, start=True, stop=False)
                    if j:
                        pe.matmul(out[:, 0:T * E], k.ones[:, :], flat(all_total[:, :, :]), start=False, stop=False)
                    for s in range(1, T):
                        mm = pe.matmul(out[:, s * E:T * E], k.ones[:, :], mine[:, 0:(T - s) * E], start=False,
                                       stop=(s == T - 1))
                    mm.then_inc(ranked, 1)


def run_experts(nc, k, stored, sent, made, w1, w2, cap, b1, b2):
    NU = cap // P
    parts = 1 if cap <= 512 else 2
    CN = cap // parts
    NB = w2.shape[1] // P
    HN = parts * NB
    RING = 3
    pairs = [(u, min(2, NU - u)) for u in range(0, NU, 2)]
    NPR = len(pairs)
    with ExitStack() as held:
        sb = tiles(nc, held)
        w1s = [sb(f"w1s{e}", [P, KD, NB * P]) for e in range(2)]
        w2s = [sb(f"w2s{e}", [P, NB, D]) for e in range(2)]
        xs = [sb(f"xs{e}", [P, NU, D]) for e in range(2)]
        b2s = [sb(f"b2s{e}", [P, D]) for e in range(2)] if b2 is not None else None
        xT = sb("xT", [P, KD, cap])
        hT = sb("hT", [P, NB, cap])
        ys = [sb(f"ys{e}", [P, NU, D]) for e in range(2)]
        loads = 3 if b2 is None else 4
        with stage(nc, "first_loaded", "second_loaded", "turned", "copied", "h_ready", "h_done", "y_ready",
                   "y_copied") as (
                block, first_loaded, second_loaded, turned, copied, h_ready, h_done, y_ready, y_copied):
            loaded = (first_loaded, second_loaded)

            @block.sync
            def _(sp):
                with sp.Fori(0, E // 2) as i:
                    for e in range(2):
                        one = bass.ds(2 * i + e, 1)
                        sp.wait_ge(y_copied, 2 * NU * i)
                        sp.dma_start(xs[e][:, :, :], sent[bass.ds((2 * i + e) * cap, cap), :].rearrange(
                            "(p u) d -> p u d", u=NU)).then_inc(loaded[e], 16)
                        sp.dma_start(w1s[e][:, :, :], w1[one].rearrange("e (c p) f -> p (e c) f", p=P)
                                     ).then_inc(loaded[e], 16)
                        sp.dma_start(w2s[e][:, :, :], w2[one].rearrange("e (c p) f -> p (e c) f", p=P)
                                     ).then_inc(loaded[e], 16)
                        if b2 is not None:
                            sp.dma_start(b2s[e][:, :], b2[one, :].to_broadcast([P, D])).then_inc(loaded[e], 16)

            @block.gpsimd
            def _(pool):
                with pool.Fori(0, E // 2) as i:
                    for e in range(2):
                        pool.wait_ge(y_copied, 2 * NU * i + NU * (e + 1))
                        pool.dma_start(made[bass.ds((2 * i + e) * cap, cap), :].rearrange("(p u) d -> p u d", u=NU),
                                       ys[e][:, :, :]).then_inc(stored, 16)
                pool.wait_ge(stored, 16 * E)

            @block.tensor
            def _(pe):
                with pe.Fori(0, E // 2) as i:
                    for e in range(2):
                        pe.wait_ge(loaded[e], 16 * loads * (i + 1))
                        for n, (u, m) in enumerate(pairs):
                            pe.wait_ge(copied, 2 * NPR * i + max(NPR * e + n - 1, 0))
                            for v in range(m):
                                for c in range(KD):
                                    mm = pe.transpose(k.ps[:, n % 2, (c * m + v) * P:(c * m + v + 1) * P],
                                                      xs[e][:, u + v, c * P:(c + 1) * P], k.ident[:, :])
                            mm.then_inc(turned, 1)
                        pe.wait_ge(copied, 2 * NPR * i + NPR * (e + 1))
                        for n in range(HN):
                            at, j = n // NB * CN, n % NB
                            pe.wait_ge(h_done, 2 * HN * i + max(HN * e + n - RING + 1, 0))
                            for c in range(KD):
                                mm = pe.matmul(k.ps[:, 2 + n % RING, 0:CN], w1s[e][:, c, j * P:(j + 1) * P],
                                               xT[:, c, at:at + CN], start=(c == 0), stop=(c == KD - 1))
                            mm.then_inc(h_ready, 1)
                        pe.wait_ge(h_done, 2 * HN * i + HN * (e + 1))
                        for u in range(NU):
                            n = NU * e + u
                            pe.wait_ge(y_copied, 2 * NU * i + max(n - 2, 0))
                            for j in range(NB):
                                mm = pe.matmul(k.ps[:, 5 + n % 3, 0:D], hT[:, j, u * P:(u + 1) * P], w2s[e][:, j, :],
                                               start=(j == 0), stop=(j == NB - 1))
                            mm.then_inc(y_ready, 1)

            @block.scalar
            def _(act):
                with act.Fori(0, E // 2) as i:
                    for e in range(2):
                        act.wait_ge(y_ready, 2 * NU * i + NU * e)
                        for n in range(HN):
                            at, j = n // NB * CN, n % NB
                            act.wait_ge(h_ready, 2 * HN * i + (HN * e + n + 1))
                            bias = 0.0 if b1 is None else b1[:, bass.ds((2 * i + e) * NB + j, 1)]
                            act.activation(hT[:, j, at:at + CN], k.ps[:, 2 + n % RING, 0:CN],
                                           ACT.Gelu if b1 is None else ACT.Relu, bias=bias).then_inc(h_done, 1)

            @block.vector
            def _(dve):
                with dve.Fori(0, E // 2) as i:
                    for e in range(2):
                        for n, (u, m) in enumerate(pairs):
                            if n == 0:
                                dve.wait_ge(h_ready, 2 * HN * i + HN * e)
                            dve.wait_ge(turned, 2 * NPR * i + (NPR * e + n + 1))
                            dve.tensor_copy(xT[:, :, u * P:(u + m) * P], k.ps[:, n % 2, 0:KD * m * P].rearrange(
                                "p (c n) -> p c n", c=KD)).then_inc(copied, 1)
                        dve.wait_ge(stored, 16 * 2 * i)
                        if b2 is not None:
                            dve.wait_ge(loaded[e], 16 * loads * (i + 1))
                        for u in range(NU):
                            n = NU * e + u
                            dve.wait_ge(y_ready, 2 * NU * i + (n + 1))
                            psY = k.ps[:, 5 + n % 3, 0:D]
                            if b2 is None:
                                dve.tensor_copy(ys[e][:, u, :], psY).then_inc(y_copied, 1)
                            else:
                                dve.tensor_tensor(ys[e][:, u, :], psY, b2s[e][:, :], ALU.add).then_inc(y_copied, 1)


def mixture(nc, k, wg, w1, w2, cap, top, b1=None, b2=None):
    slots = E * cap
    ID = nc.next_id()
    sent = nc.dram_tensor(f"sent_{ID}", (slots + top * TOK, D), F32).ap()
    made = nc.dram_tensor(f"made_{ID}", (slots, D), F32).ap()
    rows_sent, rows_stored, *rows_fetched = k.mixture_sems[top]
    with ExitStack() as held:
        sb = tiles(nc, held)
        gather_at, scatter_at = (sb(n, [P, top, T], U32) for n in ("gather_at", "scatter_at"))
        weights = sb("weights", [P, top, T])
        with ExitStack() as inner:
            sb2 = tiles(nc, inner)
            rows = sb2("rows", [P, T, D])
            zeros = sb2("zeros", [P, 2048])
            layer_norm_rows(nc, k, k.x, rows, None)
            with stage(nc, "zeroed", "filled") as (block, zeroed, filled):
                @block.vector
                def _(dve):
                    dve.memset(zeros[:, :], 0.0).then_inc(zeroed, 1)

                @block.sync
                def _(sp):
                    n = slots * D // P // 2048
                    sp.wait_ge(zeroed, 1)
                    for j in range(n):
                        sp.dma_start(sent[0:slots, :].rearrange("(p r) d -> p (r d)", p=P)[:, j * 2048:(j + 1) * 2048],
                                     zeros[:, :]).then_inc(filled, 16)
                    sp.wait_ge(filled, 16 * n)
            route(nc, k, rows, wg, cap, top, slots, gather_at, scatter_at, weights)
            with stage(nc) as (block,):
                @block.gpsimd
                def _(pool):
                    for j in range(top):
                        for t in range(T):
                            pool.indirect_dma_start(
                                sent, bass.IndirectOffsetOnAxis(ap=scatter_at[:, j, t:t + 1], axis=0),
                                rows[:, t, :], None).then_inc(rows_sent, 16)
                    pool.wait_ge(rows_sent, 16 * top * T)
        run_experts(nc, k, rows_stored, sent, made, w1, w2, cap, b1, b2)
        back = sb("back", [P, top, T, D])
        with stage(nc, "added") as (block, added):
            @block.gpsimd
            def _(pool):
                for t in range(T):
                    for j in range(top):
                        pool.indirect_dma_start(
                            back[:, j, t, :], None, made,
                            bass.IndirectOffsetOnAxis(ap=gather_at[:, j, t:t + 1], axis=0)).then_inc(rows_fetched[t // GT], 16)

            @block.vector
            def _(dve):
                for g in range(G):
                    dve.wait_ge(rows_fetched[g], 16 * top * GT)
                    for j in range(top):
                        if j:
                            dve.wait_ge(added, g + 1)
                        for u in range(GT):
                            t = g * GT + u
                            row = k.x[:, t, :]
                            ins = dve.scalar_tensor_tensor(out=row, in0=back[:, j, t, :], scalar=weights[:, j, t:t + 1], in1=row,
                                                           op0=ALU.mult, op1=ALU.add)
                        if j == 0:
                            ins.then_inc(added, 1)


def layer1_ffn(nc, k, a):
    w1, w2 = a["L1_ffn_c_fc"], a["L1_ffn_c_proj"]
    cap = 2 * TOK * 5 // 4 // E
    cap += cap % 2
    mixture(nc, k, a["L1_ffn_w_g"], w1, w2, cap, 2)


def layer3_ffn(nc, k, a):
    mixture(nc, k, a["L3_ffn_wg"], a["L3_ffn_w1"], a["L3_ffn_w2"], TOK // E, 1, k.col("L3_ffn_b1"), a["L3_ffn_b2"])


LAYERS = [layer0_attention, layer0_ffn, layer1_attention, layer1_ffn, layer2_attention, layer2_ffn, layer3_attention,
          layer3_ffn]

COLUMNS = [("L0_xattn_bq", 2), ("L0_xattn_bk", 2)]
COLUMNS += [("L1_xattn_" + n, w) for n, w in [
    ("a1_lnx_g", 2), ("a1_lnx_b", 2), ("a1_lny_g", 2), ("a1_lny_b", 2), ("a1_ln3_g", 2), ("a1_ln3_b", 2),
    ("a1_li2_b", 8), ("a2_lnx_g", 2), ("a2_lnx_b", 2), ("a2_lny_g", 1), ("a2_lny_b", 1), ("a2_ln3_g", 2),
    ("a2_ln3_b", 2), ("a2_li2_b", 8)]]

COLUMNS += [("L0_ffn_gate_up_proj_bias", 32), ("L3_xattn_bq", 2), ("L3_xattn_bk", 2), ("L3_ffn_b1", 64)]
COLUMNS += [(f"L2_ffn_{layer}_{n}", w) for layer in range(2) for n, w in [("ln_g", 2), ("ln_b", 2), ("b1", 12)]]


def build(nc, a, out, layers=range(8)):
    ncols = sum(n for _, n in COLUMNS)
    with ExitStack() as held:
        sb = tiles(nc, held)

        class K:
            x = sb("x_rows", [P, T, D])
            ctx = sb("ctx_rows", [P, BATCH, IMG])
            ctxT = sb("ctxT", [P, BATCH, CTX])
            cols = sb("cols_sb", [P, ncols])
            ident = sb("ident", [P, P])
            ones = sb("ones", [P, P])
            hm16 = sb("hm16", [P, 8])
            hm32 = sb("hm32", [P, 4])
            vmask = sb("vmask", [P, 5, 3])
            eidx = sb("eidx", [P, 8])
            upper = sb("upper", [P, P])
            ps = held.enter_context(nc.psum_tensor("ps", [P, 8, 512], F32))
            mixture_sems = {top: [held.enter_context(nc.semaphore(f"{n}_top{top}"))
                                  for n in ("rows_sent", "rows_stored", *(f"rows_fetched{g}" for g in range(G)))]
                            for top in (1, 2)}

            @staticmethod
            def col(name):
                at = 0
                for n, width in COLUMNS:
                    if n == name:
                        return K.cols[:, at:at + width]
                    at += width
                raise KeyError(name)

        build_constants(nc, K, a["columns"], a["ctx_512"], a["x"])
        for n in layers:
            LAYERS[n](nc, K, a)
        with stage(nc, "stored") as (block, stored):
            @block.sync
            def _(sp):
                sp.dma_start(out.rearrange("b (t p) d -> p (b t) d", p=P), K.x[:, :, :]).then_inc(stored, 16)
                sp.wait_ge(stored, 16)



def rotary_tables():
    f = np.float32
    half = np.arange(0, LD, 2, dtype=f)
    inv_freq = f(1.0) / f(10000.0) ** (half / f(LD))
    t = np.arange(SEQ, dtype=f)
    freqs = t[:, None] * inv_freq[None, :]
    base = (half + f(0.4 * LD)) / f(1.4 * LD)
    scale = base[None, :] ** ((t - f(SEQ // 2)) / f(P // 2))[:, None]
    cos, sin = np.cos(freqs), np.sin(freqs)
    qc, qs, kc, ks = cos * scale * f(8), sin * scale * f(8), cos / scale, sin / scale
    both = lambda q, kk, sign: np.stack([np.concatenate([sign * q, q], 1), np.concatenate([sign * kk, kk], 1)], 1)
    turn = lambda v: np.ascontiguousarray(v.reshape(TB, P, 2, LD).transpose(1, 0, 2, 3), dtype=f)
    return turn(both(qc, kc, f(1))), turn(both(qs, ks, f(-1)))


def lay_out(inputs):
    a = {n: np.ascontiguousarray(v) for n, v in inputs.items()}
    wkv = a.pop("L2_xattn_Wkv")
    a["L2_xattn_Wk"] = np.ascontiguousarray(wkv[:D].T)
    a["L2_xattn_Wv"] = np.ascontiguousarray(wkv[D:].T)
    for n in ("L2_xattn_Wq", "L2_xattn_Wo"):
        a[n] = np.ascontiguousarray(a[n].T)
    for n in ("a1_wq", "a1_wk", "a1_wv", "a2_wq", "a2_wk", "a2_wv"):
        w = a["L1_xattn_" + n]
        a["L1_xattn_" + n] = np.ascontiguousarray(w.transpose(1, 0, 2).reshape(w.shape[1], -1))
    a["rotary_cos"], a["rotary_sin"] = rotary_tables()
    for n in ("L0_ffn_gate_up_proj", "L0_ffn_gate_up_proj_bias"):
        a[n] = np.ascontiguousarray(np.concatenate([a[n][..., 0::2], a[n][..., 1::2]], axis=-1))
    of = dict(a)
    for layer in range(2):
        for n in ("ln_g", "ln_b"):
            of[f"L2_ffn_{layer}_{n}"] = a[f"L2_ffn_{n}"][layer]
        b1 = a["L2_ffn_b1"][layer].reshape(2, -1)
        of[f"L2_ffn_{layer}_b1"] = np.pad(b1, ((0, 0), (0, -b1.shape[1] % P)))
    vectors = []
    for name, n in COLUMNS:
        v = of[name].reshape(-1)
        vectors.append(v.reshape(n, P).T)
    a["columns"] = np.ascontiguousarray(np.concatenate(vectors, axis=1))
    return a


def kernel(**inputs):
    import concourse.bacc as _bacc
    from concourse.bass_utils import run_bass_kernel_spmd as _run

    arrays = lay_out(inputs)
    nc = _bacc.Bacc("TRN2", target_bir_lowering=False, num_devices=1)
    named = {f"in_{n}": v for n, v in arrays.items()}
    aps = {n: nc.dram_tensor(f"in_{n}", v.shape, mybir.dt.from_np(v.dtype), kind="ExternalInput").ap()
           for n, v in arrays.items()}
    out = nc.dram_tensor("out", (BATCH, SEQ, D), F32, kind="ExternalOutput").ap()
    build(nc, aps, out)
    r = _run(nc, [named], core_ids=[0])
    return r.results[0]["out"]
```

```python
from contextlib import ExitStack, contextmanager

import numpy as np
import concourse.bass as bass
from concourse import mybir

F32 = mybir.dt.float32
F32R = mybir.dt.float32r
BF16 = mybir.dt.bfloat16
I32 = mybir.dt.int32
U32 = mybir.dt.uint32
ALU = mybir.AluOpType
ACT = mybir.ActivationFunctionType
AX = mybir.AxisListType

P = 128
BATCH = 2
SEQ = 1024
TOK = BATCH * SEQ
T = TOK // P
TB = SEQ // P
D = 256
KD = D // P
CTX = 77
CP = 80
IMG = 128
GT = 4
G = T // GT
GN = GT * P
EPS = 1e-5
HIGH_PART = -4096
NEG = -1e30


START = 8


def after(n):
    return n + START


def slot_free(j, count, ring):
    return j - ring + 1 if j >= ring else max(m for m in range(count) if m % ring == j) - count + 1


@contextmanager
def stage(nc, *names):
    with ExitStack() as held:
        sems = [held.enter_context(nc.semaphore(n)) for n in names]
        if sems:
            with nc.Block() as opening:
                @opening.sync
                def _(sp):
                    for s in sems:
                        sp.sem_clear(s)
                        sp.sem_inc(s, START)
        with nc.Block() as block:
            yield (block, *sems)


def tiles(nc, held):
    def make(name, shape, dt=F32):
        return held.enter_context(nc.sbuf_tensor(f"{name}_{nc.next_id()}", shape, dt))
    return make


class Chain:

    def __init__(self, eng, sem, base=0):
        self.eng, self.sem, self.base, self.n = eng, sem, base, 0

    def __call__(self, ins):
        self.n += 1
        ins.then_inc(self.sem, 1)
        self.eng.wait_ge(self.sem, after(self.base + self.n))



def build_constants(nc, k, cols_dram, ctx_dram, x_dram):
    with stage(nc, "x_loaded", "vectors_loaded", "ctx_loaded", "pool_step", "ctx_turned", "ctx_copied", "ones_set") as (
            block, x_loaded, vectors_loaded, ctx_loaded, pool_step, ctx_turned, ctx_copied, ones_set):
        @block.sync
        def _(sp):
            sp.dma_start(k.x[:, :, :], x_dram.rearrange("b (t p) d -> p (b t) d", p=P)).then_inc(x_loaded, 16)
            sp.dma_start(k.ctx[0:CTX, :, :], ctx_dram.rearrange("b s d -> s b d")).then_inc(ctx_loaded, 16)
            sp.dma_start(k.cols[:, :], cols_dram).then_inc(vectors_loaded, 16)
            sp.wait_ge(x_loaded, after(16))
            sp.wait_ge(vectors_loaded, after(16))

        @block.gpsimd
        def _(pool):
            step = Chain(pool, pool_step)
            step(pool.memset(k.ident[:, :], 0.0))
            step(pool.affine_select(out=k.ident[:, :], in_=k.ident[:, :], compare_op=ALU.not_equal, fill=1.0,
                                    base=0, pattern=[[-1, P]], channel_multiplier=1))
            step(pool.memset(k.upper[:, :], 1.0))
            step(pool.affine_select(out=k.upper[:, :], in_=k.upper[:, :], compare_op=ALU.is_gt, fill=0.0,
                                    base=0, pattern=[[1, P]], channel_multiplier=-1))
            for mask, d in ((k.hm16, 16), (k.hm32, 32)):
                n = P // d
                step(pool.memset(mask[:, :], 1.0))
                step(pool.affine_select(out=mask[:, :], in_=mask[:, :], compare_op=ALU.is_ge, fill=0.0,
                                        base=0, pattern=[[-d, n]], channel_multiplier=1))
                step(pool.affine_select(out=mask[:, :], in_=mask[:, :], compare_op=ALU.is_ge, fill=0.0,
                                        base=d - 1, pattern=[[d, n]], channel_multiplier=-1))
            for j in range(5):
                h0 = heads_of_block(j)[0]
                vm = k.vmask[:, j, :]
                step(pool.memset(vm, 1.0))
                step(pool.affine_select(out=vm, in_=vm, compare_op=ALU.is_ge, fill=0.0, base=P * j - CP * h0,
                                        pattern=[[-CP, 3]], channel_multiplier=1))
                step(pool.affine_select(out=vm, in_=vm, compare_op=ALU.is_ge, fill=0.0, base=CP * h0 + CP - 1 - P * j,
                                        pattern=[[CP, 3]], channel_multiplier=-1))
            step(pool.iota(k.eidx[:, :], pattern=[[1, 8]], base=0, channel_multiplier=0,
                           allow_small_or_imprecise_dtypes=True))

        @block.tensor
        def _(pe):
            pe.wait_ge(ctx_loaded, after(16))
            pe.wait_ge(pool_step, after(2))
            for b in range(BATCH):
                pe.transpose(k.ps[:, b, 0:CTX], k.ctx[0:CTX, b, :], k.ident[0:CTX, 0:CTX]).then_inc(ctx_turned, 1)

        @block.vector
        def _(dve):
            dve.memset(k.ones[:, :], 1.0).then_inc(ones_set, 1)
            for b in range(BATCH):
                dve.wait_ge(ctx_turned, after(b + 1))
                dve.tensor_copy(k.ctxT[:, b, :], k.ps[:, b, 0:CTX]).then_inc(ctx_copied, 1)



NEWTON = 3
NORM_STEPS = 6 + 3 * NEWTON
ROOT_SEED = 0x5F3759DF


def mean_of(norm, t):
    return norm[:, 6, bass.ds(t, 1)]


def rstd_of(norm, t):
    return norm[:, 7, bass.ds(t, 1)]


def row_norms(dve, step, src, norm, first, n):
    tmp = norm[:, :, first:first + n]
    stats = tmp[:, 0:6, :]
    mean, rstd, var, dif, nw = (tmp[:, 6 + j, :] for j in range(5))
    before = step.n
    for u in range(n):
        ins = dve.bn_stats(stats[:, :, u], src[:, first + u, :])
    step(ins)
    dve.tensor_tensor(mean, stats[:, 1, :], stats[:, 4, :], ALU.add)
    dve.tensor_tensor(dif, stats[:, 1, :], stats[:, 4, :], ALU.subtract)
    step(dve.tensor_tensor(var, stats[:, 2, :], stats[:, 5, :], ALU.add))
    dve.tensor_scalar(mean, mean, 0.5, None, ALU.mult)
    dve.tensor_tensor(dif, dif, dif, ALU.mult)
    step(dve.tensor_scalar(var, var, 1.0 / src.shape[2], EPS, ALU.mult, ALU.add))
    step(dve.scalar_tensor_tensor(out=var, in0=dif, scalar=0.25, in1=var, op0=ALU.mult, op1=ALU.add))
    step(dve.tensor_scalar(nw.bitcast(I32), var.bitcast(I32), 1, None, ALU.logical_shift_right))
    step(dve.tensor_scalar(rstd.bitcast(I32), nw.bitcast(I32), -1.0, float(ROOT_SEED), ALU.mult, ALU.add))
    for _ in range(NEWTON):
        step(dve.scalar_tensor_tensor(out=nw, in0=rstd, scalar=-0.5, in1=var, op0=ALU.mult, op1=ALU.mult))
        step(dve.tensor_tensor(nw, nw, rstd, ALU.mult))
        step(dve.scalar_tensor_tensor(out=rstd, in0=nw, scalar=1.5, in1=rstd, op0=ALU.add, op1=ALU.mult))
    assert step.n - before == NORM_STEPS



def normalise_group(dve, g, xn, src, norm, turned, normed):
    for u in range(GT):
        if u == 0:
            dve.wait_ge(turned, after(g * GT))
        t = g * GT + u
        if norm is None:
            dve.tensor_copy(xn[:, u, :], src[:, t, :]).then_inc(normed, 1)
        else:
            dve.tensor_scalar(xn[:, u, :], src[:, t, :], mean_of(norm, t), rstd_of(norm, t),
                              ALU.subtract, ALU.mult).then_inc(normed, 1)


def first_group(dve, norm_step, xn, src, norm, turned, normed, meanwhile=None):
    step = Chain(dve, norm_step)
    row_norms(dve, step, src, norm, 0, GT)
    normalise_group(dve, 0, xn, src, norm, turned, normed)
    if meanwhile is not None:
        meanwhile()
    row_norms(dve, step, src, norm, GT, T - GT)


def each_group(eng, body):
    with eng.Fori(0, G - 1) as g:
        body(g, False)
    body(G - 1, True)


def turn_group(pe, g, k, xn, psT, normed, turned, copied, copies):
    for u in range(GT):
        if u == 0:
            pe.wait_ge(copied, after(g * 2 * copies))
        pe.wait_ge(normed, after(g * GT + (u + 1)))
        for c in range(KD):
            m = pe.transpose(psT[:, u // 2, (u % 2 * KD + c) * P:(u % 2 * KD + c + 1) * P],
                             xn[:, u, c * P:(c + 1) * P], k.ident[:, :])
        m.then_inc(turned, 1)


def copy_group(act, g, xT, psT, gains, turned, copied, xT_read, reads):
    for q in range(2):
        if q == 0:
            act.wait_ge(xT_read, after(g * reads))
        act.wait_ge(turned, after(g * GT + (2 * q + 2)))
        turned_pair = psT[:, q, :].rearrange("p (u c n) -> p c u n", c=KD, n=P)
        for dst, gain in zip(xT, gains):
            out = dst[:, :, q * 2 * P:(q + 1) * 2 * P].rearrange("p c (u n) -> p c u n", n=P)
            if gain is None:
                act.activation(out, turned_pair, ACT.Copy).then_inc(copied, 1)
            else:
                for c in range(KD):
                    m = act.activation(out[:, c], turned_pair[:, c], ACT.Identity,
                                       scale=gain[0][:, c:c + 1], bias=gain[1][:, c:c + 1])
                m.then_inc(copied, 1)



def low_part(eng, low, whole, high):
    return eng.tensor_tensor(low, whole, high.bitcast(F32), ALU.subtract)


def product(pe, out, left, right, start, stop):
    (lh, ll), (rh, rl) = left, right
    pe.matmul(out, lh, rh, start=start, stop=False)
    pe.matmul(out, lh, rl, start=False, stop=False)
    return pe.matmul(out, ll, rh, start=False, stop=stop)



def ffn(nc, k, src, acc, w1, w2, gain, b1, b2row, glu=False):
    F = w2.shape[0]
    blocks = [(f, min(P, F - f)) for f in range(0, F, P)]
    NB = len(blocks)
    full = F // P
    rest = F - full * P
    RING = 4
    with ExitStack() as held:
        sb = tiles(nc, held)
        w1s, w1h, w1l = (sb(n, [P, KD, w1.shape[1]], t) for n, t in (("w1s", F32), ("w1h", F32R), ("w1l", F32R)))
        w2s, w2h, w2l = (sb(n, [P, NB, D], t) for n, t in (("w2s", F32), ("w2h", F32R), ("w2l", F32R)))
        b2s = sb("b2s", [P, D])
        xn = sb("xn", [P, GT, D])
        xT = sb("xT", [P, KD, GN])
        xh, xl = sb("xh", [P, KD, GN], F32R), sb("xl", [P, KD, GN], F32R)
        hw = sb("hw", [P, RING, GN])
        hh, hl = sb("hh", [P, NB, GN], F32R), sb("hl", [P, NB, GN], F32R)
        gl = sb("gl", [P, 2, GN]) if glu else None
        norm = sb("norm", [P, 11, T])
        psT = k.ps[:, 0:2, :]
        NH = 4 if glu else 3
        psH = [k.ps[:, 2 + j, :] for j in range(NH)]
        psY = [k.ps[:, 6 + j, 0:D] for j in range(2)]
        w2_places = [(slice(0, P), slice(0, full))] + ([(slice(0, rest), slice(full, NB))] if rest else [])
        NW = 1 + len(w2_places)
        with stage(nc, "w1_loaded", "w2_loaded", "w_high", "w1_split", "w2_split", "normed", "turned", "copied", "x_high", "x_split",
                   "h_ready", "h_done", "h_high", "h_split", "gate_done", "y_ready", "y_added", "norm_step",
                   "bias_added") as (
                block, w1_loaded, w2_loaded, w_high, w1_split, w2_split, normed, turned, copied, x_high, x_split,
                h_ready, h_done, h_high, h_split, gate_done, y_ready, y_added, norm_step, bias_added):
            @block.sync
            def _(sp):
                sp.dma_start(w1s[:, :, :], w1.rearrange("(c p) f -> p c f", p=P)).then_inc(w1_loaded, 16)
                sp.dma_start(w2s[:, 0:full, :],
                             w2[0:full * P, :].rearrange("(c p) f -> p c f", p=P)).then_inc(w2_loaded, 16)
                if rest:
                    sp.dma_start(w2s[0:rest, full, :], w2[full * P:F, :]).then_inc(w2_loaded, 16)
                sp.dma_start(b2s[:, :], b2row.to_broadcast([P, D])).then_inc(w2_loaded, 16)
            w2_all = 16 * NW

            @block.tensor
            def _(pe):
                def first_layer(out, j, f, m, at):
                    for c in range(KD):
                        mm = product(pe, out[0:m, :], (w1h[:, c, at:at + m], w1l[:, c, at:at + m]),
                                     (xh[:, c, :], xl[:, c, :]), start=(c == 0), stop=(c == KD - 1))
                    mm.then_inc(h_ready, 1)

                def hidden(g):
                    pe.wait_ge(x_split, after(g + 1))
                    for j, (f, m) in enumerate(blocks):
                        if not glu:
                            pe.wait_ge(h_done, after(g * NB + slot_free(j, NB, NH)))
                            first_layer(psH[j % NH], j, f, m, f)
                        else:
                            pe.wait_ge(h_done, after(g * NB + (j - 1)))
                            first_layer(psH[2 * (j % 2) + 1], j, f, m, F + f)
                            first_layer(psH[2 * (j % 2)], j, f, m, f)

                def output(g):
                    pe.wait_ge(w2_split, after(NW - 1))
                    pe.wait_ge(h_split, after((g + 1) * NB))
                    for u in range(GT):
                        pe.wait_ge(y_added, after(g * GT + (u - 1)))
                        for j, (f, m) in enumerate(blocks):
                            at = slice(u * P, (u + 1) * P)
                            mm = product(pe, psY[u % 2], (hh[0:m, j, at], hl[0:m, j, at]),
                                         (w2h[0:m, j, :], w2l[0:m, j, :]), start=(j == 0), stop=(j == NB - 1))
                        mm.then_inc(y_ready, 1)

                def body(g, last):
                    hidden(g)
                    if not last:
                        turn_group(pe, g + 1, k, xn, psT, normed, turned, copied, 1)
                    output(g)

                turn_group(pe, 0, k, xn, psT, normed, turned, copied, 1)
                pe.wait_ge(w1_split, after(1))
                each_group(pe, body)

            @block.scalar
            def _(act):
                hidden = 2 * NB if glu else NB

                def body(g, last):
                    for j, (f, m) in enumerate(blocks):
                        if not glu:
                            act.wait_ge(h_ready, after(g * NB + (j + 1)))
                            act.wait_ge(h_split, after(g * NB + (j - RING + 1)))
                            act.activation(hw[0:m, j % RING, :], psH[j % NH][0:m, :], ACT.Gelu,
                                           bias=b1[0:m, j:j + 1]).then_inc(h_done, 1)
                        else:
                            act.wait_ge(h_ready, after(g * 2 * NB + (2 * j + 1)))
                            act.wait_ge(h_done, after(g * NB + (j - 1)))
                            act.activation(gl[0:m, j % 2, :], psH[2 * (j % 2) + 1][0:m, :], ACT.Gelu,
                                           bias=b1[0:m, NB + j:NB + j + 1]).then_inc(gate_done, 1)
                    if not last:
                        copy_group(act, g + 1, [xT], psT, [gain], turned, copied, h_ready, hidden)

                act.wait_ge(w1_loaded, after(16))
                act.activation(w1h[:, :, :], w1s[:, :, :], ACT.Copy).then_inc(w_high, 1)
                copy_group(act, 0, [xT], psT, [gain], turned, copied, h_ready, hidden)
                act.wait_ge(w2_loaded, after(w2_all))
                for p, c in w2_places:
                    act.activation(w2h[p, c, :], w2s[p, c, :], ACT.Copy).then_inc(w_high, 1)
                each_group(act, body)

            @block.vector
            def _(dve):
                def split_x(g):
                    dve.wait_ge(copied, after((g + 1) * 2))
                    dve.tensor_copy(xh[:, :, :], xT[:, :, :]).then_inc(x_high, 1)
                    dve.wait_ge(x_high, after(g + 1))
                    low_part(dve, xl[:, :, :], xT[:, :, :], xh[:, :, :]).then_inc(x_split, 1)

                def split_h(g, j, m):
                    dve.wait_ge(h_done, after(g * NB + (j + 1)))
                    dve.tensor_copy(hh[0:m, j, :], hw[0:m, j % RING, :]).then_inc(h_high, 1)
                    dve.wait_ge(h_high, after(g * NB + (j + 1)))
                    low_part(dve, hl[0:m, j, :], hw[0:m, j % RING, :], hh[0:m, j, :]).then_inc(h_split, 1)

                def body(g, last):
                    if not last:
                        normalise_group(dve, g + 1, xn, src, norm, turned, normed)
                    dve.wait_ge(y_ready, after(g * GT))
                    for j, (f, m) in enumerate(blocks):
                        if glu:
                            dve.wait_ge(h_ready, after(g * 2 * NB + (2 * j + 2)))
                            dve.wait_ge(gate_done, after(g * NB + (j + 1)))
                            dve.wait_ge(h_split, after(g * NB + j))
                            dve.scalar_tensor_tensor(out=hw[0:m, j % RING, :], in0=psH[2 * (j % 2)][0:m, :],
                                                     scalar=b1[0:m, j:j + 1], in1=gl[0:m, j % 2, :],
                                                     op0=ALU.add, op1=ALU.mult).then_inc(h_done, 1)
                        split_h(g, j, m)
                    if not last:
                        split_x(g + 1)
                    for u in range(GT):
                        t = g * GT + u
                        dve.wait_ge(bias_added, after(T))
                        dve.wait_ge(y_ready, after(g * GT + (u + 1)))
                        dve.tensor_tensor(acc[:, t, :], psY[u % 2], acc[:, t, :], ALU.add).then_inc(y_added, 1)

                def split_w1():
                    dve.wait_ge(w_high, after(1))
                    low_part(dve, w1l[:, :, :], w1s[:, :, :], w1h[:, :, :]).then_inc(w1_split, 1)
                    split_x(0)

                first_group(dve, norm_step, xn, src, norm, turned, normed, split_w1)
                each_group(dve, body)

            @block.gpsimd
            def _(pool):
                for n, (p, c) in enumerate(w2_places):
                    pool.wait_ge(w_high, after(n + 2))
                    low_part(pool, w2l[p, c, :], w2s[p, c, :], w2h[p, c, :]).then_inc(w2_split, 1)
                with pool.Fori(0, T) as t:
                    if acc is src:
                        pool.wait_ge(normed, after(t + 1))
                    pool.tensor_tensor(acc[:, t, :], acc[:, t, :], b2s[:, :], ALU.add).then_inc(bias_added, 1)



def project(nc, k, src, gains, turned_jobs, row_jobs, loads):
    with ExitStack() as held:
        sb = tiles(nc, held)
        xn = sb("xn", [P, GT, D])
        norm = sb("norm", [P, 11, T])
        xT = [sb(f"xT{j}", [P, KD, GN]) for j in range(len(gains))]
        psT = k.ps[:, 0:2, :]
        NC = len(gains)
        blocks = [(w, a, dst, bias, scale, f) for w, a, dst, bias, scale in turned_jobs
                  for f in range(w.shape[2] // P)]
        rows = [(w, a, dst, u, f) for w, a, dst in row_jobs for u in range(GT) for f in range(w.shape[2] // 512)]
        NF, NR = len(blocks), len(rows)
        RING = 3
        with stage(nc, "w_loaded", "normed", "turned", "copied", "feat_ready", "feat_out", "row_ready", "row_out",
                   "norm_step") as (
                block, w_loaded, normed, turned, copied, feat_ready, feat_out, row_ready, row_out, norm_step):
            @block.sync
            def _(sp):
                for dst, weights in loads:
                    sp.dma_start(dst, weights).then_inc(w_loaded, 16)

            @block.tensor
            def _(pe):
                def body(g, last):
                    pe.wait_ge(copied, after((g + 1) * 2 * NC))
                    for j, (w, a, dst, bias, scale, f) in enumerate(blocks):
                        pe.wait_ge(feat_out, after(g * NF + slot_free(j, NF, RING)))
                        for c in range(KD):
                            mm = pe.matmul(k.ps[:, 2 + j % RING, :], w[:, c, f * P:(f + 1) * P], xT[a][:, c, :],
                                           start=(c == 0), stop=(c == KD - 1))
                        mm.then_inc(feat_ready, 1)
                    for j, (w, a, dst, u, f) in enumerate(rows):
                        pe.wait_ge(row_out, after(g * NR + slot_free(j, NR, RING)))
                        for c in range(KD):
                            mm = pe.matmul(k.ps[:, 5 + j % RING, :], xT[a][:, c, u * P:(u + 1) * P],
                                           w[:, c, f * 512:(f + 1) * 512], start=(c == 0), stop=(c == KD - 1))
                        mm.then_inc(row_ready, 1)
                    if not last:
                        turn_group(pe, g + 1, k, xn, psT, normed, turned, copied, NC)

                turn_group(pe, 0, k, xn, psT, normed, turned, copied, NC)
                pe.wait_ge(w_loaded, after(16 * len(loads)))
                each_group(pe, body)

            @block.scalar
            def _(act):
                last_read, n = (row_ready, NR) if NR else (feat_ready, NF)

                def body(g, last):
                    for j, (w, a, dst, u, f) in enumerate(rows):
                        act.wait_ge(row_ready, after(g * NR + (j + 1)))
                        act.activation(dst[:, 4 * f:4 * f + 4, bass.ds(g * GT + u, 1), :].rearrange("p a t n -> p (a t) n"),
                                       k.ps[:, 5 + j % RING, :].rearrange("p (a n) -> p a n", a=4),
                                       ACT.Copy).then_inc(row_out, 1)
                    if not last:
                        copy_group(act, g + 1, xT, psT, gains, turned, copied, last_read, n)

                copy_group(act, 0, xT, psT, gains, turned, copied, last_read, n)
                each_group(act, body)

            @block.vector
            def _(dve):
                def body(g, last):
                    if not last:
                        normalise_group(dve, g + 1, xn, src, norm, turned, normed)
                    for j, (w, a, dst, bias, scale, f) in enumerate(blocks):
                        dve.wait_ge(feat_ready, after(g * NF + (j + 1)))
                        dve.tensor_scalar(dst[:, f, bass.ds(g * GN, GN)], k.ps[:, 2 + j % RING, :],
                                          0.0 if bias is None else bias[:, f:f + 1], scale,
                                          ALU.add, ALU.mult).then_inc(feat_out, 1)

                first_group(dve, norm_step, xn, src, norm, turned, normed)
                each_group(dve, body)


def each_pair(eng, before, body):
    n = TB // 2
    for b in range(BATCH):
        if before is not None:
            before(b, b * n)
        with eng.Fori(0, n - 1) as j:
            body(b, b * n + j, False)
        body(b, b * n + n - 1, True)



def heads_of_block(j):
    return P * j // CP, (P * j + P - 1) // CP


def cross_attention(nc, k, d, srcT, QT, O, wk, wv, bk, bvrow, scale):
    NQ = 16 * d // P
    HB = P // d
    hm = k.hm16 if d == 16 else k.hm32
    W = d + 1
    with ExitStack() as held:
        sb = tiles(nc, held)
        Kbd = sb("Kbd", [P, BATCH, 16, CTX])
        Vfirst = sb("Vfirst", [P, BATCH, 2, 8 * W])
        Vbd = sb("Vbd", [P, BATCH, 10, 3 * W])
        with ExitStack() as prep:
            sb2 = tiles(nc, prep)
            wks = sb2("wks", [P, 16 * d])
            wvs = sb2("wvs", [P, 16 * d])
            bvs = sb2("bvs", [1, 16 * d])
            rep = sb2("rep", [P, BATCH, 8, CP])
            with stage(nc, "wk_loaded", "wv_loaded", "zeroed", "rep_made", "k_ready", "k_out", "v_ready", "v_out") as (
                    block, wk_loaded, wv_loaded, zeroed, rep_made, k_ready, k_out, v_ready, v_out):
                @block.sync
                def _(sp):
                    sp.dma_start(wks[:, :], wk).then_inc(wk_loaded, 16)
                    sp.dma_start(wvs[:, :], wv).then_inc(wv_loaded, 16)
                    if bvrow is not None:
                        sp.dma_start(bvs[:, :], bvrow).then_inc(wv_loaded, 16)

                @block.gpsimd
                def _(pool):
                    pool.memset(rep[:, :, :, :], 0.0).then_inc(zeroed, 1)
                    pool.memset(Vfirst[:, :, :, :], 0.0).then_inc(zeroed, 1)
                    pool.wait_ge(zeroed, after(1))
                    for b in range(BATCH):
                        pool.tensor_copy(rep[:, b, :, 0:CTX],
                                         srcT[:, b, :].unsqueeze(1).to_broadcast([P, 8, CTX])).then_inc(rep_made, 1)

                @block.tensor
                def _(pe):
                    pe.wait_ge(wk_loaded, after(16))
                    n = 0
                    for b in range(BATCH):
                        for q in range(NQ):
                            if n >= 4:
                                pe.wait_ge(k_out, after(n - 3))
                            pe.matmul(k.ps[:, n % 4, 0:CTX], wks[:, q * P:(q + 1) * P], srcT[:, b, :],
                                      start=True, stop=True).then_inc(k_ready, 1)
                            n += 1
                    pe.wait_ge(wv_loaded, after(32 if bvrow is not None else 16))
                    pe.wait_ge(rep_made, after(BATCH))
                    n = 0
                    for b in range(BATCH):
                        flat = rep[:, b, :, :].rearrange("p h c -> p (h c)")
                        for j in range(10):
                            h0, h1 = heads_of_block(j)
                            cols = slice(h0 * d, (h1 + 1) * d)
                            if n >= 4:
                                pe.wait_ge(v_out, after(n - 3))
                            out = k.ps[:, 4 + n % 4, 0:(h1 - h0 + 1) * d]
                            mm = pe.matmul(out, flat[:, j % 5 * P:(j % 5 + 1) * P], wvs[:, cols],
                                           start=True, stop=(bvrow is None))
                            if bvrow is not None:
                                mm = pe.matmul(out, k.ones[0:1, 0:P], bvs[:, cols], start=False, stop=True)
                            mm.then_inc(v_ready, 1)
                            n += 1

                @block.vector
                def _(dve):
                    n = 0
                    for b in range(BATCH):
                        for q in range(NQ):
                            dve.wait_ge(k_ready, after(n + 1))
                            for h in range(HB):
                                m = dve.tensor_scalar(Kbd[:, b, q * HB + h, :], k.ps[:, n % 4, 0:CTX],
                                                      0.0 if bk is None else bk[:, q:q + 1], hm[:, h:h + 1],
                                                      ALU.add, ALU.mult)
                            m.then_inc(k_out, 1)
                            n += 1
                    dve.wait_ge(zeroed, after(2))
                    n = 0
                    for b in range(BATCH):
                        for j in range(10):
                            h0, h1 = heads_of_block(j)
                            nh = h1 - h0 + 1
                            dst = Vfirst[:, b, j // 5, 0:nh * W] if j % 5 == 0 else Vbd[:, b, j, 0:nh * W]
                            dst = dst.rearrange("p (h w) -> p h w", w=W)
                            dve.wait_ge(v_ready, after(n + 1))
                            mask = k.vmask[:, j % 5, 0:nh].unsqueeze(2)
                            dve.tensor_copy(dst[:, :, d:W], mask)
                            dve.tensor_tensor(dst[:, :, 0:d],
                                              k.ps[:, 4 + n % 4, 0:nh * d].rearrange("p (h w) -> p h w", w=d),
                                              mask.to_broadcast([P, nh, d]), ALU.mult).then_inc(v_out, 1)
                            n += 1

        qs = sb("qs", [P, 2, NQ, P])
        neg = sb("neg", [P, 2, 8])
        sd = sb("sd", [P, 2, 8, CTX])
        pr = sb("pr", [P, 2, 8, CP])
        pT = sb("pT", [P, 2, 5, P])
        rsum = sb("rsum", [P, 2, 8])
        score_view = lambda c: k.ps[:, 2 * (c % 2):2 * (c % 2) + 2, 0:4 * CTX].rearrange("p b (h n) -> p b h n", n=CTX)
        psPT = k.ps[:, 4:6, :]
        IT = 4
        with stage(nc, "pads_zeroed", "q_staged", "s_ready", "shifted", "exp_done", "pt_ready", "pt_copied",
                   "o_ready", "o_done", "max_done", "inverse_done") as (
                block, pads_zeroed, q_staged, s_ready, shifted, exp_done, pt_ready, pt_copied, o_ready, o_done,
                max_done, inverse_done):
            @block.gpsimd
            def _(pool):
                pool.memset(pr[:, :, :, :], 0.0).then_inc(pads_zeroed, 1)
                with pool.Fori(0, T // 2) as i:
                    for u in range(2):
                        pool.wait_ge(s_ready, after(i * IT + (2 * u - 2)))
                        pool.tensor_copy(qs[:, u, :, :], QT[:, :, bass.ds((2 * i + u) * P, P)]).then_inc(q_staged, 1)

            @block.tensor
            def _(pe):
                def scores(b, it, c):
                    u, half = c // 2 % 2, c % 2
                    pe.wait_ge(q_staged, after(it * 2 + (c // 2 + 1)))
                    pe.wait_ge(shifted, after(it * IT + (c - 1)))
                    for j in range(2):
                        h = 8 * half + 4 * j
                        mm = pe.matmul(k.ps[:, 2 * (c % 2) + j, 0:4 * CTX], qs[:, u, h // HB, :],
                                       Kbd[:, b, h:h + 4, :].rearrange("p h n -> p (h n)"), start=True, stop=True)
                    mm.then_inc(s_ready, 1)

                def turn(it, c):
                    pe.wait_ge(exp_done, after(it * IT + (c + 1)))
                    pe.wait_ge(pt_copied, after(it * IT + c))
                    flat = pr[:, c % 2, :, :].rearrange("p h n -> p (h n)")
                    for j in range(5):
                        mm = pe.transpose(psPT[:, j // 4, j % 4 * P:(j % 4 + 1) * P], flat[:, j * P:(j + 1) * P],
                                          k.ident[:, :])
                    mm.then_inc(pt_ready, 1)

                def values(b, it, c):
                    half = c % 2
                    pe.wait_ge(pt_copied, after(it * IT + (c + 1)))
                    pe.wait_ge(o_done, after(it * IT + (c - 1)))
                    for j in range(5):
                        h0, h1 = heads_of_block(5 * half + j)
                        if j == 0:
                            out, v = k.ps[:, 6 + c % 2, 0:8 * W], Vfirst[:, b, half, :]
                        else:
                            out = k.ps[:, 6 + c % 2, (h0 - 8 * half) * W:(h1 + 1 - 8 * half) * W]
                            v = Vbd[:, b, 5 * half + j, 0:(h1 - h0 + 1) * W]
                        mm = pe.matmul(out, pT[:, c % 2, j, :], v,
                                       start=(j == 0), stop=(j == 4))
                    mm.then_inc(o_ready, 1)

                def before(b, it):
                    scores(b, it, 0)
                    scores(b, it, 1)

                def body(b, it, last):
                    for c in range(IT):
                        if c + 2 < IT or not last:
                            scores(b, it, c + 2)
                        turn(it, c)
                        if c:
                            values(b, it, c - 1)
                    values(b, it, IT - 1)

                each_pair(pe, before, body)

            @block.scalar
            def _(act):
                def probs(it, c):
                    act.wait_ge(shifted, after(it * IT + (c + 1)))
                    act.wait_ge(pt_ready, after(it * IT + (c - 1)))
                    act.activation(pr[:, c % 2, :, 0:CTX], sd[:, c % 2, :, :], ACT.Exp,
                                   scale=scale).then_inc(exp_done, 1)

                def copy_pt(it, c):
                    act.wait_ge(pt_ready, after(it * IT + (c + 1)))
                    act.wait_ge(o_ready, after(it * IT + (c - 1)))
                    act.activation(pT[:, c % 2, :, :].rearrange("p a n -> p (a n)"),
                                   psPT.rearrange("p a n -> p (a n)")[:, 0:5 * P], ACT.Copy).then_inc(pt_copied, 1)

                def body(b, it, last):
                    for c in range(IT):
                        if c + 1 < IT or not last:
                            probs(it, c + 1)
                        copy_pt(it, c)

                act.wait_ge(pads_zeroed, after(1))
                each_pair(act, lambda b, it: probs(it, 0), body)

            @block.vector
            def _(dve):
                def shift(it, c):
                    dve.wait_ge(s_ready, after(it * IT + (c + 1)))
                    dve.wait_ge(exp_done, after(it * IT + (c - 1)))
                    m = neg[:, c % 2, :].rearrange("p (b h) -> p b h", b=2)
                    dve.tensor_reduce(m, score_view(c), AX.X, ALU.max).then_inc(max_done, 1)
                    dve.wait_ge(max_done, after(it * IT + (c + 1)))
                    dve.tensor_tensor(sd[:, c % 2, :, :].rearrange("p (b h) n -> p b h n", b=2), score_view(c),
                                      m.unsqueeze(3).to_broadcast([P, 2, 4, CTX]), ALU.subtract).then_inc(shifted, 1)

                def normal(it, c):
                    u, half = c // 2, c % 2
                    dve.wait_ge(o_ready, after(it * IT + (c + 1)))
                    o = k.ps[:, 6 + c % 2, 0:8 * W].rearrange("p (h w) -> p h w", w=W)
                    dve.reciprocal(rsum[:, c % 2, :], o[:, :, d]).then_inc(inverse_done, 1)
                    dve.wait_ge(inverse_done, after(it * IT + (c + 1)))
                    dve.tensor_tensor(
                        O[:, half * NQ // 2:(half + 1) * NQ // 2, bass.ds(2 * it + u, 1), :].rearrange(
                            "p a t (h w) -> p (a t) h w", w=d),
                        o[:, :, 0:d].rearrange("p (a h) w -> p a h w", h=HB),
                        rsum[:, c % 2, :].rearrange("p (a h) -> p a h", h=HB).unsqueeze(3).to_broadcast(
                            [P, NQ // 2, HB, d]), ALU.mult).then_inc(o_done, 1)

                def before(b, it):
                    shift(it, 0)
                    shift(it, 1)

                def body(b, it, last):
                    for c in range(IT):
                        if c + 2 < IT or not last:
                            shift(it, c + 2)
                        if c:
                            normal(it, c - 1)
                    normal(it, IT - 1)

                each_pair(dve, before, body)



def out_project(nc, k, O, w, brow, add_to, also=None):
    NB = w.shape[0] // P
    with ExitStack() as held:
        sb = tiles(nc, held)
        ws = sb("ws", [P, NB, D])
        bs = sb("bs", [1, D])
        ot = sb("ot", [P, 2, NB * P])
        OT = sb("OT", [P, 2, NB * P])
        with stage(nc, "w_loaded", "o_staged", "turned", "copied", "y_ready", "y_added", "summed") as (
                block, w_loaded, o_staged, turned, copied, y_ready, y_added, summed):
            @block.sync
            def _(sp):
                sp.dma_start(ws[:, :, :], w.rearrange("(c p) f -> p c f", p=P)).then_inc(w_loaded, 16)
                if brow is not None:
                    sp.dma_start(bs[:, :], brow).then_inc(w_loaded, 16)

            @block.gpsimd
            def _(pool):
                with pool.Fori(0, T // 2) as i:
                    pool.wait_ge(turned, after(2 * i))
                    for u in range(2):
                        pool.tensor_copy(ot[:, u, :].rearrange("p (a n) -> p a n", n=P),
                                         O[:, :, bass.ds(2 * i + u, 1), :].rearrange("p a t n -> p (a t) n")
                                         ).then_inc(o_staged, 1)

            @block.tensor
            def _(pe):
                pe.wait_ge(w_loaded, after(32 if brow is not None else 16))
                with pe.Fori(0, T // 2) as i:
                    for u in range(2):
                        pe.wait_ge(o_staged, after(2 * i + (u + 1)))
                        pe.wait_ge(copied, after(2 * i))
                        for c in range(NB):
                            mm = pe.transpose(k.ps[:, u, c * P:(c + 1) * P], ot[:, u, c * P:(c + 1) * P], k.ident[:, :])
                        mm.then_inc(turned, 1)
                    for u in range(2):
                        pe.wait_ge(copied, after(2 * i + (u + 1)))
                        pe.wait_ge(y_added, after(2 * i))
                        if brow is not None:
                            pe.matmul(k.ps[:, 2 + u, 0:D], k.ones[0:1, 0:P], bs[:, :], start=True, stop=False)
                        for c in range(NB):
                            mm = pe.matmul(k.ps[:, 2 + u, 0:D], OT[:, u, c * P:(c + 1) * P], ws[:, c, :],
                                           start=(c == 0 and brow is None), stop=(c == NB - 1))
                        mm.then_inc(y_ready, 1)

            @block.scalar
            def _(act):
                with act.Fori(0, T // 2) as i:
                    act.wait_ge(y_ready, after(2 * i))
                    for u in range(2):
                        act.wait_ge(turned, after(2 * i + (u + 1)))
                        act.activation(OT[:, u, :], k.ps[:, u, 0:NB * P], ACT.Copy).then_inc(copied, 1)

            @block.vector
            def _(dve):
                with dve.Fori(0, T // 2) as i:
                    for u in range(2):
                        t = 2 * i + u
                        dve.wait_ge(y_ready, after(2 * i + (u + 1)))
                        if also is None:
                            dve.tensor_tensor(add_to[:, t, :], k.ps[:, 2 + u, 0:D], add_to[:, t, :],
                                              ALU.add).then_inc(y_added, 1)
                        else:
                            dve.scalar_tensor_tensor(out=also[:, t, :], in0=add_to[:, t, :], scalar=2.0,
                                                     in1=k.ps[:, 2 + u, 0:D], op0=ALU.mult, op1=ALU.add).then_inc(summed, 1)
                            dve.wait_ge(summed, after(2 * i + (u + 1)))
                            dve.tensor_tensor(add_to[:, t, :], k.ps[:, 2 + u, 0:D], add_to[:, t, :],
                                              ALU.add).then_inc(y_added, 1)


def normalise_context(nc, k, gain, yT):
    with ExitStack() as held:
        sb = tiles(nc, held)
        norm = sb("norm", [P, 11, BATCH])
        cn = sb("cn", [P, BATCH, IMG])
        with stage(nc, "norm_step", "normed", "turned") as (block, norm_step, normed, turned):
            @block.vector
            def _(dve):
                row_norms(dve, Chain(dve, norm_step), k.ctx[0:CTX], norm[0:CTX], 0, BATCH)
                for b in range(BATCH):
                    dve.tensor_scalar(cn[0:CTX, b, :], k.ctx[0:CTX, b, :], mean_of(norm[0:CTX], b), rstd_of(norm[0:CTX], b),
                                      ALU.subtract, ALU.mult).then_inc(normed, 1)

            @block.tensor
            def _(pe):
                for b in range(BATCH):
                    pe.wait_ge(normed, after(b + 1))
                    pe.transpose(k.ps[:, b, 0:CTX], cn[0:CTX, b, :], k.ident[0:CTX, 0:CTX]).then_inc(turned, 1)

            @block.scalar
            def _(act):
                for b in range(BATCH):
                    act.wait_ge(turned, after(b + 1))
                    act.activation(yT[:, b, :], k.ps[:, b, 0:CTX], ACT.Identity, scale=gain[0], bias=gain[1])



def turned_weights(w):
    return w.rearrange("(c p) f -> p c f", p=P)


def row_of(v):
    return v.rearrange("(a n) -> a n", a=1)


def cross_layer(nc, k, d, src, add_to, also, wq, bq, wk, bk, wv, bvrow, wo, borow, gain, ctxT):
    W = 16 * d
    with ExitStack() as outer:
        O = tiles(nc, outer)("O", [P, W // P, T, P])
        with ExitStack() as held:
            sb = tiles(nc, held)
            QT = sb("QT", [P, W // P, TOK])
            with ExitStack() as front:
                wqs = tiles(nc, front)("wqs", [P, KD, W])
                project(nc, k, src, [gain], [(wqs, 0, QT, bq, 1.0)], [],
                        [(wqs[:, :, :], turned_weights(wq))])
            cross_attention(nc, k, d, ctxT, QT, O, wk, wv, bk, bvrow, float(d) ** -0.5)
        out_project(nc, k, O, wo, borow, add_to, also)


def layer0_attention(nc, k, a):
    cross_layer(nc, k, 16, k.x, k.x, None, a["L0_xattn_Wq"], k.col("L0_xattn_bq"), a["L0_xattn_Wk"],
                k.col("L0_xattn_bk"), a["L0_xattn_Wv"], row_of(a["L0_xattn_bv"]), a["L0_xattn_Wo"],
                row_of(a["L0_xattn_bo"]), None, k.ctxT)


def layer2_attention(nc, k, a):
    cross_layer(nc, k, 16, k.x, k.x, None, a["L2_xattn_Wq"], None, a["L2_xattn_Wk"],
                None, a["L2_xattn_Wv"], None, a["L2_xattn_Wo"], None, None, k.ctxT)



SH = 32
HG = P // SH


def self_attention(nc, k, QT, KT, V):
    QB = TB
    NB = BATCH * (16 // HG)
    QT = QT[:, :, :].rearrange("p a n -> p (a n)")
    KT = KT[:, :, :].rearrange("p a n -> p (a n)")
    V = V[:, :, :, :].rearrange("p a t n -> p (a t n)")
    UNITS = [(h, q) for h in range(HG) for q in range(QB)]
    NU = len(UNITS)
    HALF = QB // 2
    NW = HG * HALF
    wide_before = lambda n: n // QB * HALF + min(n % QB, HALF)
    LOAD = 16 * 8
    with ExitStack() as held:
        sb = tiles(nc, held)
        parts = sb("parts", [P, 4, SEQ])
        qst, kst = sb("qst", [P, 2, SEQ]), sb("kst", [P, 2, SEQ])
        pr = sb("pr", [P, 4, SEQ])
        pT = sb("pT", [P, 2, SEQ])
        neg = sb("neg", [P, 2])
        rs = sb("rs", [P, 4])
        inv = sb("inv", [P, 2])
        with stage(nc, "split_done", "even_stacked", "odd_stacked", "s_ready", "max_done", "exp_done", "masked",
                   "near_turned", "near_copied", "far_turned", "far_copied", "o_ready", "inverse_done", "o_done") as (
                block, split_done, even_stacked, odd_stacked, s_ready, max_done, exp_done, masked,
                near_turned, near_copied, far_turned, far_copied, o_ready, inverse_done, o_done):
            stacked = (even_stacked, odd_stacked)

            @block.sync
            def _(sp):
                def stack(it, h):
                    r = slice(SH * (h % HG), SH * (h % HG + 1))
                    for m, (qpart, kpart) in enumerate(((0, 2), (1, 2), (0, 3), (1, 3))):
                        to = slice(SH * m, SH * (m + 1))
                        sp.dma_start(qst[to, h % 2, :], parts[r, qpart, :]).then_inc(stacked[h % 2], 16)
                        sp.dma_start(kst[to, h % 2, :], parts[r, kpart, :]).then_inc(stacked[h % 2], 16)

                sp.wait_ge(split_done, after(4))
                stack(0, 0)
                stack(0, 1)
                with sp.Fori(0, NB - 1) as it:
                    for h in range(2, HG + 2):
                        sp.wait_ge(max_done, after(it * NU + QB * (h - 1)))
                        stack(it, h)
                for h in range(2, HG):
                    sp.wait_ge(s_ready, after((NB - 1) * NU + QB * (h - 1)))
                    stack(NB - 1, h)

            @block.gpsimd
            def _(pool):
                with pool.Fori(0, NB) as it:
                    for n, (h, q) in enumerate(UNITS):
                        pool.wait_ge(exp_done, after(it * NU + (n + 1)))
                        own = pr[:, n % 4, q * P:(q + 1) * P]
                        pool.tensor_tensor(own, own, k.upper[:, :], ALU.mult).then_inc(masked, 1)

            @block.tensor
            def _(pe):
                def scores(it, n):
                    h, q = UNITS[n % NU]
                    if q == 0:
                        pe.wait_ge(stacked[h % 2], after(LOAD * 2 * it + LOAD * (n // QB // 2 + 1)))
                    pe.wait_ge(exp_done, after(it * NU + (n - 1)))
                    for j in range(2):
                        mm = pe.matmul(k.ps[:, 2 * (n % 2) + j, :], qst[:, h % 2, q * P:(q + 1) * P].bitcast(F32R),
                                       kst[:, h % 2, j * 512:(j + 1) * 512].bitcast(F32R), start=True, stop=True)
                    mm.then_inc(s_ready, 1)

                def turn(it, n):
                    q = UNITS[n][1]
                    pe.wait_ge(masked, after(it * NU + (n + 1)))
                    pe.wait_ge(near_copied, after(it * NU + n))
                    for c in range(q, min(q + HALF, QB)):
                        mm = pe.transpose(k.ps[:, 4, (c - q) * P:(c - q + 1) * P], pr[:, n % 4, c * P:(c + 1) * P],
                                          k.ident[:, :])
                    mm.then_inc(near_turned, 1)
                    if q < HALF:
                        pe.wait_ge(far_copied, after(it * NW + wide_before(n)))
                        for c in range(q + HALF, QB):
                            mm = pe.transpose(k.ps[:, 5, (c - q - HALF) * P:(c - q - HALF + 1) * P],
                                              pr[:, n % 4, c * P:(c + 1) * P], k.ident[:, :])
                        mm.then_inc(far_turned, 1)

                def values(it, n):
                    h, q = UNITS[n]
                    pe.wait_ge(near_copied, after(it * NU + (n + 1)))
                    if q < HALF:
                        pe.wait_ge(far_copied, after(it * NW + wide_before(n + 1)))
                    pe.wait_ge(o_done, after(it * NU + (n - 1)))
                    for c in range(q, QB):
                        mm = pe.matmul(k.ps[:, 6 + n % 2, 0:SH], pT[:, n % 2, (c - q) * P:(c - q + 1) * P],
                                       V[:, bass.ds((it * QB + c) * P + h * SH, SH)], start=(c == q), stop=(c == QB - 1))
                    mm.then_inc(o_ready, 1)

                def units(it, last):
                    for n in range(NU):
                        if n + 2 < NU or not last:
                            scores(it, n + 2)
                        turn(it, n)
                        if n:
                            values(it, n - 1)
                    values(it, NU - 1)

                scores(0, 0)
                scores(0, 1)
                with pe.Fori(0, NB - 1) as it:
                    units(it, False)
                units(NB - 1, True)

            @block.scalar
            def _(act):
                def exps(it, n):
                    act.wait_ge(max_done, after(it * NU + (n + 1)))
                    act.wait_ge(o_done, after(it * NU + (n - 3)))
                    act.activation(pr[:, n % 4, :], k.ps[:, 2 * (n % 2):2 * (n % 2) + 2, :].rearrange("p a n -> p (a n)"),
                                   ACT.Exp, bias=neg[:, n % 2:n % 2 + 1],
                                   accum_out=rs[:, n % 4:n % 4 + 1]).then_inc(exp_done, 1)

                def copy_near(it, n):
                    near = min(HALF, QB - UNITS[n][1]) * P
                    act.wait_ge(o_ready, after(it * NU + (n - 1)))
                    act.wait_ge(near_turned, after(it * NU + (n + 1)))
                    act.activation(pT[:, n % 2, 0:near], k.ps[:, 4, 0:near], ACT.Copy).then_inc(near_copied, 1)

                def units(it, last):
                    for n in range(NU):
                        if n + 1 < NU or not last:
                            exps(it, n + 1)
                        copy_near(it, n)

                exps(0, 0)
                with act.Fori(0, NB - 1) as it:
                    units(it, False)
                units(NB - 1, True)

            @block.vector
            def _(dve):
                def split(it):
                    for j, src in ((0, QT), (2, KT)):
                        dve.tensor_scalar(parts[:, j, :].bitcast(I32), src[:, bass.ds(it * SEQ, SEQ)].bitcast(I32),
                                          HIGH_PART, None, ALU.bitwise_and).then_inc(split_done, 1)
                    dve.wait_ge(split_done, after(4 * it + 2))
                    for j, src in ((1, QT), (3, KT)):
                        dve.tensor_tensor(parts[:, j, :], src[:, bass.ds(it * SEQ, SEQ)], parts[:, j - 1, :],
                                          ALU.subtract).then_inc(split_done, 1)

                def maxima(it, n):
                    dve.wait_ge(s_ready, after(it * NU + (n + 1)))
                    dve.tensor_reduce(neg[:, n % 2:n % 2 + 1], k.ps[:, 2 * (n % 2):2 * (n % 2) + 2, :], AX.XY,
                                      ALU.max, negate=True).then_inc(max_done, 1)

                def copy_far(it, n):
                    near, far = HALF * P, (HALF - UNITS[n][1]) * P
                    dve.wait_ge(o_ready, after(it * NU + (n - 1)))
                    dve.wait_ge(far_turned, after(it * NW + wide_before(n + 1)))
                    dve.tensor_copy(pT[:, n % 2, near:near + far], k.ps[:, 5, 0:far]).then_inc(far_copied, 1)

                def normal(it, n):
                    h, q = UNITS[n]
                    dve.wait_ge(o_ready, after(it * NU + (n + 1)))
                    dve.reciprocal(inv[:, n % 2:n % 2 + 1], rs[:, n % 4:n % 4 + 1]).then_inc(inverse_done, 1)
                    dve.wait_ge(inverse_done, after(it * NU + (n + 1)))
                    dve.tensor_scalar(QT[:, bass.ds((it * QB + q) * P + h * SH, SH)], k.ps[:, 6 + n % 2, 0:SH],
                                      inv[:, n % 2:n % 2 + 1], None, ALU.mult).then_inc(o_done, 1)

                def units(it, last):
                    for n in range(NU):
                        if n == NU - QB - HALF and not last:
                            for s in stacked:
                                dve.wait_ge(s, after(LOAD * 2 * it + LOAD * 2))
                            split(it + 1)
                        if n + 2 < NU or not last:
                            maxima(it, n + 2)
                        if UNITS[n][1] < HALF:
                            copy_far(it, n)
                        if n:
                            normal(it, n - 1)
                    normal(it, NU - 1)

                split(0)
                maxima(0, 0)
                maxima(0, 1)
                with dve.Fori(0, NB - 1) as it:
                    units(it, False)
                units(NB - 1, True)


def layer1_attention(nc, k, a):
    with ExitStack() as held:
        sb = tiles(nc, held)
        y = sb("y_rows", [P, T, D])
        base = sb("base_rows", [P, T, D])
        layer_norm_rows(nc, k, k.x, y, None)
        layer_norm_rows(nc, k, y, y, ("L1_xattn_ln1_g", "L1_xattn_ln1_b"), a)
        A = "L1_xattn_a1_"
        with ExitStack() as outer:
            QT = tiles(nc, outer)("QT", [P, 4, TOK])
            with ExitStack() as inner:
                sb2 = tiles(nc, inner)
                KT, V = sb2("KT", [P, 4, TOK]), sb2("V", [P, 4, T, P])
                with ExitStack() as front:
                    sb3 = tiles(nc, front)
                    ws = [sb3(f"w{n}", [P, KD, 512]) for n in "qkv"]
                    project(nc, k, y,
                            [(k.col(A + "lnx_g"), k.col(A + "lnx_b")), (k.col(A + "lny_g"), k.col(A + "lny_b"))],
                            [(ws[0], 0, QT, None, float(SH) ** -0.5), (ws[1], 1, KT, None, 1.0)], [(ws[2], 1, V)],
                            [(w[:, :, :], turned_weights(a[A + n])) for w, n in zip(ws, ("wq", "wk", "wv"))])
                self_attention(nc, k, QT, KT, V)
            O = QT[:, :, :].rearrange("p a (t n) -> p a t n", n=P)
            out_project(nc, k, O, a[A + "li1_w"], row_of(a[A + "li1_b"]), y, base)
        ffn(nc, k, y, base, a[A + "li2_w"], a[A + "li3_w"], (k.col(A + "ln3_g"), k.col(A + "ln3_b")),
            k.col(A + "li2_b"), row_of(a[A + "li3_b"]))
        layer_norm_rows(nc, k, base, y, ("L1_xattn_ln2_g", "L1_xattn_ln2_b"), a)
        A = "L1_xattn_a2_"
        yT = sb("yT", [P, BATCH, CTX])
        normalise_context(nc, k, (k.col(A + "lny_g"), k.col(A + "lny_b")), yT)
        cross_layer(nc, k, 32, y, y, base, a[A + "wq"], None, a[A + "wk"], None, a[A + "wv"], None,
                    a[A + "li1_w"], row_of(a[A + "li1_b"]), (k.col(A + "lnx_g"), k.col(A + "lnx_b")), yT)
        ffn(nc, k, y, base, a[A + "li2_w"], a[A + "li3_w"], (k.col(A + "ln3_g"), k.col(A + "ln3_b")),
            k.col(A + "li2_b"), row_of(a[A + "li3_b"]))
        add_rows(nc, k, base)


def add_rows(nc, k, rows):
    with stage(nc) as (block,):
        @block.vector
        def _(dve):
            dve.tensor_tensor(k.x[:, :, :], k.x[:, :, :], rows[:, :, :], ALU.add)


def layer_norm_rows(nc, k, src, dst, gain, a=None, keep=None):
    with ExitStack() as held:
        sb = tiles(nc, held)
        norm = sb("norm", [P, 11, T])
        gb = sb("gb", [P, 2, D])
        part = sb("part", [P, GT, D])
        with stage(nc, "gain_loaded", "norm_step", "scaled", "src_kept") as (
                block, gain_loaded, norm_step, scaled, src_kept):
            @block.sync
            def _(sp):
                if keep is not None:
                    sp.dma_start(keep, src[:, :, :].rearrange("p t d -> p (t d)")).then_inc(src_kept, 16)
                    sp.wait_ge(src_kept, after(16))
                if gain is not None:
                    for j, n in enumerate(gain):
                        sp.dma_start(gb[:, j, :], row_of(a[n]).to_broadcast([P, D])).then_inc(gain_loaded, 16)
                    sp.wait_ge(gain_loaded, after(32))

            @block.vector
            def _(dve):
                step = Chain(dve, norm_step)
                row_norms(dve, step, src, norm, 0, T)
                if gain is not None:
                    dve.wait_ge(gain_loaded, after(32))
                for g in range(G):
                    for u in range(GT):
                        t = g * GT + u
                        if gain is None:
                            dve.tensor_scalar(dst[:, t, :], src[:, t, :], mean_of(norm, t), rstd_of(norm, t),
                                              ALU.subtract, ALU.mult)
                        else:
                            ins = dve.scalar_tensor_tensor(out=part[:, u, :], in0=src[:, t, :], scalar=mean_of(norm, t),
                                                           in1=gb[:, 0, :], op0=ALU.subtract, op1=ALU.mult)
                    if gain is not None:
                        ins.then_inc(scaled, 1)
                        dve.wait_ge(scaled, after(g + 1))
                        for u in range(GT):
                            t = g * GT + u
                            ins = dve.scalar_tensor_tensor(out=dst[:, t, :], in0=part[:, u, :], scalar=rstd_of(norm, t),
                                                           in1=gb[:, 1, :], op0=ALU.mult, op1=ALU.add)
                        step(ins)



def layer3_attention(nc, k, a):
    with ExitStack() as held:
        sb = tiles(nc, held)
        QT = sb("QT", [P, KD, TOK])
        KT = sb("KT", [P, KD, BATCH, CTX])
        V = sb("V", [P, BATCH, D])
        with ExitStack() as front:
            sb2 = tiles(nc, front)
            wqs, wks, wvs, bvs = sb2("wqs", [P, KD, D]), sb2("wks", [P, D]), sb2("wvs", [P, D]), sb2("bvs", [1, D])
            project(nc, k, k.x, [None], [(wqs, 0, QT, k.col("L3_xattn_bq"), 1.0)], [],
                    [(wqs[:, :, :], turned_weights(a["L3_xattn_Wq"]))])
            with stage(nc, "wk_loaded", "wv_loaded", "k_ready", "v_ready") as (
                    block, wk_loaded, wv_loaded, k_ready, v_ready):
                @block.sync
                def _(sp):
                    sp.dma_start(wks[:, :], a["L3_xattn_Wk"]).then_inc(wk_loaded, 16)
                    sp.dma_start(wvs[:, :], a["L3_xattn_Wv"]).then_inc(wv_loaded, 16)
                    sp.dma_start(bvs[:, :], row_of(a["L3_xattn_bv"])).then_inc(wv_loaded, 16)

                @block.tensor
                def _(pe):
                    pe.wait_ge(wk_loaded, after(16))
                    for b in range(BATCH):
                        for c in range(KD):
                            pe.matmul(k.ps[:, KD * b + c, 0:CTX], wks[:, c * P:(c + 1) * P], k.ctxT[:, b, :],
                                      start=True, stop=True).then_inc(k_ready, 1)
                    pe.wait_ge(wv_loaded, after(32))
                    for b in range(BATCH):
                        pe.matmul(k.ps[0:CTX, 4 + b, 0:D], k.ctxT[:, b, :], wvs[:, :], start=True, stop=False)
                        pe.matmul(k.ps[0:CTX, 4 + b, 0:D], k.ones[0:1, 0:CTX], bvs[:, :], start=False,
                                  stop=True).then_inc(v_ready, 1)

                @block.vector
                def _(dve):
                    bk = k.col("L3_xattn_bk")
                    for b in range(BATCH):
                        for c in range(KD):
                            dve.wait_ge(k_ready, after(KD * b + c + 1))
                            dve.tensor_scalar(KT[:, c, b, :], k.ps[:, KD * b + c, 0:CTX], bk[:, c:c + 1], None, ALU.add)
                    for b in range(BATCH):
                        dve.wait_ge(v_ready, after(b + 1))
                        dve.tensor_copy(V[0:CTX, b, :], k.ps[0:CTX, 4 + b, 0:D])

        qs = sb("qs", [P, 2, KD, P])
        pr = sb("pr", [P, 2, CTX])
        pT = sb("pT", [P, 2, P])
        neg, rs, inv = sb("neg", [P, 2]), sb("rs", [P, 2]), sb("inv", [P, 2])
        with stage(nc, "q_staged", "s_ready", "max_done", "exp_done", "pt_ready", "pt_copied", "o_ready",
                   "inverse_done", "o_done") as (
                block, q_staged, s_ready, max_done, exp_done, pt_ready, pt_copied, o_ready, inverse_done, o_done):
            @block.gpsimd
            def _(pool):
                with pool.Fori(0, T // 2) as i:
                    pool.wait_ge(s_ready, after(2 * i))
                    for u in range(2):
                        pool.tensor_copy(qs[:, u, :, :], QT[:, :, bass.ds((2 * i + u) * P, P)]).then_inc(q_staged, 1)

            @block.tensor
            def _(pe):
                with pe.Fori(0, BATCH) as b:
                    with pe.Fori(0, TB // 2) as j:
                        i = b * (TB // 2) + j
                        for u in range(2):
                            pe.wait_ge(q_staged, after(2 * i + (u + 1)))
                            pe.wait_ge(exp_done, after(2 * i))
                            for c in range(KD):
                                mm = pe.matmul(k.ps[:, u, 0:CTX], qs[:, u, c, :], KT[:, c, bass.ds(b, 1), :].rearrange(
                                    "p a n -> p (a n)"), start=(c == 0), stop=(c == KD - 1))
                            mm.then_inc(s_ready, 1)
                        for u in range(2):
                            pe.wait_ge(exp_done, after(2 * i + (u + 1)))
                            pe.wait_ge(pt_copied, after(2 * i))
                            pe.transpose(k.ps[0:CTX, 2 + u, 0:P], pr[:, u, :], k.ident[:, :]).then_inc(pt_ready, 1)
                        for u in range(2):
                            pe.wait_ge(pt_copied, after(2 * i + (u + 1)))
                            pe.wait_ge(o_done, after(2 * i))
                            pe.matmul(k.ps[:, 4 + u, 0:D], pT[0:CTX, u, :], V[0:CTX, bass.ds(b, 1), :].rearrange(
                                "p a n -> p (a n)"), start=True, stop=True).then_inc(o_ready, 1)

            @block.scalar
            def _(act):
                with act.Fori(0, T // 2) as i:
                    for u in range(2):
                        act.wait_ge(max_done, after(2 * i + (u + 1)))
                        act.wait_ge(o_done, after(2 * i))
                        act.activation(pr[:, u, :], k.ps[:, u, 0:CTX], ACT.Exp, bias=neg[:, u:u + 1],
                                       accum_out=rs[:, u:u + 1]).then_inc(exp_done, 1)
                    for u in range(2):
                        act.wait_ge(pt_ready, after(2 * i + (u + 1)))
                        act.activation(pT[0:CTX, u, :], k.ps[0:CTX, 2 + u, 0:P], ACT.Copy).then_inc(pt_copied, 1)

            @block.vector
            def _(dve):
                with dve.Fori(0, T // 2) as i:
                    for u in range(2):
                        dve.wait_ge(s_ready, after(2 * i + (u + 1)))
                        dve.tensor_reduce(neg[:, u:u + 1], k.ps[:, u, 0:CTX], AX.X, ALU.max,
                                          negate=True).then_inc(max_done, 1)
                    for u in range(2):
                        dve.wait_ge(o_ready, after(2 * i + (u + 1)))
                        dve.reciprocal(inv[:, u:u + 1], rs[:, u:u + 1]).then_inc(inverse_done, 1)
                        dve.wait_ge(inverse_done, after(2 * i + (u + 1)))
                        row = k.x[:, 2 * i + u, :]
                        dve.scalar_tensor_tensor(out=row, in0=k.ps[:, 4 + u, 0:D], scalar=inv[:, u:u + 1], in1=row,
                                                 op0=ALU.mult, op1=ALU.add).then_inc(o_done, 1)



LH = 8
LD = 64
LW = LH * LD


def shift_rows(nc, k, x, h):
    H = D // 2
    with stage(nc, "zeroed", "moved", "copied") as (block, zeroed, moved, copied):
        @block.vector
        def _(dve):
            for b in range(BATCH):
                dve.memset(h[0:1, b * TB, H:D], 0.0).then_inc(zeroed, 1)
            dve.tensor_copy(h[:, :, 0:H], x[:, :, 0:H]).then_inc(copied, 1)

        @block.sync
        def _(sp):
            sp.dma_start(h[1:P, :, H:D], x[0:P - 1, :, H:D]).then_inc(moved, 16)
            for b in range(BATCH):
                sp.dma_start(h[0:1, b * TB + 1:(b + 1) * TB, H:D],
                             x[P - 1:P, b * TB:(b + 1) * TB - 1, H:D]).then_inc(moved, 16)
            sp.wait_ge(moved, after(16 * (1 + BATCH)))


def local_qkv(nc, k, a, layer, h, ws, bb, ab, QT, KT, V):
    with ExitStack() as held:
        sb = tiles(nc, held)
        cosT = sb("cosT", [P, TB, 2, LD])
        sinT = sb("sinT", [P, TB, 2, LD])
        qks = sb("qks", [P, 2, LD])
        qkw = sb("qkw", [P, 2, LD])
        with stage(nc, "tables_loaded", "scaled") as (block, tables_loaded, scaled):
            @block.sync
            def _(sp):
                sp.dma_start(cosT[:, :, :, :], a["rotary_cos"]).then_inc(tables_loaded, 16)
                sp.dma_start(sinT[:, :, :, :], a["rotary_sin"]).then_inc(tables_loaded, 16)
                for j, n in enumerate(("L2_ffn_q_scale", "L2_ffn_k_scale")):
                    v = a[n][layer:layer + 1, :]
                    sp.dma_start(qks[:, j, :], v.to_broadcast([P, LD])).then_inc(tables_loaded, 16)
                    for m in range(2):
                        sp.dma_start(qkw[:, j, m * LD // 2:(m + 1) * LD // 2],
                                     v[:, (1 - m) * LD // 2:(2 - m) * LD // 2].to_broadcast([P, LD // 2])
                                     ).then_inc(tables_loaded, 16)
                sp.wait_ge(tables_loaded, after(16 * 8))

            @block.vector
            def _(dve):
                dve.wait_ge(tables_loaded, after(16 * 8))
                for tab, sc in ((cosT, qks), (sinT, qkw)):
                    dve.tensor_tensor(tab[:, :, :, :], tab[:, :, :, :],
                                      sc[:, :, :].unsqueeze(1).to_broadcast([P, TB, 2, LD]), ALU.mult)

        xn = sb("xn", [P, GT, D])
        xT = sb("xT", [P, KD, GN])
        sq = sb("sq", [P, 2 * LH, LD])
        qk = sb("qk", [P, 2, 2, LW])
        ss = sb("ss", [P, 2, 2 * LH])
        root = sb("root", [P, 2, 2 * LH])
        rn = sb("rn", [P, 2, 2 * LH])
        psT = k.ps[:, 0:2, :]
        CH = 6
        heads = lambda ap: ap.rearrange("p b (h w) -> p b h w", w=LD)
        with stage(nc, "w_loaded", "normed", "turned", "copied", "qk_ready", "qk_out", "v_ready", "v_out", "squared",
                   "products", "summed", "ss_ready", "root_ready", "chain", "rotated", "qkt_ready", "qkt_out") as (
                block, w_loaded, normed, turned, copied, qk_ready, qk_out, v_ready, v_out, squared,
                products, summed, ss_ready, root_ready, chain, rotated, qkt_ready, qkt_out):
            @block.sync
            def _(sp):
                sp.dma_start(ws[:, :, :], turned_weights(a["L2_ffn_wqkv"][layer])).then_inc(w_loaded, 16)

            def each_tile(eng, group, tile, lagging):
                def body(g, first):
                    group(g)
                    for u in range(GT):
                        tile(g, u)
                        if u >= 2 or not first:
                            lagging(g, u - 2)
                body(0, True)
                with eng.Fori(1, G) as g:
                    body(g, False)
                lagging(G - 1, GT - 2)
                lagging(G - 1, GT - 1)

            @block.tensor
            def _(pe):
                def group(g):
                    turn_group(pe, g, k, xn, psT, normed, turned, copied, 1)
                    pe.wait_ge(w_loaded, after(16))
                    pe.wait_ge(copied, after((g + 1) * 2))

                def tile(g, u):
                    pe.wait_ge(qk_out, after(g * GT + (u - 1)))
                    for j in range(3):
                        if j == 2:
                            pe.wait_ge(v_out, after(g * GT + u))
                        out = k.ps[:, 6, :] if j == 2 else k.ps[:, 2 + 2 * (u % 2) + j, :]
                        for c in range(KD):
                            mm = pe.matmul(out, xT[:, c, u * P:(u + 1) * P], ws[:, c, j * LW:(j + 1) * LW],
                                           start=(c == 0), stop=(c == KD - 1))
                        if j:
                            mm.then_inc(qk_ready if j == 1 else v_ready, 1)

                def turn_qk(g, u):
                    for j in range(2):
                        pe.wait_ge(rotated, after(g * GT + (u + 1)))
                        pe.wait_ge(qkt_out, after(g * 2 * GT + (2 * u + j)))
                        flat = ab[:, u % 4, :, :].rearrange("p h w -> p (h w)")
                        for c in range(4):
                            mm = pe.transpose(k.ps[:, 7, c * P:(c + 1) * P],
                                              flat[:, (4 * j + c) * P:(4 * j + c + 1) * P], k.ident[:, :])
                        mm.then_inc(qkt_ready, 1)

                each_tile(pe, group, tile, turn_qk)

            @block.scalar
            def _(act):
                def group(g):
                    copy_group(act, g, [xT], psT, [None], turned, copied, v_ready, GT)

                def roots(g, u):
                    act.wait_ge(ss_ready, after(g * GT + (u + 1)))
                    act.activation(root[:, u % 2, :], ss[:, u % 2, :], ACT.Sqrt).then_inc(root_ready, 1)

                def tile(g, u):
                    act.wait_ge(qk_ready, after(g * GT + (u + 1)))
                    act.wait_ge(products, after(g * GT + (u - 1)))
                    act.activation(qk[:, u % 2, :, :], k.ps[:, 2 + 2 * (u % 2):4 + 2 * (u % 2), :],
                                   ACT.Copy).then_inc(qk_out, 1)
                    act.wait_ge(qk_out, after(g * GT + (u + 1)))
                    act.wait_ge(ss_ready, after(g * GT + u))
                    act.activation(sq[:, :, :].rearrange("p h w -> p (h w)"),
                                   qk[:, u % 2, :, :].rearrange("p b n -> p (b n)"), ACT.Square).then_inc(squared, 1)
                    if u or not isinstance(g, int):
                        roots(g, u - 1)
                    act.wait_ge(v_ready, after(g * GT + (u + 1)))
                    act.activation(V[:, :, bass.ds(g * GT + u + 1, 1), :].rearrange("p a t n -> p (a t) n"),
                                   k.ps[:, 6, :].rearrange("p (a n) -> p a n", a=4), ACT.Copy).then_inc(v_out, 1)

                def copy_qk(g, u):
                    if isinstance(g, int) and (g, u) == (G - 1, GT - 2):
                        roots(G - 1, GT - 1)
                    for j, dst in enumerate((QT, KT)):
                        act.wait_ge(qkt_ready, after(g * 2 * GT + (2 * u + j + 1)))
                        at = (g * GT + u + 1) * P
                        act.activation(dst[:, :, bass.ds(at, P)], k.ps[:, 7, :].rearrange("p (c n) -> p c n", c=4),
                                       ACT.Copy).then_inc(qkt_out, 1)

                each_tile(act, group, tile, copy_qk)

            @block.vector
            def _(dve):
                H = LD // 2
                two = lambda ap: ap.rearrange("p (b h) w -> p b h w", b=2)

                def rotate(t):
                    i = t % TB
                    A, B = ab[:, t % 4, :, :], bb[:, :, :]
                    dve.wait_ge(qk_out, after(t + 1))
                    dve.wait_ge(qkt_ready, after(2 * (t - 3)))
                    dve.wait_ge(summed, after(t))
                    dve.tensor_tensor(two(A), heads(qk[:, t % 2, :, :]),
                                      cosT[:, i, :, :].unsqueeze(2).to_broadcast([P, 2, LH, LD]), ALU.mult)
                    for m in range(2):
                        ins = dve.tensor_tensor(
                            two(B)[:, :, :, m * H:(m + 1) * H], heads(qk[:, t % 2, :, :])[:, :, :, (1 - m) * H:(2 - m) * H],
                            sinT[:, i, :, m * H:(m + 1) * H].unsqueeze(2).to_broadcast([P, 2, LH, H]), ALU.mult)
                    ins.then_inc(products, 1)
                    dve.wait_ge(squared, after(t + 1))
                    dve.tensor_reduce(ss[:, t % 2, :], sq[:, :, :], AX.X, ALU.add).then_inc(ss_ready, 1)

                def scale(t):
                    A, s, m = ab[:, t % 4, :, :], ss[:, t % 2, :], root[:, t % 2, :]
                    dve.wait_ge(root_ready, after(t + 1))
                    step = Chain(dve, chain, t * CH)
                    r0, r1 = rn[:, 0, :], rn[:, 1, :]
                    step(dve.tensor_scalar(m, m, 1e-12, None, ALU.max))
                    step(dve.reciprocal(r0, m))
                    step(dve.tensor_tensor(r0, r0, s, ALU.mult))
                    step(dve.tensor_tensor(r0, r0, m, ALU.add))
                    step(dve.tensor_scalar(r0, r0, 0.5, 1e-12, ALU.mult, ALU.max))
                    step(dve.reciprocal(r1, r0))
                    assert step.n == CH
                    dve.wait_ge(summed, after(t + 1))
                    dve.tensor_tensor(A, A, r1.unsqueeze(2).to_broadcast([P, 2 * LH, LD]), ALU.mult).then_inc(rotated, 1)

                normalise_group(dve, 0, xn, h, None, turned, normed)
                for t in range(T):
                    rotate(t)
                    if t:
                        scale(t - 1)
                    if t % GT == 1 and t // GT + 1 < G:
                        normalise_group(dve, t // GT + 1, xn, h, None, turned, normed)
                scale(T - 1)

            @block.gpsimd
            def _(pool):
                with pool.Fori(0, G) as g:
                    for u in range(GT):
                        pool.wait_ge(products, after(g * GT + (u + 1)))
                        A, B = ab[:, u % 4, :, :], bb[:, :, :]
                        pool.tensor_tensor(A, A, B, ALU.add).then_inc(summed, 1)


def local_attention(nc, k, QT, KT, V, O):
    HB = P // LD
    with ExitStack() as held:
        sb = tiles(nc, held)
        mask = sb("mask", [P, 2, 2, 2 * P], BF16)
        ident16 = sb("ident16", [P, P], BF16)
        qz = sb("qz", [P, 2, 4, HB, P])
        pr = sb("pr", [P, 2, 4, 2 * P])
        pT = sb("pT", [P, 2, 8, P])
        neg, rs, inv = sb("neg", [P, 4, 4]), sb("rs", [P, 4, 4]), sb("inv", [P, 2, 4])
        with stage(nc, "pool_step") as (block, pool_step):
            @block.gpsimd
            def _(pool):
                step = Chain(pool, pool_step)
                step(pool.memset(mask[:, :, :, :], 0.0))
                for j in range(2):
                    m = mask[:, 0, j, 0:P]
                    step(pool.affine_select(out=m, in_=m, compare_op=ALU.is_ge, fill=NEG, base=0,
                                            pattern=[[1, P]], channel_multiplier=-1))
                    m = mask[:, :, j, P:2 * P]
                    step(pool.affine_select(out=m, in_=m, compare_op=ALU.is_ge, fill=NEG, base=0,
                                            pattern=[[0, 2], [-1, P]], channel_multiplier=1))
                    step(pool.memset(mask[:, 1, j, 0:P], NEG))
                step(pool.tensor_copy(ident16[:, :], k.ident[:, :]))
                pool.memset(qz[:, :, :, :, :], 0.0)
        N4 = 4
        with stage(nc, "q_staged", "s_ready", "max_done", "exp_done", "near_turned", "near_copied", "far_turned",
                   "far_copied", "o_ready", "inverse_done", "o_done") as (
                block, q_staged, s_ready, max_done, exp_done, near_turned, near_copied, far_turned,
                far_copied, o_ready, inverse_done, o_done):
            @block.gpsimd
            def _(pool):
                with pool.Fori(0, T // 2) as i:
                    for u in range(2):
                        pool.wait_ge(s_ready, after(i * N4 + (2 * u - 2)))
                        for e in range(HB):
                            r = slice(e * LD, (e + 1) * LD)
                            pool.tensor_copy(qz[r, u, :, e, :], QT[r, :, bass.ds((2 * i + u + 1) * P, P)]
                                             ).then_inc(q_staged, 1)
                            pool.wait_ge(q_staged, after(2 * HB * i + (HB * u + e + 1)))

            @block.tensor
            def _(pe):
                def scores(i, c, first=False):
                    u, half = c // 2 % 2, c % 2
                    pe.wait_ge(q_staged, after(2 * HB * i + HB * (c // 2 + 1)))
                    pe.wait_ge(exp_done, after(i * N4 + (c - 1)))
                    for m in range(2):
                        bank = k.ps[:, 2 * (c % 2) + m, :]
                        pe.matmul(bank, ident16[:, :], mask[:, int(first), :, :].rearrange("p b n -> p (b n)"),
                                  start=True, stop=False)
                        for e in range(HB):
                            blk = 2 * half + m
                            mm = pe.matmul(bank[:, e * 2 * P:(e + 1) * 2 * P], qz[:, u, blk, e, :],
                                           KT[:, blk, bass.ds((2 * i + c // 2) * P, 2 * P)], start=False, stop=(e == 1))
                    mm.then_inc(s_ready, 1)

                def turn(i, c):
                    pe.wait_ge(exp_done, after(i * N4 + (c + 1)))
                    flat = pr[:, c % 2, :, :].rearrange("p h n -> p (h n)")
                    for bank, out, turned in ((4, near_copied, near_turned), (5, far_copied, far_turned)):
                        pe.wait_ge(out, after(i * N4 + c))
                        for m in range(4):
                            at = ((bank - 4) * 4 + m) * P
                            mm = pe.transpose(k.ps[:, bank, m * P:(m + 1) * P], flat[:, at:at + P], k.ident[:, :])
                        mm.then_inc(turned, 1)

                def values(i, c):
                    u, half = c // 2, c % 2
                    pe.wait_ge(near_copied, after(i * N4 + (c + 1)))
                    pe.wait_ge(far_copied, after(i * N4 + (c + 1)))
                    pe.wait_ge(o_done, after(i * N4 + (c - 1)))
                    for hh in range(4):
                        h = 4 * half + hh
                        for w in range(2):
                            mm = pe.matmul(k.ps[:, 6 + c % 2, hh * LD:(hh + 1) * LD], pT[:, c % 2, 2 * hh + w, :],
                                           V[:, h // HB, bass.ds(2 * i + u + w, 1), h % HB * LD:(h % HB + 1) * LD].rearrange(
                                               "p t n -> p (t n)"), start=(w == 0), stop=(w == 1))
                    mm.then_inc(o_ready, 1)

                def before(b, i):
                    scores(i, 0, first=True)
                    scores(i, 1, first=True)

                def body(b, i, last):
                    for c in range(N4):
                        if c + 2 < N4 or not last:
                            scores(i, c + 2)
                        turn(i, c)
                        if c:
                            values(i, c - 1)
                    values(i, N4 - 1)

                each_pair(pe, before, body)

            @block.scalar
            def _(act):
                def exps(i, c):
                    act.wait_ge(max_done, after(i * N4 + (c + 1)))
                    act.wait_ge(far_turned, after(i * N4 + (c - 1)))
                    act.wait_ge(o_done, after(i * N4 + (c - 3)))
                    for hh in range(4):
                        ins = act.activation(pr[:, c % 2, hh, :], k.ps[:, 2 * (c % 2) + hh // 2,
                                                                     hh % 2 * 2 * P:(hh % 2 + 1) * 2 * P],
                                             ACT.Exp, bias=neg[:, c % 4, hh:hh + 1], accum_out=rs[:, c % 4, hh:hh + 1])
                    ins.then_inc(exp_done, 1)

                def copy_near(i, c):
                    act.wait_ge(near_turned, after(i * N4 + (c + 1)))
                    act.wait_ge(o_ready, after(i * N4 + (c - 1)))
                    act.activation(pT[:, c % 2, 0:4, :].rearrange("p a n -> p (a n)"), k.ps[:, 4, :],
                                   ACT.Copy).then_inc(near_copied, 1)

                def body(b, i, last):
                    for c in range(N4):
                        if c + 1 < N4 or not last:
                            exps(i, c + 1)
                        copy_near(i, c)

                each_pair(act, lambda b, i: exps(i, 0), body)

            @block.vector
            def _(dve):
                def maxima(i, c):
                    dve.wait_ge(s_ready, after(i * N4 + (c + 1)))
                    dve.tensor_reduce(neg[:, c % 4, :], k.ps[:, 2 * (c % 2):2 * (c % 2) + 2, :].rearrange(
                        "p b (h n) -> p (b h) n", h=2), AX.X, ALU.max, negate=True).then_inc(max_done, 1)

                def copy_far(i, c):
                    dve.wait_ge(far_turned, after(i * N4 + (c + 1)))
                    dve.wait_ge(o_ready, after(i * N4 + (c - 1)))
                    dve.tensor_copy(pT[:, c % 2, 4:8, :].rearrange("p a n -> p (a n)"), k.ps[:, 5, :]
                                    ).then_inc(far_copied, 1)

                def normal(i, c):
                    u, half = c // 2, c % 2
                    dve.wait_ge(o_ready, after(i * N4 + (c + 1)))
                    dve.reciprocal(inv[:, c % 2, :], rs[:, c, :]).then_inc(inverse_done, 1)
                    dve.wait_ge(inverse_done, after(i * N4 + (c + 1)))
                    dve.tensor_tensor(
                        O[:, 2 * half:2 * half + 2, bass.ds(2 * i + u, 1), :].rearrange(
                            "p a t (h w) -> p (a t) h w", w=LD),
                        k.ps[:, 6 + c % 2, 0:4 * LD].rearrange("p (a h w) -> p a h w", a=2, w=LD),
                        inv[:, c % 2, :].rearrange("p (a h) -> p a h", a=2).unsqueeze(3).to_broadcast([P, 2, 2, LD]),
                        ALU.mult).then_inc(o_done, 1)

                def before(b, i):
                    maxima(i, 0)
                    maxima(i, 1)

                def body(b, i, last):
                    for c in range(N4):
                        if c + 2 < N4 or not last:
                            maxima(i, c + 2)
                        copy_far(i, c)
                        if c:
                            normal(i, c - 1)
                    normal(i, N4 - 1)

                each_pair(dve, before, body)


def layer2_ffn(nc, k, a):
    with ExitStack() as held:
        y = tiles(nc, held)("y_rows", [P, T, D])
        kept = nc.dram_tensor("kept_x", (P, T * D), F32).ap()
        layer_norm_rows(nc, k, k.x, y, None, keep=kept)
        for layer in range(2):
            with ExitStack() as outer:
                O = tiles(nc, outer)("O", [P, 4, T, P])
                with ExitStack() as inner:
                    sb = tiles(nc, inner)
                    QT, KT = sb("QT", [P, 4, TOK + P]), sb("KT", [P, 4, TOK + P])
                    V = sb("V", [P, 4, T + 1, P])
                    flat = O[:, :, :, :].rearrange("p a t n -> p (a t n)")
                    h = flat[:, 0:T * D].rearrange("p (t d) -> p t d", d=D)
                    ws = flat[:, T * D:T * D + KD * 3 * LW].rearrange("p (c n) -> p c n", c=KD)
                    bb = flat[:, T * D + KD * 3 * LW:T * D + KD * 3 * LW + 2 * LW].rearrange("p (h w) -> p h w", w=LD)
                    ab = k.x[:, :, :].rearrange("p (j t) d -> p j (t d)", j=4).rearrange("p j (h w) -> p j h w", w=LD)
                    shift_rows(nc, k, y, h)
                    with stage(nc, "zeroed") as (block, zeroed):
                        @block.gpsimd
                        def _(pool):
                            pool.memset(KT[:, :, 0:P], 0.0)
                            pool.memset(V[:, :, 0, :], 0.0)
                    local_qkv(nc, k, a, layer, h, ws, bb, ab, QT, KT, V)
                    local_attention(nc, k, QT, KT, V, O)
                out_project(nc, k, O, a["L2_ffn_wo"][layer], None, y)
            with ExitStack() as inner:
                h = tiles(nc, inner)("h", [P, T, D])
                shift_rows(nc, k, y, h)
                C = f"L2_ffn_{layer}_"
                ffn(nc, k, h, y, a["L2_ffn_w1"][layer], a["L2_ffn_w2"][layer],
                    (k.col(C + "ln_g"), k.col(C + "ln_b")), k.col(C + "b1"), a["L2_ffn_b2"][layer:layer + 1, :], glu=True)
        with stage(nc, "x_back") as (block, x_back):
            @block.sync
            def _(sp):
                sp.dma_start(k.x[:, :, :].rearrange("p t d -> p (t d)"), kept).then_inc(x_back, 16)
                sp.wait_ge(x_back, after(16))
        add_rows(nc, k, y)



E = 8


def layer0_ffn(nc, k, a):
    NT = 4
    NF = 2
    with ExitStack() as held:
        sb = tiles(nc, held)
        norm = sb("norm", [P, 11, T])
        xn = sb("xn", [P, GT, D])
        xT = sb("xT", [P, KD, GN])
        bias_cols = k.col("L0_ffn_gate_up_proj_bias")
        gu = [sb(f"gu{e}", [P, KD, 4 * P]) for e in range(2)]
        dn = [sb(f"dn{e}", [P, NF, D]) for e in range(2)]
        gate, up, sig = (sb(n, [P, NF, GN]) for n in ("gate", "up", "sig"))
        inter = sb("inter", [P, 2, NF, GN])
        idx, idf = sb("idx", [P, NT, 2], I32), sb("idf", [P, NT, 2])
        rw = sb("rw", [P, NT, E])
        pick = sb("pick", [P, 2, NT, E])
        weight = sb("weight", [P, NT, E])
        weightT = sb("weightT", [E, NT, P])
        bd = sb("bd", [E, D])
        psT = k.ps[:, 0:2, :]
        with stage(nc, "loaded", "normed", "turned", "copied", "h_ready", "picked", "weights_turned",
                   "weights_copied", "y_ready", "norm_step") as (
                block, loaded, normed, turned, copied, h_ready, picked, weights_turned, weights_copied, y_ready,
                norm_step):
            @block.sync
            def _(sp):
                sp.dma_start(idx[:, :, :], a["L0_ffn_router_indices"].rearrange("(t p) k -> p t k", p=P)
                             ).then_inc(loaded, 16)
                sp.dma_start(rw[:, :, :], a["L0_ffn_routing_weights"].rearrange("(t p) e -> p t e", p=P)
                             ).then_inc(loaded, 16)
                sp.dma_start(bd[:, :], a["L0_ffn_down_proj_bias"]).then_inc(loaded, 16)
                sp.wait_ge(loaded, after(48))

            @block.vector
            def _(dve):
                row_norms(dve, Chain(dve, norm_step), k.x, norm, 0, NT)
                normalise_group(dve, 0, xn, k.x, norm, turned, normed)
                step = Chain(dve, picked)
                dve.wait_ge(loaded, after(48))
                step(dve.tensor_copy(idf[:, :, :], idx[:, :, :]))
                for j in range(2):
                    ins = dve.tensor_tensor(pick[:, j], idf[:, :, j:j + 1].to_broadcast([P, NT, E]),
                                            k.eidx[:, :].unsqueeze(1).to_broadcast([P, NT, E]), ALU.is_equal)
                    step(ins)
                step(dve.tensor_tensor(pick[:, 0], pick[:, 0], pick[:, 1], ALU.add))
                step(dve.tensor_tensor(weight[:, :, :], pick[:, 0], rw[:, :, :], ALU.mult))
                dve.wait_ge(weights_turned, after(1))
                dve.tensor_copy(weightT[:, :, :].rearrange("p t n -> p (t n)"), k.ps[0:E, 2, :]).then_inc(weights_copied, 1)
                for t in range(NT):
                    dve.wait_ge(y_ready, after(t + 1))
                    dve.tensor_tensor(k.x[:, t, :], k.x[:, t, :], k.ps[:, 3 + t, 0:D], ALU.add)

            @block.tensor
            def _(pe):
                turn_group(pe, 0, k, xn, psT, normed, turned, copied, 1)
                pe.wait_ge(picked, after(5))
                for t in range(NT):
                    mm = pe.transpose(k.ps[0:E, 2, t * P:(t + 1) * P], weight[:, t, :], k.ident[:, :])
                mm.then_inc(weights_turned, 1)
                pe.wait_ge(weights_copied, after(1))
                pe.wait_ge(loaded, after(48))
                for t in range(NT):
                    pe.matmul(k.ps[:, 3 + t, 0:D], weightT[:, t, :], bd[:, :], start=True, stop=True).then_inc(y_ready, 1)

            @block.scalar
            def _(act):
                copy_group(act, 0, [xT], psT, [None], turned, copied, h_ready, 1)

        with stage(nc, "first_loaded", "second_loaded", "h_ready", "h_read", "gate_ready", "up_ready", "sig_ready",
                   "prod_ready", "inter_done", "y_ready", "y_added") as (
                block, first_loaded, second_loaded, h_ready, h_read, gate_ready, up_ready, sig_ready,
                prod_ready, inter_done, y_ready, y_added):
            w_loaded = (first_loaded, second_loaded)

            @block.sync
            def _(sp):
                with sp.Fori(0, E // 2) as i:
                    for e in range(2):
                        sp.wait_ge(y_ready, after(2 * NT * i))
                        sp.dma_start(gu[e][:, :, :], a["L0_ffn_gate_up_proj"][bass.ds(2 * i + e, 1)].rearrange(
                            "e (c p) f -> p (e c) f", p=P)).then_inc(w_loaded[e], 16)
                        sp.dma_start(dn[e][:, :, :], a["L0_ffn_down_proj"][bass.ds(2 * i + e, 1)].rearrange(
                            "e (c p) f -> p (e c) f", p=P)).then_inc(w_loaded[e], 16)

            @block.tensor
            def _(pe):
                def hidden(i, e):
                    pe.wait_ge(w_loaded[e], after(32 * (i + 1)))
                    for f in range(NF):
                        pe.wait_ge(h_read, after(2 * NF * i + (NF * e + f - 1)))
                        for half in range(2):
                            for c in range(KD):
                                at = (NF * half + f) * P
                                mm = pe.matmul(k.ps[:, 2 * f + half, :], gu[e][:, c, at:at + P], xT[:, c, :],
                                               start=(c == 0), stop=(c == KD - 1))
                        mm.then_inc(h_ready, 1)

                def down(i, e):
                    pe.wait_ge(inter_done, after(2 * NF * i + NF * (e + 1)))
                    for t in range(NT):
                        pe.wait_ge(y_added, after(2 * NT * i + (NT * e + t - 3)))
                        for f in range(NF):
                            mm = pe.matmul(k.ps[:, 4 + t, 0:D], inter[:, e, f, t * P:(t + 1) * P], dn[e][:, f, :],
                                           start=(f == 0), stop=(f == NF - 1))
                        mm.then_inc(y_ready, 1)

                with pe.Fori(0, E // 2) as i:
                    hidden(i, 0)
                    hidden(i, 1)
                    down(i, 0)
                    down(i, 1)

            @block.vector
            def _(dve):
                def gates(i, e):
                    dve.wait_ge(inter_done, after(2 * NF * i + NF * e))
                    for f in range(NF):
                        n = 2 * NF * i + NF * e + f
                        col = lambda half: bias_cols[:, bass.ds((2 * i + e) * 4 + NF * half + f, 1)]
                        dve.wait_ge(h_ready, after(n + 1))
                        dve.tensor_scalar(gate[:, f, :], k.ps[:, 2 * f, :], col(0), 7.0, ALU.add,
                                          ALU.min).then_inc(gate_ready, 1)
                        dve.tensor_scalar(up[:, f, :], k.ps[:, 2 * f + 1, :], col(1), 7.0, ALU.add,
                                          ALU.min).then_inc(h_read, 1)
                        dve.wait_ge(h_read, after(n + 1))
                        dve.tensor_scalar(up[:, f, :], up[:, f, :], -7.0, 1.0, ALU.max, ALU.add).then_inc(up_ready, 1)
                    for f in range(NF):
                        n = 2 * NF * i + NF * e + f
                        dve.wait_ge(sig_ready, after(n + 1))
                        dve.wait_ge(prod_ready, after(n + 1))
                        dve.tensor_tensor(inter[:, e, f, :], up[:, f, :], sig[:, f, :], ALU.mult).then_inc(inter_done, 1)

                with dve.Fori(0, E // 2) as i:
                    gates(i, 0)
                    gates(i, 1)
                    for e in range(2):
                        for t in range(NT):
                            dve.wait_ge(y_ready, after(2 * NT * i + (NT * e + t + 1)))
                            row = k.x[:, t, :]
                            dve.scalar_tensor_tensor(out=row, in0=k.ps[:, 4 + t, 0:D],
                                                     scalar=weight[:, t, bass.ds(2 * i + e, 1)], in1=row,
                                                     op0=ALU.mult, op1=ALU.add).then_inc(y_added, 1)

            @block.gpsimd
            def _(pool):
                with pool.Fori(0, E // 2) as i:
                    for m in range(2 * NF):
                        pool.wait_ge(up_ready, after(2 * NF * i + (m + 1)))
                        u = up[:, m % NF, :]
                        pool.tensor_tensor(u, u, gate[:, m % NF, :], ALU.mult).then_inc(prod_ready, 1)

            @block.scalar
            def _(act):
                with act.Fori(0, E // 2) as i:
                    for m in range(2 * NF):
                        act.wait_ge(gate_ready, after(2 * NF * i + (m + 1)))
                        act.wait_ge(inter_done, after(2 * NF * i + (m - 1)))
                        act.activation(sig[:, m % NF, :], gate[:, m % NF, :], ACT.Sigmoid,
                                       scale=1.702).then_inc(sig_ready, 1)



def route(nc, k, rows, wg, cap, top, slots, gather_at, scatter_at, weights):
    with ExitStack() as held:
        sb = tiles(nc, held)
        wgs = sb("wgs", [P, KD, E])
        xn = sb("xn", [P, GT, D])
        xT = sb("xT", [P, KD, GN])
        psT = k.ps[:, 0:2, :]
        with stage(nc, "w_loaded", "normed", "turned", "copied", "logits_ready") as (
                block, w_loaded, normed, turned, copied, logits_ready):
            @block.sync
            def _(sp):
                sp.dma_start(wgs[:, :, :], turned_weights(wg)).then_inc(w_loaded, 16)

            @block.vector
            def _(dve):
                with dve.Fori(0, G) as g:
                    normalise_group(dve, g, xn, rows, None, turned, normed)

            @block.scalar
            def _(act):
                with act.Fori(0, G) as g:
                    copy_group(act, g, [xT], psT, [None], turned, copied, logits_ready, GT)

            @block.tensor
            def _(pe):
                pe.wait_ge(w_loaded, after(16))
                with pe.Fori(0, G) as g:
                    turn_group(pe, g, k, xn, psT, normed, turned, copied, 1)
                    pe.wait_ge(copied, after((g + 1) * 2))
                    for u in range(GT):
                        for c in range(KD):
                            mm = pe.matmul(k.ps[:, 2, bass.ds((g * GT + u) * E, E)], xT[:, c, u * P:(u + 1) * P],
                                           wgs[:, c, :], start=(c == 0), stop=(c == KD - 1))
                        mm.then_inc(logits_ready, 1)

        lg = sb("lg", [P, T, E])
        less = sb("less", [P, T, E])
        cand = sb("cand", [P, T, E])
        oh = sb("oh", [P, top, T, E])
        best, first = sb("best", [P, 2, T]), sb("first", [P, 2, T])
        e8 = sb("e8", [P, E])
        gate = sb("gate", [P, 2, T])
        dif, den = sb("dif", [P, T]), sb("den", [P, T])
        total = sb("total", [P, E])
        all_total = sb("all_total", [P, T, E])
        spare = sb("spare", [P, top, T])
        rank, keep, slot = (sb(n, [P, T]) for n in ("rank", "keep", "slot"))
        wide = lambda v: v.unsqueeze(2).to_broadcast([P, T, E])
        experts = lambda v: v.unsqueeze(1).to_broadcast([P, T, E])
        flat = lambda v: v.rearrange("p t e -> p (t e)")
        with stage(nc, "dve_step", "exp_asked", "exp_done", "chosen", "ranked", "spare_made") as (
                block, dve_step, exp_asked, exp_done, chosen, ranked, spare_made):
            @block.gpsimd
            def _(pool):
                pool.iota(spare[:, :, :], pattern=[[TOK, top], [P, T]], base=slots, channel_multiplier=1,
                          allow_small_or_imprecise_dtypes=True).then_inc(spare_made, 1)

            @block.vector
            def _(dve):
                step = Chain(dve, dve_step)

                def first_best(values, j):
                    step(dve.tensor_reduce(best[:, j, :], values, AX.X, ALU.max))
                    step(dve.tensor_tensor(cand[:, :, :], values, wide(best[:, j, :]), ALU.is_equal))
                    step(dve.tensor_tensor(cand[:, :, :], cand[:, :, :], experts(e8[:, :]), ALU.mult))
                    step(dve.tensor_reduce(first[:, j, :], cand[:, :, :], AX.X, ALU.min))
                    step(dve.tensor_tensor(oh[:, j], experts(e8[:, :]), wide(first[:, j, :]), ALU.is_equal))

                step(dve.tensor_scalar(e8[:, :], k.eidx[:, :], -8.0, None, ALU.add))
                step(dve.tensor_copy(flat(lg[:, :, :]), k.ps[:, 2, 0:T * E]))
                if top == 2:
                    first_best(lg[:, :, :], 0)
                    step(dve.scalar_tensor_tensor(out=less[:, :, :], in0=oh[:, 0], scalar=NEG, in1=lg[:, :, :],
                                                  op0=ALU.mult, op1=ALU.add))
                    first_best(less[:, :, :], 1)
                    dve.tensor_tensor(dif[:, :], best[:, 1, :], best[:, 0, :], ALU.subtract).then_inc(exp_asked, 1)
                    step(dve.tensor_reduce(total[:, :], oh[:, 0].rearrange("p t e -> p e t"), AX.X, ALU.add))
                    dve.tensor_copy(all_total[:, :, :], experts(total[:, :])).then_inc(chosen, 1)
                    dve.wait_ge(exp_done, after(1))
                    step(dve.tensor_scalar(den[:, :], gate[:, 1, :], 1.0, None, ALU.add))
                    step(dve.reciprocal(gate[:, 0, :], den[:, :]))
                    step(dve.tensor_tensor(gate[:, 1, :], gate[:, 1, :], gate[:, 0, :], ALU.mult))
                else:
                    step(dve.tensor_reduce(best[:, 0, :], lg[:, :, :], AX.X, ALU.max))
                    dve.tensor_tensor(lg[:, :, :], lg[:, :, :], wide(best[:, 0, :]), ALU.subtract).then_inc(exp_asked, 1)
                    dve.wait_ge(exp_done, after(1))
                    step(dve.tensor_reduce(den[:, :], less[:, :, :], AX.X, ALU.add))
                    step(dve.reciprocal(dif[:, :], den[:, :]))
                    step(dve.tensor_tensor(less[:, :, :], less[:, :, :], wide(dif[:, :]), ALU.mult))
                    first_best(less[:, :, :], 0)
                    step(dve.tensor_copy(gate[:, 0, :], best[:, 0, :]))
                    dve.tensor_copy(den[:, :], best[:, 0, :]).then_inc(chosen, 1)
                dve.wait_ge(spare_made, after(1))
                for j in range(top):
                    dve.wait_ge(ranked, after(j + 1))
                    step(dve.tensor_tensor(flat(cand[:, :, :]), k.ps[:, 3 + j, 0:T * E], flat(oh[:, j]), ALU.mult))
                    step(dve.tensor_reduce(rank[:, :], cand[:, :, :], AX.X, ALU.add))
                    step(dve.tensor_scalar(keep[:, :], rank[:, :], float(cap), None, ALU.is_lt))
                    step(dve.tensor_tensor(weights[:, j, :], gate[:, j, :], keep[:, :], ALU.mult))
                    step(dve.tensor_scalar(slot[:, :], first[:, j, :], 8.0, float(cap), ALU.add, ALU.mult))
                    step(dve.tensor_tensor(slot[:, :], slot[:, :], rank[:, :], ALU.add))
                    step(dve.tensor_tensor(slot[:, :], slot[:, :], keep[:, :], ALU.mult))
                    step(dve.tensor_copy(gather_at[:, j, :], slot[:, :]))
                    step(dve.tensor_scalar(keep[:, :], keep[:, :], -1.0, 1.0, ALU.mult, ALU.add))
                    step(dve.tensor_tensor(keep[:, :], keep[:, :], spare[:, j, :], ALU.mult))
                    step(dve.tensor_tensor(slot[:, :], slot[:, :], keep[:, :], ALU.add))
                    step(dve.tensor_copy(scatter_at[:, j, :], slot[:, :]))

            @block.scalar
            def _(act):
                act.wait_ge(exp_asked, after(1))
                if top == 2:
                    act.activation(gate[:, 1, :], dif[:, :], ACT.Exp).then_inc(exp_done, 1)
                else:
                    act.activation(less[:, :, :], lg[:, :, :], ACT.Exp).then_inc(exp_done, 1)

            @block.tensor
            def _(pe):
                pe.wait_ge(chosen, after(1))
                for j in range(top):
                    mine = flat(oh[:, j])
                    out = k.ps[:, 3 + j, :]
                    pe.matmul(out[:, 0:T * E], k.upper[:, :], mine, start=True, stop=False)
                    if j:
                        pe.matmul(out[:, 0:T * E], k.ones[:, :], flat(all_total[:, :, :]), start=False, stop=False)
                    for s in range(1, T):
                        mm = pe.matmul(out[:, s * E:T * E], k.ones[:, :], mine[:, 0:(T - s) * E], start=False,
                                       stop=(s == T - 1))
                    mm.then_inc(ranked, 1)


def run_experts(nc, k, sent, made, w1, w2, cap, b1, b2):
    NU = cap // P
    parts = 1 if cap <= 512 else 2
    CN = cap // parts
    NB = w2.shape[1] // P
    HN = parts * NB
    RING = 3
    pairs = [(u, min(2, NU - u)) for u in range(0, NU, 2)]
    NPR = len(pairs)
    with ExitStack() as held:
        sb = tiles(nc, held)
        w1s = [sb(f"w1s{e}", [P, KD, NB * P]) for e in range(2)]
        w2s = [sb(f"w2s{e}", [P, NB, D]) for e in range(2)]
        xs = [sb(f"xs{e}", [P, NU, D]) for e in range(2)]
        b2s = [sb(f"b2s{e}", [P, D]) for e in range(2)] if b2 is not None else None
        xT = sb("xT", [P, KD, cap])
        hT = sb("hT", [P, NB, cap])
        ys = [sb(f"ys{e}", [P, NU, D]) for e in range(2)]
        loads = 3 if b2 is None else 4
        with stage(nc, "first_loaded", "second_loaded", "turned", "copied", "h_ready", "h_done", "y_ready",
                   "y_copied", "stored") as (
                block, first_loaded, second_loaded, turned, copied, h_ready, h_done, y_ready, y_copied, stored):
            loaded = (first_loaded, second_loaded)

            @block.sync
            def _(sp):
                def load(i, e):
                    one = bass.ds(2 * i + e, 1)
                    sp.dma_start(xs[e][:, :, :], sent[bass.ds((2 * i + e) * cap, cap), :].rearrange(
                        "(p u) d -> p u d", u=NU)).then_inc(loaded[e], 16)
                    sp.dma_start(w1s[e][:, :, :], w1[one].rearrange("e (c p) f -> p (e c) f", p=P)
                                 ).then_inc(loaded[e], 16)
                    sp.dma_start(w2s[e][:, :, :], w2[one].rearrange("e (c p) f -> p (e c) f", p=P)
                                 ).then_inc(loaded[e], 16)
                    if b2 is not None:
                        sp.dma_start(b2s[e][:, :], b2[one, :].to_broadcast([P, D])).then_inc(loaded[e], 16)

                def store(i, e):
                    sp.wait_ge(y_copied, after(2 * NU * i + NU * (e + 1)))
                    sp.dma_start(made[bass.ds((2 * i + e) * cap, cap), :].rearrange("(p u) d -> p u d", u=NU),
                                 ys[e][:, :, :]).then_inc(stored, 16)

                for e in range(2):
                    load(0, e)
                with sp.Fori(0, E // 2 - 1) as i:
                    for e in range(2):
                        store(i, e)
                        load(i + 1, e)
                for e in range(2):
                    store(E // 2 - 1, e)
                sp.wait_ge(stored, after(16 * E))

            @block.tensor
            def _(pe):
                with pe.Fori(0, E // 2) as i:
                    for e in range(2):
                        pe.wait_ge(loaded[e], after(16 * loads * (i + 1)))
                        for n, (u, m) in enumerate(pairs):
                            pe.wait_ge(copied, after(2 * NPR * i + (NPR * e + slot_free(n, NPR, 2))))
                            for v in range(m):
                                for c in range(KD):
                                    mm = pe.transpose(k.ps[:, n % 2, (c * m + v) * P:(c * m + v + 1) * P],
                                                      xs[e][:, u + v, c * P:(c + 1) * P], k.ident[:, :])
                            mm.then_inc(turned, 1)
                        pe.wait_ge(copied, after(2 * NPR * i + NPR * (e + 1)))
                        for n in range(HN):
                            at, j = n // NB * CN, n % NB
                            pe.wait_ge(h_done, after(2 * HN * i + (HN * e + slot_free(n, HN, RING))))
                            for c in range(KD):
                                mm = pe.matmul(k.ps[:, 2 + n % RING, 0:CN], w1s[e][:, c, j * P:(j + 1) * P],
                                               xT[:, c, at:at + CN], start=(c == 0), stop=(c == KD - 1))
                            mm.then_inc(h_ready, 1)
                        pe.wait_ge(h_done, after(2 * HN * i + HN * (e + 1)))
                        for u in range(NU):
                            n = NU * e + u
                            pe.wait_ge(y_copied, after(2 * NU * i + slot_free(n, 2 * NU, 3)))
                            for j in range(NB):
                                mm = pe.matmul(k.ps[:, 5 + n % 3, 0:D], hT[:, j, u * P:(u + 1) * P], w2s[e][:, j, :],
                                               start=(j == 0), stop=(j == NB - 1))
                            mm.then_inc(y_ready, 1)

            @block.scalar
            def _(act):
                with act.Fori(0, E // 2) as i:
                    for e in range(2):
                        act.wait_ge(y_ready, after(2 * NU * i + NU * e))
                        for n in range(HN):
                            at, j = n // NB * CN, n % NB
                            act.wait_ge(h_ready, after(2 * HN * i + (HN * e + n + 1)))
                            bias = 0.0 if b1 is None else b1[:, bass.ds((2 * i + e) * NB + j, 1)]
                            act.activation(hT[:, j, at:at + CN], k.ps[:, 2 + n % RING, 0:CN],
                                           ACT.Gelu if b1 is None else ACT.Relu, bias=bias).then_inc(h_done, 1)

            @block.vector
            def _(dve):
                with dve.Fori(0, E // 2) as i:
                    for e in range(2):
                        for n, (u, m) in enumerate(pairs):
                            if n == 0:
                                dve.wait_ge(h_ready, after(2 * HN * i + HN * e))
                            dve.wait_ge(turned, after(2 * NPR * i + (NPR * e + n + 1)))
                            dve.tensor_copy(xT[:, :, u * P:(u + m) * P], k.ps[:, n % 2, 0:KD * m * P].rearrange(
                                "p (c n) -> p c n", c=KD)).then_inc(copied, 1)
                        dve.wait_ge(stored, after(16 * 2 * i))
                        if b2 is not None:
                            dve.wait_ge(loaded[e], after(16 * loads * (i + 1)))
                        for u in range(NU):
                            n = NU * e + u
                            dve.wait_ge(y_ready, after(2 * NU * i + (n + 1)))
                            psY = k.ps[:, 5 + n % 3, 0:D]
                            if b2 is None:
                                dve.tensor_copy(ys[e][:, u, :], psY).then_inc(y_copied, 1)
                            else:
                                dve.tensor_tensor(ys[e][:, u, :], psY, b2s[e][:, :], ALU.add).then_inc(y_copied, 1)


def mixture(nc, k, wg, w1, w2, cap, top, b1=None, b2=None):
    slots = E * cap
    ID = nc.next_id()
    sent = nc.dram_tensor(f"sent_{ID}", (slots + top * TOK, D), F32).ap()
    made = nc.dram_tensor(f"made_{ID}", (slots, D), F32).ap()
    rows_sent, *rows_fetched = k.mixture_sems[top]
    with ExitStack() as held:
        sb = tiles(nc, held)
        gather_at, scatter_at = (sb(n, [P, top, T], U32) for n in ("gather_at", "scatter_at"))
        weights = sb("weights", [P, top, T])
        with ExitStack() as inner:
            sb2 = tiles(nc, inner)
            rows = sb2("rows", [P, T, D])
            zeros = sb2("zeros", [P, 2048])
            layer_norm_rows(nc, k, k.x, rows, None)
            with stage(nc, "zeroed", "filled") as (block, zeroed, filled):
                @block.vector
                def _(dve):
                    dve.memset(zeros[:, :], 0.0).then_inc(zeroed, 1)

                @block.sync
                def _(sp):
                    n = slots * D // P // 2048
                    sp.wait_ge(zeroed, after(1))
                    for j in range(n):
                        sp.dma_start(sent[0:slots, :].rearrange("(p r) d -> p (r d)", p=P)[:, j * 2048:(j + 1) * 2048],
                                     zeros[:, :]).then_inc(filled, 16)
                    sp.wait_ge(filled, after(16 * n))
            route(nc, k, rows, wg, cap, top, slots, gather_at, scatter_at, weights)
            with stage(nc) as (block,):
                @block.gpsimd
                def _(pool):
                    for j in range(top):
                        for t in range(T):
                            pool.indirect_dma_start(
                                sent, bass.IndirectOffsetOnAxis(ap=scatter_at[:, j, t:t + 1], axis=0),
                                rows[:, t, :], None).then_inc(rows_sent, 16)
                    pool.wait_ge(rows_sent, 16 * top * T)
        run_experts(nc, k, sent, made, w1, w2, cap, b1, b2)
        back = sb("back", [P, top, T, D])
        with stage(nc, "added") as (block, added):
            @block.gpsimd
            def _(pool):
                for t in range(T):
                    for j in range(top):
                        pool.indirect_dma_start(
                            back[:, j, t, :], None, made,
                            bass.IndirectOffsetOnAxis(ap=gather_at[:, j, t:t + 1], axis=0)).then_inc(rows_fetched[t // GT], 16)

            @block.vector
            def _(dve):
                for g in range(G):
                    dve.wait_ge(rows_fetched[g], 16 * top * GT)
                    for j in range(top):
                        if j:
                            dve.wait_ge(added, after(g + 1))
                        for u in range(GT):
                            t = g * GT + u
                            row = k.x[:, t, :]
                            ins = dve.scalar_tensor_tensor(out=row, in0=back[:, j, t, :], scalar=weights[:, j, t:t + 1], in1=row,
                                                           op0=ALU.mult, op1=ALU.add)
                        if j == 0:
                            ins.then_inc(added, 1)


def layer1_ffn(nc, k, a):
    w1, w2 = a["L1_ffn_c_fc"], a["L1_ffn_c_proj"]
    cap = 2 * TOK * 5 // 4 // E
    cap += cap % 2
    mixture(nc, k, a["L1_ffn_w_g"], w1, w2, cap, 2)


def layer3_ffn(nc, k, a):
    mixture(nc, k, a["L3_ffn_wg"], a["L3_ffn_w1"], a["L3_ffn_w2"], TOK // E, 1, k.col("L3_ffn_b1"), a["L3_ffn_b2"])


LAYERS = [layer0_attention, layer0_ffn, layer1_attention, layer1_ffn, layer2_attention, layer2_ffn, layer3_attention,
          layer3_ffn]

COLUMNS = [("L0_xattn_bq", 2), ("L0_xattn_bk", 2)]
COLUMNS += [("L1_xattn_" + n, w) for n, w in [
    ("a1_lnx_g", 2), ("a1_lnx_b", 2), ("a1_lny_g", 2), ("a1_lny_b", 2), ("a1_ln3_g", 2), ("a1_ln3_b", 2),
    ("a1_li2_b", 8), ("a2_lnx_g", 2), ("a2_lnx_b", 2), ("a2_lny_g", 1), ("a2_lny_b", 1), ("a2_ln3_g", 2),
    ("a2_ln3_b", 2), ("a2_li2_b", 8)]]

COLUMNS += [("L0_ffn_gate_up_proj_bias", 32), ("L3_xattn_bq", 2), ("L3_xattn_bk", 2), ("L3_ffn_b1", 64)]
COLUMNS += [(f"L2_ffn_{layer}_{n}", w) for layer in range(2) for n, w in [("ln_g", 2), ("ln_b", 2), ("b1", 12)]]


def build(nc, a, out, layers=range(8)):
    ncols = sum(n for _, n in COLUMNS)
    with ExitStack() as held:
        sb = tiles(nc, held)

        class K:
            x = sb("x_rows", [P, T, D])
            ctx = sb("ctx_rows", [P, BATCH, IMG])
            ctxT = sb("ctxT", [P, BATCH, CTX])
            cols = sb("cols_sb", [P, ncols])
            ident = sb("ident", [P, P])
            ones = sb("ones", [P, P])
            hm16 = sb("hm16", [P, 8])
            hm32 = sb("hm32", [P, 4])
            vmask = sb("vmask", [P, 5, 3])
            eidx = sb("eidx", [P, 8])
            upper = sb("upper", [P, P])
            ps = held.enter_context(nc.psum_tensor("ps", [P, 8, 512], F32))
            mixture_sems = {top: [held.enter_context(nc.semaphore(f"{n}_top{top}"))
                                  for n in ("rows_sent", *(f"rows_fetched{g}" for g in range(G)))]
                            for top in (1, 2)}

            @staticmethod
            def col(name):
                at = 0
                for n, width in COLUMNS:
                    if n == name:
                        return K.cols[:, at:at + width]
                    at += width
                raise KeyError(name)

        build_constants(nc, K, a["columns"], a["ctx_512"], a["x"])
        for n in layers:
            LAYERS[n](nc, K, a)
        with stage(nc, "stored") as (block, stored):
            @block.sync
            def _(sp):
                sp.dma_start(out.rearrange("b (t p) d -> p (b t) d", p=P), K.x[:, :, :]).then_inc(stored, 16)
                sp.wait_ge(stored, after(16))



def rotary_tables():
    f = np.float32
    half = np.arange(0, LD, 2, dtype=f)
    inv_freq = f(1.0) / f(10000.0) ** (half / f(LD))
    t = np.arange(SEQ, dtype=f)
    freqs = t[:, None] * inv_freq[None, :]
    base = (half + f(0.4 * LD)) / f(1.4 * LD)
    scale = base[None, :] ** ((t - f(SEQ // 2)) / f(P // 2))[:, None]
    cos, sin = np.cos(freqs), np.sin(freqs)
    qc, qs, kc, ks = cos * scale * f(8), sin * scale * f(8), cos / scale, sin / scale
    both = lambda q, kk, sign: np.stack([np.concatenate([sign * q, q], 1), np.concatenate([sign * kk, kk], 1)], 1)
    turn = lambda v: np.ascontiguousarray(v.reshape(TB, P, 2, LD).transpose(1, 0, 2, 3), dtype=f)
    return turn(both(qc, kc, f(1))), turn(both(qs, ks, f(-1)))


def lay_out(inputs):
    a = {n: np.ascontiguousarray(v) for n, v in inputs.items()}
    wkv = a.pop("L2_xattn_Wkv")
    a["L2_xattn_Wk"] = np.ascontiguousarray(wkv[:D].T)
    a["L2_xattn_Wv"] = np.ascontiguousarray(wkv[D:].T)
    for n in ("L2_xattn_Wq", "L2_xattn_Wo"):
        a[n] = np.ascontiguousarray(a[n].T)
    for n in ("a1_wq", "a1_wk", "a1_wv", "a2_wq", "a2_wk", "a2_wv"):
        w = a["L1_xattn_" + n]
        a["L1_xattn_" + n] = np.ascontiguousarray(w.transpose(1, 0, 2).reshape(w.shape[1], -1))
    a["rotary_cos"], a["rotary_sin"] = rotary_tables()
    for n in ("L0_ffn_gate_up_proj", "L0_ffn_gate_up_proj_bias"):
        a[n] = np.ascontiguousarray(np.concatenate([a[n][..., 0::2], a[n][..., 1::2]], axis=-1))
    of = dict(a)
    for layer in range(2):
        for n in ("ln_g", "ln_b"):
            of[f"L2_ffn_{layer}_{n}"] = a[f"L2_ffn_{n}"][layer]
        b1 = a["L2_ffn_b1"][layer].reshape(2, -1)
        of[f"L2_ffn_{layer}_b1"] = np.pad(b1, ((0, 0), (0, -b1.shape[1] % P)))
    vectors = []
    for name, n in COLUMNS:
        v = of[name].reshape(-1)
        vectors.append(v.reshape(n, P).T)
    a["columns"] = np.ascontiguousarray(np.concatenate(vectors, axis=1))
    return a


def kernel(**inputs):
    import concourse.bacc as _bacc
    from concourse.bass_utils import run_bass_kernel_spmd as _run

    arrays = lay_out(inputs)
    nc = _bacc.Bacc("TRN2", target_bir_lowering=False, num_devices=1)
    named = {f"in_{n}": v for n, v in arrays.items()}
    aps = {n: nc.dram_tensor(f"in_{n}", v.shape, mybir.dt.from_np(v.dtype), kind="ExternalInput").ap()
           for n, v in arrays.items()}
    out = nc.dram_tensor("out", (BATCH, SEQ, D), F32, kind="ExternalOutput").ap()
    build(nc, aps, out)
    r = _run(nc, [named], core_ids=[0])
    return r.results[0]["out"]
```

```python
from contextlib import ExitStack, contextmanager

import numpy as np
import concourse.bass as bass
from concourse import mybir

F32 = mybir.dt.float32
F32R = mybir.dt.float32r
BF16 = mybir.dt.bfloat16
I32 = mybir.dt.int32
U32 = mybir.dt.uint32
ALU = mybir.AluOpType
ACT = mybir.ActivationFunctionType
AX = mybir.AxisListType

P = 128
BATCH = 2
SEQ = 1024
TOK = BATCH * SEQ
T = TOK // P
TB = SEQ // P
D = 256
KD = D // P
CTX = 77
CP = 80
IMG = 128
GT = 4
G = T // GT
GN = GT * P
EPS = 1e-5
HIGH_PART = -4096
NEG = -1e30


START = 8


def after(n):
    return n + START


def slot_free(j, count, ring):
    return j - ring + 1 if j >= ring else max(m for m in range(count) if m % ring == j) - count + 1


@contextmanager
def stage(nc, *names):
    with ExitStack() as held:
        sems = [held.enter_context(nc.semaphore(n)) for n in names]
        if sems:
            with nc.Block() as opening:
                @opening.sync
                def _(sp):
                    for s in sems:
                        sp.sem_clear(s)
                        sp.sem_inc(s, START)
        with nc.Block() as block:
            yield (block, *sems)


def tiles(nc, held):
    def make(name, shape, dt=F32):
        return held.enter_context(nc.sbuf_tensor(f"{name}_{nc.next_id()}", shape, dt))
    return make


class Chain:

    def __init__(self, eng, sem, base=0):
        self.eng, self.sem, self.base, self.n = eng, sem, base, 0

    def __call__(self, ins):
        self.n += 1
        ins.then_inc(self.sem, 1)
        self.eng.wait_ge(self.sem, after(self.base + self.n))



def build_constants(nc, k, cols_dram, ctx_dram, x_dram):
    with stage(nc, "x_loaded", "vectors_loaded", "ctx_loaded", "pool_step", "ctx_turned", "ctx_copied", "ones_set") as (
            block, x_loaded, vectors_loaded, ctx_loaded, pool_step, ctx_turned, ctx_copied, ones_set):
        @block.sync
        def _(sp):
            sp.dma_start(k.x[:, :, :], x_dram.rearrange("b (t p) d -> p (b t) d", p=P)).then_inc(x_loaded, 16)
            sp.dma_start(k.ctx[0:CTX, :, :], ctx_dram.rearrange("b s d -> s b d")).then_inc(ctx_loaded, 16)
            sp.dma_start(k.cols[:, :], cols_dram).then_inc(vectors_loaded, 16)
            sp.wait_ge(x_loaded, after(16))
            sp.wait_ge(vectors_loaded, after(16))

        @block.gpsimd
        def _(pool):
            step = Chain(pool, pool_step)
            step(pool.memset(k.ident[:, :], 0.0))
            step(pool.affine_select(out=k.ident[:, :], in_=k.ident[:, :], compare_op=ALU.not_equal, fill=1.0,
                                    base=0, pattern=[[-1, P]], channel_multiplier=1))
            step(pool.memset(k.upper[:, :], 1.0))
            step(pool.affine_select(out=k.upper[:, :], in_=k.upper[:, :], compare_op=ALU.is_gt, fill=0.0,
                                    base=0, pattern=[[1, P]], channel_multiplier=-1))
            for mask, d in ((k.hm16, 16), (k.hm32, 32)):
                n = P // d
                step(pool.memset(mask[:, :], 1.0))
                step(pool.affine_select(out=mask[:, :], in_=mask[:, :], compare_op=ALU.is_ge, fill=0.0,
                                        base=0, pattern=[[-d, n]], channel_multiplier=1))
                step(pool.affine_select(out=mask[:, :], in_=mask[:, :], compare_op=ALU.is_ge, fill=0.0,
                                        base=d - 1, pattern=[[d, n]], channel_multiplier=-1))
            for j in range(5):
                h0 = heads_of_block(j)[0]
                vm = k.vmask[:, j, :]
                step(pool.memset(vm, 1.0))
                step(pool.affine_select(out=vm, in_=vm, compare_op=ALU.is_ge, fill=0.0, base=P * j - CP * h0,
                                        pattern=[[-CP, 3]], channel_multiplier=1))
                step(pool.affine_select(out=vm, in_=vm, compare_op=ALU.is_ge, fill=0.0, base=CP * h0 + CP - 1 - P * j,
                                        pattern=[[CP, 3]], channel_multiplier=-1))
            step(pool.iota(k.eidx[:, :], pattern=[[1, 8]], base=0, channel_multiplier=0,
                           allow_small_or_imprecise_dtypes=True))

        @block.tensor
        def _(pe):
            pe.wait_ge(ctx_loaded, after(16))
            pe.wait_ge(pool_step, after(2))
            for b in range(BATCH):
                pe.transpose(k.ps[:, b, 0:CTX], k.ctx[0:CTX, b, :], k.ident[0:CTX, 0:CTX]).then_inc(ctx_turned, 1)

        @block.vector
        def _(dve):
            dve.memset(k.ones[:, :], 1.0).then_inc(ones_set, 1)
            for b in range(BATCH):
                dve.wait_ge(ctx_turned, after(b + 1))
                dve.tensor_copy(k.ctxT[:, b, :], k.ps[:, b, 0:CTX]).then_inc(ctx_copied, 1)



NEWTON = 3
NORM_STEPS = 6 + 3 * NEWTON
ROOT_SEED = 0x5F3759DF


def mean_of(norm, t):
    return norm[:, 6, bass.ds(t, 1)]


def rstd_of(norm, t):
    return norm[:, 7, bass.ds(t, 1)]


def row_norms(dve, step, src, norm, first, n):
    tmp = norm[:, :, first:first + n]
    stats = tmp[:, 0:6, :]
    mean, rstd, var, dif, nw = (tmp[:, 6 + j, :] for j in range(5))
    before = step.n
    for u in range(n):
        ins = dve.bn_stats(stats[:, :, u], src[:, first + u, :])
    step(ins)
    dve.tensor_tensor(mean, stats[:, 1, :], stats[:, 4, :], ALU.add)
    dve.tensor_tensor(dif, stats[:, 1, :], stats[:, 4, :], ALU.subtract)
    step(dve.tensor_tensor(var, stats[:, 2, :], stats[:, 5, :], ALU.add))
    dve.tensor_scalar(mean, mean, 0.5, None, ALU.mult)
    dve.tensor_tensor(dif, dif, dif, ALU.mult)
    step(dve.tensor_scalar(var, var, 1.0 / src.shape[2], EPS, ALU.mult, ALU.add))
    step(dve.scalar_tensor_tensor(out=var, in0=dif, scalar=0.25, in1=var, op0=ALU.mult, op1=ALU.add))
    step(dve.tensor_scalar(nw.bitcast(I32), var.bitcast(I32), 1, None, ALU.logical_shift_right))
    step(dve.tensor_scalar(rstd.bitcast(I32), nw.bitcast(I32), -1.0, float(ROOT_SEED), ALU.mult, ALU.add))
    for _ in range(NEWTON):
        step(dve.scalar_tensor_tensor(out=nw, in0=rstd, scalar=-0.5, in1=var, op0=ALU.mult, op1=ALU.mult))
        step(dve.tensor_tensor(nw, nw, rstd, ALU.mult))
        step(dve.scalar_tensor_tensor(out=rstd, in0=nw, scalar=1.5, in1=rstd, op0=ALU.add, op1=ALU.mult))
    assert step.n - before == NORM_STEPS



def normalise_group(dve, g, xn, src, norm, turned, normed):
    for u in range(GT):
        if u == 0:
            dve.wait_ge(turned, after(g * GT))
        t = g * GT + u
        if norm is None:
            dve.tensor_copy(xn[:, u, :], src[:, t, :]).then_inc(normed, 1)
        else:
            dve.tensor_scalar(xn[:, u, :], src[:, t, :], mean_of(norm, t), rstd_of(norm, t),
                              ALU.subtract, ALU.mult).then_inc(normed, 1)


def first_group(dve, norm_step, xn, src, norm, turned, normed, meanwhile=None):
    step = Chain(dve, norm_step)
    row_norms(dve, step, src, norm, 0, GT)
    normalise_group(dve, 0, xn, src, norm, turned, normed)
    if meanwhile is not None:
        meanwhile()
    row_norms(dve, step, src, norm, GT, T - GT)


def each_group(eng, body):
    with eng.Fori(0, G - 1) as g:
        body(g, False)
    body(G - 1, True)


def turn_group(pe, g, k, xn, psT, normed, turned, copied, copies):
    for u in range(GT):
        if u == 0:
            pe.wait_ge(copied, after(g * 2 * copies))
        pe.wait_ge(normed, after(g * GT + (u + 1)))
        for c in range(KD):
            m = pe.transpose(psT[:, u // 2, (u % 2 * KD + c) * P:(u % 2 * KD + c + 1) * P],
                             xn[:, u, c * P:(c + 1) * P], k.ident[:, :])
        m.then_inc(turned, 1)


def copy_group(act, g, xT, psT, gains, turned, copied, xT_read, reads):
    for q in range(2):
        if q == 0 and xT_read is not None:
            act.wait_ge(xT_read, after(g * reads))
        act.wait_ge(turned, after(g * GT + (2 * q + 2)))
        turned_pair = psT[:, q, :].rearrange("p (u c n) -> p c u n", c=KD, n=P)
        for dst, gain in zip(xT, gains):
            out = dst[:, :, q * 2 * P:(q + 1) * 2 * P].rearrange("p c (u n) -> p c u n", n=P)
            if gain is None:
                act.activation(out, turned_pair, ACT.Copy).then_inc(copied, 1)
            else:
                for c in range(KD):
                    m = act.activation(out[:, c], turned_pair[:, c], ACT.Identity,
                                       scale=gain[0][:, c:c + 1], bias=gain[1][:, c:c + 1])
                m.then_inc(copied, 1)



def low_part(eng, low, whole, high):
    return eng.tensor_tensor(low, whole, high.bitcast(F32), ALU.subtract)


def product(pe, out, left, right, start, stop):
    (lh, ll), (rh, rl) = left, right
    pe.matmul(out, lh, rh, start=start, stop=False)
    pe.matmul(out, lh, rl, start=False, stop=False)
    return pe.matmul(out, ll, rh, start=False, stop=stop)



def ffn(nc, k, src, acc, w1, w2, gain, b1, b2row, glu=False, meanwhile=None):
    F = w2.shape[0]
    blocks = [(f, min(P, F - f)) for f in range(0, F, P)]
    NB = len(blocks)
    full = F // P
    rest = F - full * P
    RING = 4
    with ExitStack() as held:
        sb = tiles(nc, held)
        w1s, w1h, w1l = (sb(n, [P, KD, w1.shape[1]], t) for n, t in (("w1s", F32), ("w1h", F32R), ("w1l", F32R)))
        w2s, w2h, w2l = (sb(n, [P, NB, D], t) for n, t in (("w2s", F32), ("w2h", F32R), ("w2l", F32R)))
        b2s = sb("b2s", [P, D])
        xn = sb("xn", [P, GT, D])
        xT = sb("xT", [P, KD, GN])
        xh, xl = sb("xh", [P, KD, GN], F32R), sb("xl", [P, KD, GN], F32R)
        hw = sb("hw", [P, RING, GN])
        hh, hl = sb("hh", [P, NB, GN], F32R), sb("hl", [P, NB, GN], F32R)
        gl = sb("gl", [P, 2, GN]) if glu else None
        norm = sb("norm", [P, 11, T])
        psT = k.ps[:, 0:2, :]
        NH = 4 if glu else 3
        psH = [k.ps[:, 2 + j, :] for j in range(NH)]
        psY = [k.ps[:, 6 + j, 0:D] for j in range(2)]
        w2_places = [(slice(0, P), slice(0, full))] + ([(slice(0, rest), slice(full, NB))] if rest else [])
        NW = 1 + len(w2_places)
        with stage(nc, "w1_loaded", "w2_loaded", "w_high", "w1_split", "w2_split", "normed", "turned", "copied",
                   "x_high", "x_split", "h_ready", "h_done", "h_high", "h_split", "gate_done", "y_ready", "y_added",
                   "norm_step", "bias_added", "moved") as (
                block, w1_loaded, w2_loaded, w_high, w1_split, w2_split, normed, turned, copied,
                x_high, x_split, h_ready, h_done, h_high, h_split, gate_done, y_ready, y_added,
                norm_step, bias_added, moved):
            @block.sync
            def _(sp):
                sp.dma_start(w1s[:, :, :], w1.rearrange("(c p) f -> p c f", p=P)).then_inc(w1_loaded, 16)
                sp.dma_start(w2s[:, 0:full, :],
                             w2[0:full * P, :].rearrange("(c p) f -> p c f", p=P)).then_inc(w2_loaded, 16)
                if rest:
                    sp.dma_start(w2s[0:rest, full, :], w2[full * P:F, :]).then_inc(w2_loaded, 16)
                sp.dma_start(b2s[:, :], b2row.to_broadcast([P, D])).then_inc(w2_loaded, 16)
                if meanwhile:
                    sp.dma_start(*meanwhile).then_inc(moved, 16)
                    sp.wait_ge(moved, after(16))
            w2_all = 16 * NW

            @block.tensor
            def _(pe):
                def first_layer(out, m, at):
                    for c in range(KD):
                        mm = product(pe, out[0:m, :], (w1h[:, c, at:at + m], w1l[:, c, at:at + m]),
                                     (xh[:, c, :], xl[:, c, :]), start=(c == 0), stop=(c == KD - 1))
                    mm.then_inc(h_ready, 1)

                def hidden(g):
                    pe.wait_ge(x_split, after(g + 1))
                    for j, (f, m) in enumerate(blocks):
                        if not glu:
                            pe.wait_ge(h_done, after(g * NB + slot_free(j, NB, NH)))
                            first_layer(psH[j % NH], m, f)
                        else:
                            pe.wait_ge(h_done, after(g * NB + (j - 1)))
                            first_layer(psH[2 * (j % 2) + 1], m, F + f)
                            first_layer(psH[2 * (j % 2)], m, f)

                def output(g):
                    pe.wait_ge(w2_split, after(NW - 1))
                    pe.wait_ge(h_split, after((g + 1) * NB))
                    for u in range(GT):
                        pe.wait_ge(y_added, after(g * GT + (u - 1)))
                        for j, (f, m) in enumerate(blocks):
                            at = slice(u * P, (u + 1) * P)
                            mm = product(pe, psY[u % 2], (hh[0:m, j, at], hl[0:m, j, at]),
                                         (w2h[0:m, j, :], w2l[0:m, j, :]), start=(j == 0), stop=(j == NB - 1))
                        mm.then_inc(y_ready, 1)

                def body(g, last):
                    hidden(g)
                    if not last:
                        turn_group(pe, g + 1, k, xn, psT, normed, turned, copied, 1)
                    output(g)

                turn_group(pe, 0, k, xn, psT, normed, turned, copied, 1)
                pe.wait_ge(w1_split, after(1))
                each_group(pe, body)

            @block.scalar
            def _(act):
                hidden = 2 * NB if glu else NB

                def body(g, last):
                    for j, (f, m) in enumerate(blocks):
                        if not glu:
                            act.wait_ge(h_ready, after(g * NB + (j + 1)))
                            act.wait_ge(h_split, after(g * NB + (j - RING + 1)))
                            act.activation(hw[0:m, j % RING, :], psH[j % NH][0:m, :], ACT.Gelu,
                                           bias=b1[0:m, j:j + 1]).then_inc(h_done, 1)
                        else:
                            act.wait_ge(h_ready, after(g * 2 * NB + (2 * j + 1)))
                            act.wait_ge(h_done, after(g * NB + (j - 1)))
                            act.activation(gl[0:m, j % 2, :], psH[2 * (j % 2) + 1][0:m, :], ACT.Gelu,
                                           bias=b1[0:m, NB + j:NB + j + 1]).then_inc(gate_done, 1)
                    if not last:
                        copy_group(act, g + 1, [xT], psT, [gain], turned, copied, h_ready, hidden)

                act.wait_ge(w1_loaded, after(16))
                act.activation(w1h[:, :, :], w1s[:, :, :], ACT.Copy).then_inc(w_high, 1)
                copy_group(act, 0, [xT], psT, [gain], turned, copied, h_ready, hidden)
                act.wait_ge(w2_loaded, after(w2_all))
                for p, c in w2_places:
                    act.activation(w2h[p, c, :], w2s[p, c, :], ACT.Copy).then_inc(w_high, 1)
                each_group(act, body)

            @block.vector
            def _(dve):
                def split_x(g):
                    dve.wait_ge(copied, after((g + 1) * 2))
                    dve.tensor_copy(xh[:, :, :], xT[:, :, :]).then_inc(x_high, 1)
                    dve.wait_ge(x_high, after(g + 1))
                    low_part(dve, xl[:, :, :], xT[:, :, :], xh[:, :, :]).then_inc(x_split, 1)

                def split_h(g, j, m):
                    dve.wait_ge(h_done, after(g * NB + (j + 1)))
                    dve.tensor_copy(hh[0:m, j, :], hw[0:m, j % RING, :]).then_inc(h_high, 1)
                    dve.wait_ge(h_high, after(g * NB + (j + 1)))
                    low_part(dve, hl[0:m, j, :], hw[0:m, j % RING, :], hh[0:m, j, :]).then_inc(h_split, 1)

                def body(g, last):
                    if not last:
                        normalise_group(dve, g + 1, xn, src, norm, turned, normed)
                    dve.wait_ge(y_ready, after(g * GT))
                    for j, (f, m) in enumerate(blocks):
                        if glu:
                            dve.wait_ge(h_ready, after(g * 2 * NB + (2 * j + 2)))
                            dve.wait_ge(gate_done, after(g * NB + (j + 1)))
                            dve.wait_ge(h_split, after(g * NB + j))
                            dve.scalar_tensor_tensor(out=hw[0:m, j % RING, :], in0=psH[2 * (j % 2)][0:m, :],
                                                     scalar=b1[0:m, j:j + 1], in1=gl[0:m, j % 2, :],
                                                     op0=ALU.add, op1=ALU.mult).then_inc(h_done, 1)
                        split_h(g, j, m)
                    if not last:
                        split_x(g + 1)
                    for u in range(GT):
                        t = g * GT + u
                        dve.wait_ge(bias_added, after(T))
                        dve.wait_ge(y_ready, after(g * GT + (u + 1)))
                        dve.tensor_tensor(acc[:, t, :], psY[u % 2], acc[:, t, :], ALU.add).then_inc(y_added, 1)

                def split_w1():
                    dve.wait_ge(w_high, after(1))
                    low_part(dve, w1l[:, :, :], w1s[:, :, :], w1h[:, :, :]).then_inc(w1_split, 1)
                    split_x(0)

                first_group(dve, norm_step, xn, src, norm, turned, normed, split_w1)
                each_group(dve, body)

            @block.gpsimd
            def _(pool):
                for n, (p, c) in enumerate(w2_places):
                    pool.wait_ge(w_high, after(n + 2))
                    low_part(pool, w2l[p, c, :], w2s[p, c, :], w2h[p, c, :]).then_inc(w2_split, 1)
                with pool.Fori(0, T) as t:
                    if acc is src:
                        pool.wait_ge(normed, after(t + 1))
                    pool.tensor_tensor(acc[:, t, :], acc[:, t, :], b2s[:, :], ALU.add).then_inc(bias_added, 1)



def project(nc, k, src, gains, turned_jobs, row_jobs, loads):
    with ExitStack() as held:
        sb = tiles(nc, held)
        xn = sb("xn", [P, GT, D])
        norm = sb("norm", [P, 11, T])
        xT = [sb(f"xT{j}", [P, KD, GN]) for j in range(len(gains))]
        psT = k.ps[:, 0:2, :]
        NC = len(gains)
        blocks = [(w, a, dst, bias, scale, f) for w, a, dst, bias, scale in turned_jobs
                  for f in range(w.shape[2] // P)]
        rows = [(w, a, dst, u, f) for w, a, dst in row_jobs for u in range(GT) for f in range(w.shape[2] // 512)]
        NF, NR = len(blocks), len(rows)
        blocks_of = [[(j, job) for j, job in enumerate(blocks) if job[1] == a] for a in range(NC)]
        rows_of = [[(j, job) for j, job in enumerate(rows) if job[1] == a] for a in range(NC)]
        RING = 3
        with stage(nc, "w_loaded", "normed", "turned", "copied_0", "copied_1", "feat_ready", "feat_out", "row_ready",
                   "row_out", "norm_step") as (
                block, w_loaded, normed, turned, copied_0, copied_1, feat_ready, feat_out, row_ready,
                row_out, norm_step):
            copied = (copied_0, copied_1)[:NC]

            @block.sync
            def _(sp):
                for dst, weights in loads:
                    sp.dma_start(dst, weights).then_inc(w_loaded, 16)

            @block.tensor
            def _(pe):
                def body(g, last):
                    for s in range(NC):
                        pe.wait_ge(copied[s], after((g + 1) * 2))
                        for j, (w, a, dst, bias, scale, f) in blocks_of[s]:
                            pe.wait_ge(feat_out, after(g * NF + slot_free(j, NF, RING)))
                            for c in range(KD):
                                mm = pe.matmul(k.ps[:, 2 + j % RING, :], w[:, c, f * P:(f + 1) * P], xT[a][:, c, :],
                                               start=(c == 0), stop=(c == KD - 1))
                            mm.then_inc(feat_ready, 1)
                        for j, (w, a, dst, u, f) in rows_of[s]:
                            pe.wait_ge(row_out, after(g * NR + slot_free(j, NR, RING)))
                            for c in range(KD):
                                mm = pe.matmul(k.ps[:, 5 + j % RING, :], xT[a][:, c, u * P:(u + 1) * P],
                                               w[:, c, f * 512:(f + 1) * 512], start=(c == 0), stop=(c == KD - 1))
                            mm.then_inc(row_ready, 1)
                        if s == 0 and not last:
                            turn_group(pe, g + 1, k, xn, psT, normed, turned, copied[-1], 1)

                turn_group(pe, 0, k, xn, psT, normed, turned, copied[-1], 1)
                pe.wait_ge(w_loaded, after(16 * len(loads)))
                each_group(pe, body)

            @block.scalar
            def _(act):
                def copy(g, s, first=False):
                    if not first:
                        if rows_of[s]:
                            act.wait_ge(row_ready, after((g - 1) * NR + (rows_of[s][-1][0] + 1)))
                        else:
                            act.wait_ge(feat_ready, after((g - 1) * NF + (blocks_of[s][-1][0] + 1)))
                    copy_group(act, g, [xT[s]], psT, [gains[s]], turned, copied[s], None, 0)

                def body(g, last):
                    for s in range(NC):
                        for j, (w, a, dst, u, f) in rows_of[s]:
                            act.wait_ge(row_ready, after(g * NR + (j + 1)))
                            act.activation(dst[:, 4 * f:4 * f + 4, bass.ds(g * GT + u, 1), :].rearrange("p a t n -> p (a t) n"),
                                           k.ps[:, 5 + j % RING, :].rearrange("p (a n) -> p a n", a=4),
                                           ACT.Copy).then_inc(row_out, 1)
                        if not last:
                            copy(g + 1, s)

                for s in range(NC):
                    copy(0, s, first=True)
                each_group(act, body)

            @block.vector
            def _(dve):
                def body(g, last):
                    if not last:
                        normalise_group(dve, g + 1, xn, src, norm, turned, normed)
                    for j, (w, a, dst, bias, scale, f) in enumerate(blocks):
                        dve.wait_ge(feat_ready, after(g * NF + (j + 1)))
                        dve.tensor_scalar(dst[:, f, bass.ds(g * GN, GN)], k.ps[:, 2 + j % RING, :],
                                          0.0 if bias is None else bias[:, f:f + 1], scale,
                                          ALU.add, ALU.mult).then_inc(feat_out, 1)

                first_group(dve, norm_step, xn, src, norm, turned, normed)
                each_group(dve, body)


def each_pair(eng, before, body):
    n = TB // 2
    for b in range(BATCH):
        if before is not None:
            before(b, b * n)
        with eng.Fori(0, n - 1) as j:
            body(b, b * n + j, False)
        body(b, b * n + n - 1, True)



def heads_of_block(j):
    return P * j // CP, (P * j + P - 1) // CP


def cross_attention(nc, k, d, srcT, QT, O, wk, wv, bk, bvrow, scale):
    NQ = 16 * d // P
    HB = P // d
    hm = k.hm16 if d == 16 else k.hm32
    W = d + 1
    with ExitStack() as held:
        sb = tiles(nc, held)
        Kbd = sb("Kbd", [P, BATCH, 16, CTX])
        Vfirst = sb("Vfirst", [P, BATCH, 2, 8 * W])
        Vbd = sb("Vbd", [P, BATCH, 10, 3 * W])
        with ExitStack() as prep:
            sb2 = tiles(nc, prep)
            wks = sb2("wks", [P, 16 * d])
            wvs = sb2("wvs", [P, 16 * d])
            bvs = sb2("bvs", [1, 16 * d])
            rep = sb2("rep", [P, BATCH, 8, CP])
            with stage(nc, "wk_loaded", "wv_loaded", "zeroed", "rep_made", "k_ready", "k_out", "v_ready", "v_out") as (
                    block, wk_loaded, wv_loaded, zeroed, rep_made, k_ready, k_out, v_ready, v_out):
                @block.sync
                def _(sp):
                    sp.dma_start(wks[:, :], wk).then_inc(wk_loaded, 16)
                    sp.dma_start(wvs[:, :], wv).then_inc(wv_loaded, 16)
                    if bvrow is not None:
                        sp.dma_start(bvs[:, :], bvrow).then_inc(wv_loaded, 16)

                @block.gpsimd
                def _(pool):
                    pool.memset(rep[:, :, :, :], 0.0).then_inc(zeroed, 1)
                    pool.memset(Vfirst[:, :, :, :], 0.0).then_inc(zeroed, 1)
                    pool.wait_ge(zeroed, after(1))
                    for b in range(BATCH):
                        pool.tensor_copy(rep[:, b, :, 0:CTX],
                                         srcT[:, b, :].unsqueeze(1).to_broadcast([P, 8, CTX])).then_inc(rep_made, 1)

                @block.tensor
                def _(pe):
                    pe.wait_ge(wk_loaded, after(16))
                    n = 0
                    for b in range(BATCH):
                        for q in range(NQ):
                            if n >= 4:
                                pe.wait_ge(k_out, after(n - 3))
                            pe.matmul(k.ps[:, n % 4, 0:CTX], wks[:, q * P:(q + 1) * P], srcT[:, b, :],
                                      start=True, stop=True).then_inc(k_ready, 1)
                            n += 1
                    pe.wait_ge(wv_loaded, after(32 if bvrow is not None else 16))
                    pe.wait_ge(rep_made, after(BATCH))
                    n = 0
                    for b in range(BATCH):
                        flat = rep[:, b, :, :].rearrange("p h c -> p (h c)")
                        for j in range(10):
                            h0, h1 = heads_of_block(j)
                            cols = slice(h0 * d, (h1 + 1) * d)
                            if n >= 4:
                                pe.wait_ge(v_out, after(n - 3))
                            out = k.ps[:, 4 + n % 4, 0:(h1 - h0 + 1) * d]
                            mm = pe.matmul(out, flat[:, j % 5 * P:(j % 5 + 1) * P], wvs[:, cols],
                                           start=True, stop=(bvrow is None))
                            if bvrow is not None:
                                mm = pe.matmul(out, k.ones[0:1, 0:P], bvs[:, cols], start=False, stop=True)
                            mm.then_inc(v_ready, 1)
                            n += 1

                @block.vector
                def _(dve):
                    n = 0
                    for b in range(BATCH):
                        for q in range(NQ):
                            dve.wait_ge(k_ready, after(n + 1))
                            for h in range(HB):
                                m = dve.tensor_scalar(Kbd[:, b, q * HB + h, :], k.ps[:, n % 4, 0:CTX],
                                                      0.0 if bk is None else bk[:, q:q + 1], hm[:, h:h + 1],
                                                      ALU.add, ALU.mult)
                            m.then_inc(k_out, 1)
                            n += 1
                    dve.wait_ge(zeroed, after(2))
                    n = 0
                    for b in range(BATCH):
                        for j in range(10):
                            h0, h1 = heads_of_block(j)
                            nh = h1 - h0 + 1
                            dst = Vfirst[:, b, j // 5, 0:nh * W] if j % 5 == 0 else Vbd[:, b, j, 0:nh * W]
                            dst = dst.rearrange("p (h w) -> p h w", w=W)
                            dve.wait_ge(v_ready, after(n + 1))
                            mask = k.vmask[:, j % 5, 0:nh].unsqueeze(2)
                            dve.tensor_copy(dst[:, :, d:W], mask)
                            dve.tensor_tensor(dst[:, :, 0:d],
                                              k.ps[:, 4 + n % 4, 0:nh * d].rearrange("p (h w) -> p h w", w=d),
                                              mask.to_broadcast([P, nh, d]), ALU.mult).then_inc(v_out, 1)
                            n += 1

        qs = sb("qs", [P, 2, NQ, P])
        neg = sb("neg", [P, 2, 8])
        sd = sb("sd", [P, 2, 8, CTX])
        pr = sb("pr", [P, 2, 8, CP])
        pT = sb("pT", [P, 2, 5, P])
        rsum = sb("rsum", [P, 2, 8])
        score_view = lambda c: k.ps[:, 2 * (c % 2):2 * (c % 2) + 2, 0:4 * CTX].rearrange("p b (h n) -> p b h n", n=CTX)
        psPT = k.ps[:, 4:6, :]
        IT = 4
        with stage(nc, "pads_zeroed", "q_staged", "s_ready", "shifted", "exp_done", "pt_ready", "pt_copied",
                   "o_ready", "o_done", "max_done", "inverse_done") as (
                block, pads_zeroed, q_staged, s_ready, shifted, exp_done, pt_ready, pt_copied, o_ready, o_done,
                max_done, inverse_done):
            @block.gpsimd
            def _(pool):
                pool.memset(pr[:, :, :, :], 0.0).then_inc(pads_zeroed, 1)
                with pool.Fori(0, T // 2) as i:
                    for u in range(2):
                        pool.wait_ge(s_ready, after(i * IT + (2 * u - 2)))
                        pool.tensor_copy(qs[:, u, :, :], QT[:, :, bass.ds((2 * i + u) * P, P)]).then_inc(q_staged, 1)

            @block.tensor
            def _(pe):
                def scores(b, it, c):
                    u, half = c // 2 % 2, c % 2
                    pe.wait_ge(q_staged, after(it * 2 + (c // 2 + 1)))
                    pe.wait_ge(shifted, after(it * IT + (c - 1)))
                    for j in range(2):
                        h = 8 * half + 4 * j
                        mm = pe.matmul(k.ps[:, 2 * (c % 2) + j, 0:4 * CTX], qs[:, u, h // HB, :],
                                       Kbd[:, b, h:h + 4, :].rearrange("p h n -> p (h n)"), start=True, stop=True)
                    mm.then_inc(s_ready, 1)

                def turn(it, c):
                    pe.wait_ge(exp_done, after(it * IT + (c + 1)))
                    pe.wait_ge(pt_copied, after(it * IT + c))
                    flat = pr[:, c % 2, :, :].rearrange("p h n -> p (h n)")
                    for j in range(5):
                        mm = pe.transpose(psPT[:, j // 4, j % 4 * P:(j % 4 + 1) * P], flat[:, j * P:(j + 1) * P],
                                          k.ident[:, :])
                    mm.then_inc(pt_ready, 1)

                def values(b, it, c):
                    half = c % 2
                    pe.wait_ge(pt_copied, after(it * IT + (c + 1)))
                    pe.wait_ge(o_done, after(it * IT + (c - 1)))
                    for j in range(5):
                        h0, h1 = heads_of_block(5 * half + j)
                        if j == 0:
                            out, v = k.ps[:, 6 + c % 2, 0:8 * W], Vfirst[:, b, half, :]
                        else:
                            out = k.ps[:, 6 + c % 2, (h0 - 8 * half) * W:(h1 + 1 - 8 * half) * W]
                            v = Vbd[:, b, 5 * half + j, 0:(h1 - h0 + 1) * W]
                        mm = pe.matmul(out, pT[:, c % 2, j, :], v,
                                       start=(j == 0), stop=(j == 4))
                    mm.then_inc(o_ready, 1)

                def before(b, it):
                    scores(b, it, 0)
                    scores(b, it, 1)

                def body(b, it, last):
                    for c in range(IT):
                        if c + 2 < IT or not last:
                            scores(b, it, c + 2)
                        turn(it, c)
                        if c:
                            values(b, it, c - 1)
                    values(b, it, IT - 1)

                each_pair(pe, before, body)

            @block.scalar
            def _(act):
                def probs(it, c):
                    act.wait_ge(shifted, after(it * IT + (c + 1)))
                    act.wait_ge(pt_ready, after(it * IT + (c - 1)))
                    act.activation(pr[:, c % 2, :, 0:CTX], sd[:, c % 2, :, :], ACT.Exp,
                                   scale=scale).then_inc(exp_done, 1)

                def copy_pt(it, c):
                    act.wait_ge(pt_ready, after(it * IT + (c + 1)))
                    act.wait_ge(o_ready, after(it * IT + (c - 1)))
                    act.activation(pT[:, c % 2, :, :].rearrange("p a n -> p (a n)"),
                                   psPT.rearrange("p a n -> p (a n)")[:, 0:5 * P], ACT.Copy).then_inc(pt_copied, 1)

                def body(b, it, last):
                    for c in range(IT):
                        if c + 1 < IT or not last:
                            probs(it, c + 1)
                        copy_pt(it, c)

                act.wait_ge(pads_zeroed, after(1))
                each_pair(act, lambda b, it: probs(it, 0), body)

            @block.vector
            def _(dve):
                def shift(it, c):
                    dve.wait_ge(s_ready, after(it * IT + (c + 1)))
                    dve.wait_ge(exp_done, after(it * IT + (c - 1)))
                    m = neg[:, c % 2, :].rearrange("p (b h) -> p b h", b=2)
                    dve.tensor_reduce(m, score_view(c), AX.X, ALU.max).then_inc(max_done, 1)
                    dve.wait_ge(max_done, after(it * IT + (c + 1)))
                    dve.tensor_tensor(sd[:, c % 2, :, :].rearrange("p (b h) n -> p b h n", b=2), score_view(c),
                                      m.unsqueeze(3).to_broadcast([P, 2, 4, CTX]), ALU.subtract).then_inc(shifted, 1)

                def normal(it, c):
                    u, half = c // 2, c % 2
                    dve.wait_ge(o_ready, after(it * IT + (c + 1)))
                    o = k.ps[:, 6 + c % 2, 0:8 * W].rearrange("p (h w) -> p h w", w=W)
                    dve.reciprocal(rsum[:, c % 2, :], o[:, :, d]).then_inc(inverse_done, 1)
                    dve.wait_ge(inverse_done, after(it * IT + (c + 1)))
                    dve.tensor_tensor(
                        O[:, half * NQ // 2:(half + 1) * NQ // 2, bass.ds(2 * it + u, 1), :].rearrange(
                            "p a t (h w) -> p (a t) h w", w=d),
                        o[:, :, 0:d].rearrange("p (a h) w -> p a h w", h=HB),
                        rsum[:, c % 2, :].rearrange("p (a h) -> p a h", h=HB).unsqueeze(3).to_broadcast(
                            [P, NQ // 2, HB, d]), ALU.mult).then_inc(o_done, 1)

                def before(b, it):
                    shift(it, 0)
                    shift(it, 1)

                def body(b, it, last):
                    for c in range(IT):
                        if c + 2 < IT or not last:
                            shift(it, c + 2)
                        if c:
                            normal(it, c - 1)
                    normal(it, IT - 1)

                each_pair(dve, before, body)



def out_project(nc, k, O, w, brow, add_to, also=None):
    NB = w.shape[0] // P
    with ExitStack() as held:
        sb = tiles(nc, held)
        ws = sb("ws", [P, NB, D])
        bs = sb("bs", [P, D])
        ot = sb("ot", [P, 2, NB * P])
        OT = sb("OT", [P, 2, NB * P])
        with stage(nc, "w_loaded", "b_loaded", "kept", "bias_added", "o_staged", "turned", "copied", "y_ready",
                   "y_added") as (
                block, w_loaded, b_loaded, kept, bias_added, o_staged, turned, copied, y_ready, y_added):
            @block.sync
            def _(sp):
                sp.dma_start(ws[:, :, :], w.rearrange("(c p) f -> p c f", p=P)).then_inc(w_loaded, 16)
                if brow is not None:
                    sp.dma_start(bs[:, :], brow.to_broadcast([P, D])).then_inc(b_loaded, 16)

            @block.gpsimd
            def _(pool):
                with pool.Fori(0, T // 2) as i:
                    for u in range(2):
                        t = 2 * i + u
                        pool.wait_ge(turned, after(2 * i + (u - 1)))
                        pool.tensor_copy(ot[:, u, :].rearrange("p (a n) -> p a n", n=P),
                                         O[:, :, bass.ds(t, 1), :].rearrange("p a t n -> p (a t) n")
                                         ).then_inc(o_staged, 1)
                        if also is not None:
                            pool.tensor_copy(also[:, t, :], add_to[:, t, :]).then_inc(kept, 1)

            @block.tensor
            def _(pe):
                def turn(i, u):
                    pe.wait_ge(o_staged, after(2 * i + (u + 1)))
                    pe.wait_ge(copied, after(2 * i + (u - 1)))
                    for c in range(NB):
                        mm = pe.transpose(k.ps[:, u, c * P:(c + 1) * P], ot[:, u, c * P:(c + 1) * P], k.ident[:, :])
                    mm.then_inc(turned, 1)

                def products(i, u):
                    pe.wait_ge(copied, after(2 * i + (u + 1)))
                    pe.wait_ge(y_added, after(2 * i + (u - 1)))
                    for c in range(NB):
                        mm = pe.matmul(k.ps[:, 2 + u, 0:D], OT[:, u, c * P:(c + 1) * P], ws[:, c, :],
                                       start=(c == 0), stop=(c == NB - 1))
                    mm.then_inc(y_ready, 1)

                for u in range(2):
                    turn(0, u)
                pe.wait_ge(w_loaded, after(16))
                with pe.Fori(0, T // 2 - 1) as i:
                    for u in range(2):
                        turn(i + 1, u)
                        products(i, u)
                for u in range(2):
                    products(T // 2 - 1, u)

            @block.scalar
            def _(act):
                with act.Fori(0, T // 2) as i:
                    for u in range(2):
                        act.wait_ge(turned, after(2 * i + (u + 1)))
                        act.wait_ge(y_ready, after(2 * i + (u - 1)))
                        act.activation(OT[:, u, :], k.ps[:, u, 0:NB * P], ACT.Copy).then_inc(copied, 1)

            @block.vector
            def _(dve):
                if brow is not None:
                    dve.wait_ge(b_loaded, after(16))
                with dve.Fori(0, T // 2) as i:
                    for u in range(2):
                        t = 2 * i + u
                        if also is not None:
                            dve.wait_ge(kept, after(2 * i + (u + 1)))
                        if brow is not None:
                            dve.tensor_tensor(add_to[:, t, :], add_to[:, t, :], bs[:, :],
                                              ALU.add).then_inc(bias_added, 1)
                            dve.wait_ge(bias_added, after(2 * i + (u + 1)))
                        dve.wait_ge(y_ready, after(2 * i + (u + 1)))
                        dve.tensor_tensor(add_to[:, t, :], k.ps[:, 2 + u, 0:D], add_to[:, t, :],
                                          ALU.add).then_inc(y_added, 1)
                        if also is not None:
                            dve.wait_ge(y_added, after(2 * i + (u + 1)))
                            dve.tensor_tensor(also[:, t, :], also[:, t, :], add_to[:, t, :], ALU.add)


def normalise_context(nc, k, gain, yT):
    with ExitStack() as held:
        sb = tiles(nc, held)
        norm = sb("norm", [P, 11, BATCH])
        cn = sb("cn", [P, BATCH, IMG])
        with stage(nc, "norm_step", "normed", "turned") as (block, norm_step, normed, turned):
            @block.vector
            def _(dve):
                row_norms(dve, Chain(dve, norm_step), k.ctx[0:CTX], norm[0:CTX], 0, BATCH)
                for b in range(BATCH):
                    dve.tensor_scalar(cn[0:CTX, b, :], k.ctx[0:CTX, b, :], mean_of(norm[0:CTX], b), rstd_of(norm[0:CTX], b),
                                      ALU.subtract, ALU.mult).then_inc(normed, 1)

            @block.tensor
            def _(pe):
                for b in range(BATCH):
                    pe.wait_ge(normed, after(b + 1))
                    pe.transpose(k.ps[:, b, 0:CTX], cn[0:CTX, b, :], k.ident[0:CTX, 0:CTX]).then_inc(turned, 1)

            @block.scalar
            def _(act):
                for b in range(BATCH):
                    act.wait_ge(turned, after(b + 1))
                    act.activation(yT[:, b, :], k.ps[:, b, 0:CTX], ACT.Identity, scale=gain[0], bias=gain[1])



def turned_weights(w):
    return w.rearrange("(c p) f -> p c f", p=P)


def row_of(v):
    return v.rearrange("(a n) -> a n", a=1)


def cross_layer(nc, k, d, src, add_to, also, wq, bq, wk, bk, wv, bvrow, wo, borow, gain, ctxT):
    W = 16 * d
    with ExitStack() as outer:
        O = tiles(nc, outer)("O", [P, W // P, T, P])
        with ExitStack() as held:
            sb = tiles(nc, held)
            QT = sb("QT", [P, W // P, TOK])
            with ExitStack() as front:
                wqs = tiles(nc, front)("wqs", [P, KD, W])
                project(nc, k, src, [gain], [(wqs, 0, QT, bq, 1.0)], [],
                        [(wqs[:, :, :], turned_weights(wq))])
            cross_attention(nc, k, d, ctxT, QT, O, wk, wv, bk, bvrow, float(d) ** -0.5)
        out_project(nc, k, O, wo, borow, add_to, also)


def layer0_attention(nc, k, a):
    cross_layer(nc, k, 16, k.x, k.x, None, a["L0_xattn_Wq"], k.col("L0_xattn_bq"), a["L0_xattn_Wk"],
                k.col("L0_xattn_bk"), a["L0_xattn_Wv"], row_of(a["L0_xattn_bv"]), a["L0_xattn_Wo"],
                row_of(a["L0_xattn_bo"]), None, k.ctxT)


def layer2_attention(nc, k, a):
    cross_layer(nc, k, 16, k.x, k.x, None, a["L2_xattn_Wq"], None, a["L2_xattn_Wk"],
                None, a["L2_xattn_Wv"], None, a["L2_xattn_Wo"], None, None, k.ctxT)



SH = 32
HG = P // SH


def self_attention(nc, k, QT, KT, V):
    QB = TB
    NB = BATCH * (16 // HG)
    QT = QT[:, :, :].rearrange("p a n -> p (a n)")
    KT = KT[:, :, :].rearrange("p a n -> p (a n)")
    V = V[:, :, :, :].rearrange("p a t n -> p (a t n)")
    UNITS = [(h, q) for h in range(HG) for q in range(QB)]
    NU = len(UNITS)
    HALF = QB // 2
    NW = HG * HALF
    wide_before = lambda n: n // QB * HALF + min(n % QB, HALF)
    LOAD = 16 * 8
    with ExitStack() as held:
        sb = tiles(nc, held)
        parts = sb("parts", [P, 4, SEQ])
        qst, kst = sb("qst", [P, 2, SEQ]), sb("kst", [P, 2, SEQ])
        pr = sb("pr", [P, 4, SEQ])
        pT = sb("pT", [P, 2, SEQ])
        neg = sb("neg", [P, 2])
        rs = sb("rs", [P, 4])
        inv = sb("inv", [P, 2])
        with stage(nc, "split_done", "even_stacked", "odd_stacked", "s_ready", "max_done", "exp_done", "masked",
                   "near_turned", "near_copied", "far_turned", "far_copied", "o_ready", "inverse_done", "o_done") as (
                block, split_done, even_stacked, odd_stacked, s_ready, max_done, exp_done, masked,
                near_turned, near_copied, far_turned, far_copied, o_ready, inverse_done, o_done):
            stacked = (even_stacked, odd_stacked)

            @block.sync
            def _(sp):
                def stack(it, h):
                    r = slice(SH * (h % HG), SH * (h % HG + 1))
                    for m, (qpart, kpart) in enumerate(((0, 2), (1, 2), (0, 3), (1, 3))):
                        to = slice(SH * m, SH * (m + 1))
                        sp.dma_start(qst[to, h % 2, :], parts[r, qpart, :]).then_inc(stacked[h % 2], 16)
                        sp.dma_start(kst[to, h % 2, :], parts[r, kpart, :]).then_inc(stacked[h % 2], 16)

                sp.wait_ge(split_done, after(4))
                stack(0, 0)
                stack(0, 1)
                with sp.Fori(0, NB - 1) as it:
                    for h in range(2, HG + 2):
                        sp.wait_ge(max_done, after(it * NU + QB * (h - 1)))
                        stack(it, h)
                for h in range(2, HG):
                    sp.wait_ge(s_ready, after((NB - 1) * NU + QB * (h - 1)))
                    stack(NB - 1, h)

            @block.gpsimd
            def _(pool):
                with pool.Fori(0, NB) as it:
                    for n, (h, q) in enumerate(UNITS):
                        pool.wait_ge(exp_done, after(it * NU + (n + 1)))
                        own = pr[:, n % 4, q * P:(q + 1) * P]
                        pool.tensor_tensor(own, own, k.upper[:, :], ALU.mult).then_inc(masked, 1)

            @block.tensor
            def _(pe):
                def scores(it, n):
                    h, q = UNITS[n % NU]
                    if q == 0:
                        pe.wait_ge(stacked[h % 2], after(LOAD * 2 * it + LOAD * (n // QB // 2 + 1)))
                    pe.wait_ge(exp_done, after(it * NU + (n - 1)))
                    for j in range(2):
                        mm = pe.matmul(k.ps[:, 2 * (n % 2) + j, :], qst[:, h % 2, q * P:(q + 1) * P].bitcast(F32R),
                                       kst[:, h % 2, j * 512:(j + 1) * 512].bitcast(F32R), start=True, stop=True)
                    mm.then_inc(s_ready, 1)

                def turn(it, n):
                    q = UNITS[n][1]
                    pe.wait_ge(masked, after(it * NU + (n + 1)))
                    pe.wait_ge(near_copied, after(it * NU + n))
                    for c in range(q, min(q + HALF, QB)):
                        mm = pe.transpose(k.ps[:, 4, (c - q) * P:(c - q + 1) * P], pr[:, n % 4, c * P:(c + 1) * P],
                                          k.ident[:, :])
                    mm.then_inc(near_turned, 1)
                    if q < HALF:
                        pe.wait_ge(far_copied, after(it * NW + wide_before(n)))
                        for c in range(q + HALF, QB):
                            mm = pe.transpose(k.ps[:, 5, (c - q - HALF) * P:(c - q - HALF + 1) * P],
                                              pr[:, n % 4, c * P:(c + 1) * P], k.ident[:, :])
                        mm.then_inc(far_turned, 1)

                def values(it, n):
                    h, q = UNITS[n]
                    pe.wait_ge(near_copied, after(it * NU + (n + 1)))
                    if q < HALF:
                        pe.wait_ge(far_copied, after(it * NW + wide_before(n + 1)))
                    pe.wait_ge(o_done, after(it * NU + (n - 1)))
                    for c in range(q, QB):
                        mm = pe.matmul(k.ps[:, 6 + n % 2, 0:SH], pT[:, n % 2, (c - q) * P:(c - q + 1) * P],
                                       V[:, bass.ds((it * QB + c) * P + h * SH, SH)], start=(c == q), stop=(c == QB - 1))
                    mm.then_inc(o_ready, 1)

                def units(it, last):
                    for n in range(NU):
                        if n + 2 < NU or not last:
                            scores(it, n + 2)
                        turn(it, n)
                        if n:
                            values(it, n - 1)
                    values(it, NU - 1)

                scores(0, 0)
                scores(0, 1)
                with pe.Fori(0, NB - 1) as it:
                    units(it, False)
                units(NB - 1, True)

            @block.scalar
            def _(act):
                def exps(it, n):
                    act.wait_ge(max_done, after(it * NU + (n + 1)))
                    act.wait_ge(o_done, after(it * NU + (n - 3)))
                    act.activation(pr[:, n % 4, :], k.ps[:, 2 * (n % 2):2 * (n % 2) + 2, :].rearrange("p a n -> p (a n)"),
                                   ACT.Exp, bias=neg[:, n % 2:n % 2 + 1],
                                   accum_out=rs[:, n % 4:n % 4 + 1]).then_inc(exp_done, 1)

                def copy_near(it, n):
                    near = min(HALF, QB - UNITS[n][1]) * P
                    act.wait_ge(o_ready, after(it * NU + (n - 1)))
                    act.wait_ge(near_turned, after(it * NU + (n + 1)))
                    act.activation(pT[:, n % 2, 0:near], k.ps[:, 4, 0:near], ACT.Copy).then_inc(near_copied, 1)

                def units(it, last):
                    for n in range(NU):
                        if n + 1 < NU or not last:
                            exps(it, n + 1)
                        copy_near(it, n)

                exps(0, 0)
                with act.Fori(0, NB - 1) as it:
                    units(it, False)
                units(NB - 1, True)

            @block.vector
            def _(dve):
                def split(it):
                    for j, src in ((0, QT), (2, KT)):
                        dve.tensor_scalar(parts[:, j, :].bitcast(I32), src[:, bass.ds(it * SEQ, SEQ)].bitcast(I32),
                                          HIGH_PART, None, ALU.bitwise_and).then_inc(split_done, 1)
                    dve.wait_ge(split_done, after(4 * it + 2))
                    for j, src in ((1, QT), (3, KT)):
                        dve.tensor_tensor(parts[:, j, :], src[:, bass.ds(it * SEQ, SEQ)], parts[:, j - 1, :],
                                          ALU.subtract).then_inc(split_done, 1)

                def maxima(it, n):
                    dve.wait_ge(s_ready, after(it * NU + (n + 1)))
                    dve.tensor_reduce(neg[:, n % 2:n % 2 + 1], k.ps[:, 2 * (n % 2):2 * (n % 2) + 2, :], AX.XY,
                                      ALU.max, negate=True).then_inc(max_done, 1)

                def copy_far(it, n):
                    near, far = HALF * P, (HALF - UNITS[n][1]) * P
                    dve.wait_ge(o_ready, after(it * NU + (n - 1)))
                    dve.wait_ge(far_turned, after(it * NW + wide_before(n + 1)))
                    dve.tensor_copy(pT[:, n % 2, near:near + far], k.ps[:, 5, 0:far]).then_inc(far_copied, 1)

                def normal(it, n):
                    h, q = UNITS[n]
                    dve.wait_ge(o_ready, after(it * NU + (n + 1)))
                    dve.reciprocal(inv[:, n % 2:n % 2 + 1], rs[:, n % 4:n % 4 + 1]).then_inc(inverse_done, 1)
                    dve.wait_ge(inverse_done, after(it * NU + (n + 1)))
                    dve.tensor_scalar(QT[:, bass.ds((it * QB + q) * P + h * SH, SH)], k.ps[:, 6 + n % 2, 0:SH],
                                      inv[:, n % 2:n % 2 + 1], None, ALU.mult).then_inc(o_done, 1)

                def units(it, last):
                    for n in range(NU):
                        if n == NU - QB - HALF and not last:
                            for s in stacked:
                                dve.wait_ge(s, after(LOAD * 2 * it + LOAD * 2))
                            split(it + 1)
                        if n + 2 < NU or not last:
                            maxima(it, n + 2)
                        if UNITS[n][1] < HALF:
                            copy_far(it, n)
                        if n:
                            normal(it, n - 1)
                    normal(it, NU - 1)

                split(0)
                maxima(0, 0)
                maxima(0, 1)
                with dve.Fori(0, NB - 1) as it:
                    units(it, False)
                units(NB - 1, True)


def layer1_attention(nc, k, a):
    with ExitStack() as held:
        sb = tiles(nc, held)
        y = sb("y_rows", [P, T, D])
        base = sb("base_rows", [P, T, D])
        layer_norm_rows(nc, k, k.x, y, None)
        layer_norm_rows(nc, k, y, y, ("L1_xattn_ln1_g", "L1_xattn_ln1_b"), a)
        A = "L1_xattn_a1_"
        with ExitStack() as outer:
            QT = tiles(nc, outer)("QT", [P, 4, TOK])
            with ExitStack() as inner:
                sb2 = tiles(nc, inner)
                KT, V = sb2("KT", [P, 4, TOK]), sb2("V", [P, 4, T, P])
                with ExitStack() as front:
                    sb3 = tiles(nc, front)
                    ws = [sb3(f"w{n}", [P, KD, 512]) for n in "qkv"]
                    project(nc, k, y,
                            [(k.col(A + "lnx_g"), k.col(A + "lnx_b")), (k.col(A + "lny_g"), k.col(A + "lny_b"))],
                            [(ws[0], 0, QT, None, float(SH) ** -0.5), (ws[1], 1, KT, None, 1.0)], [(ws[2], 1, V)],
                            [(w[:, :, :], turned_weights(a[A + n])) for w, n in zip(ws, ("wq", "wk", "wv"))])
                self_attention(nc, k, QT, KT, V)
            O = QT[:, :, :].rearrange("p a (t n) -> p a t n", n=P)
            out_project(nc, k, O, a[A + "li1_w"], row_of(a[A + "li1_b"]), y, base)
        ffn(nc, k, y, base, a[A + "li2_w"], a[A + "li3_w"], (k.col(A + "ln3_g"), k.col(A + "ln3_b")),
            k.col(A + "li2_b"), row_of(a[A + "li3_b"]))
        layer_norm_rows(nc, k, base, y, ("L1_xattn_ln2_g", "L1_xattn_ln2_b"), a)
        A = "L1_xattn_a2_"
        yT = sb("yT", [P, BATCH, CTX])
        normalise_context(nc, k, (k.col(A + "lny_g"), k.col(A + "lny_b")), yT)
        cross_layer(nc, k, 32, y, y, base, a[A + "wq"], None, a[A + "wk"], None, a[A + "wv"], None,
                    a[A + "li1_w"], row_of(a[A + "li1_b"]), (k.col(A + "lnx_g"), k.col(A + "lnx_b")), yT)
        ffn(nc, k, y, base, a[A + "li2_w"], a[A + "li3_w"], (k.col(A + "ln3_g"), k.col(A + "ln3_b")),
            k.col(A + "li2_b"), row_of(a[A + "li3_b"]))
        add_rows(nc, k, base)


def add_rows(nc, k, rows):
    with stage(nc) as (block,):
        @block.vector
        def _(dve):
            dve.tensor_tensor(k.x[:, :, :], k.x[:, :, :], rows[:, :, :], ALU.add)


def layer_norm_rows(nc, k, src, dst, gain, a=None, keep=None):
    with ExitStack() as held:
        sb = tiles(nc, held)
        norm = sb("norm", [P, 11, T])
        gb = sb("gb", [P, 2, D])
        part = sb("part", [P, GT, D])
        with stage(nc, "gain_loaded", "norm_step", "scaled", "src_kept") as (
                block, gain_loaded, norm_step, scaled, src_kept):
            @block.sync
            def _(sp):
                if keep is not None:
                    sp.dma_start(keep, src[:, :, :].rearrange("p t d -> p (t d)")).then_inc(src_kept, 16)
                    sp.wait_ge(src_kept, after(16))
                if gain is not None:
                    for j, n in enumerate(gain):
                        sp.dma_start(gb[:, j, :], row_of(a[n]).to_broadcast([P, D])).then_inc(gain_loaded, 16)
                    sp.wait_ge(gain_loaded, after(32))

            @block.vector
            def _(dve):
                step = Chain(dve, norm_step)
                row_norms(dve, step, src, norm, 0, T)
                if gain is not None:
                    dve.wait_ge(gain_loaded, after(32))
                for g in range(G):
                    for u in range(GT):
                        t = g * GT + u
                        if gain is None:
                            dve.tensor_scalar(dst[:, t, :], src[:, t, :], mean_of(norm, t), rstd_of(norm, t),
                                              ALU.subtract, ALU.mult)
                        else:
                            ins = dve.scalar_tensor_tensor(out=part[:, u, :], in0=src[:, t, :], scalar=mean_of(norm, t),
                                                           in1=gb[:, 0, :], op0=ALU.subtract, op1=ALU.mult)
                    if gain is not None:
                        ins.then_inc(scaled, 1)
                        dve.wait_ge(scaled, after(g + 1))
                        for u in range(GT):
                            t = g * GT + u
                            ins = dve.scalar_tensor_tensor(out=dst[:, t, :], in0=part[:, u, :], scalar=rstd_of(norm, t),
                                                           in1=gb[:, 1, :], op0=ALU.mult, op1=ALU.add)
                        step(ins)



def layer3_attention(nc, k, a):
    with ExitStack() as held:
        sb = tiles(nc, held)
        QT = sb("QT", [P, KD, TOK])
        KT = sb("KT", [P, KD, BATCH, CTX])
        V = sb("V", [P, BATCH, D])
        with ExitStack() as front:
            sb2 = tiles(nc, front)
            wqs, wks, wvs, bvs = sb2("wqs", [P, KD, D]), sb2("wks", [P, D]), sb2("wvs", [P, D]), sb2("bvs", [1, D])
            project(nc, k, k.x, [None], [(wqs, 0, QT, k.col("L3_xattn_bq"), 1.0)], [],
                    [(wqs[:, :, :], turned_weights(a["L3_xattn_Wq"]))])
            with stage(nc, "wk_loaded", "wv_loaded", "k_ready", "v_ready") as (
                    block, wk_loaded, wv_loaded, k_ready, v_ready):
                @block.sync
                def _(sp):
                    sp.dma_start(wks[:, :], a["L3_xattn_Wk"]).then_inc(wk_loaded, 16)
                    sp.dma_start(wvs[:, :], a["L3_xattn_Wv"]).then_inc(wv_loaded, 16)
                    sp.dma_start(bvs[:, :], row_of(a["L3_xattn_bv"])).then_inc(wv_loaded, 16)

                @block.tensor
                def _(pe):
                    pe.wait_ge(wk_loaded, after(16))
                    for b in range(BATCH):
                        for c in range(KD):
                            pe.matmul(k.ps[:, KD * b + c, 0:CTX], wks[:, c * P:(c + 1) * P], k.ctxT[:, b, :],
                                      start=True, stop=True).then_inc(k_ready, 1)
                    pe.wait_ge(wv_loaded, after(32))
                    for b in range(BATCH):
                        pe.matmul(k.ps[0:CTX, 4 + b, 0:D], k.ctxT[:, b, :], wvs[:, :], start=True, stop=False)
                        pe.matmul(k.ps[0:CTX, 4 + b, 0:D], k.ones[0:1, 0:CTX], bvs[:, :], start=False,
                                  stop=True).then_inc(v_ready, 1)

                @block.vector
                def _(dve):
                    bk = k.col("L3_xattn_bk")
                    for b in range(BATCH):
                        for c in range(KD):
                            dve.wait_ge(k_ready, after(KD * b + c + 1))
                            dve.tensor_scalar(KT[:, c, b, :], k.ps[:, KD * b + c, 0:CTX], bk[:, c:c + 1], None, ALU.add)
                    for b in range(BATCH):
                        dve.wait_ge(v_ready, after(b + 1))
                        dve.tensor_copy(V[0:CTX, b, :], k.ps[0:CTX, 4 + b, 0:D])

        qs = sb("qs", [P, 2, KD, P])
        pr = sb("pr", [P, 2, CTX])
        pT = sb("pT", [P, 2, P])
        neg, rs, inv = sb("neg", [P, 2]), sb("rs", [P, T]), sb("inv", [P, 2])
        with stage(nc, "q_staged", "s_ready", "max_done", "exp_done", "pt_ready", "pt_copied", "o_ready",
                   "inverse_done", "o_done") as (
                block, q_staged, s_ready, max_done, exp_done, pt_ready, pt_copied, o_ready, inverse_done, o_done):
            @block.gpsimd
            def _(pool):
                with pool.Fori(0, T // 2) as i:
                    for u in range(2):
                        pool.wait_ge(s_ready, after(2 * i + (u - 1)))
                        pool.tensor_copy(qs[:, u, :, :], QT[:, :, bass.ds((2 * i + u) * P, P)]).then_inc(q_staged, 1)

            @block.tensor
            def _(pe):
                def scores(b, i):
                    for u in range(2):
                        pe.wait_ge(q_staged, after(2 * i + (u + 1)))
                        pe.wait_ge(exp_done, after(2 * i + (u - 1)))
                        for c in range(KD):
                            mm = pe.matmul(k.ps[:, u, 0:CTX], qs[:, u, c, :], KT[:, c, b, :],
                                           start=(c == 0), stop=(c == KD - 1))
                        mm.then_inc(s_ready, 1)

                def body(b, i, last):
                    if not last:
                        scores(b, i + 1)
                    for u in range(2):
                        pe.wait_ge(exp_done, after(2 * i + (u + 1)))
                        pe.wait_ge(pt_copied, after(2 * i + (u - 1)))
                        pe.transpose(k.ps[0:CTX, 2 + u, 0:P], pr[:, u, :], k.ident[:, :]).then_inc(pt_ready, 1)
                    for u in range(2):
                        pe.wait_ge(pt_copied, after(2 * i + (u + 1)))
                        pe.wait_ge(o_done, after(2 * i + (u - 1)))
                        pe.matmul(k.ps[:, 4 + u, 0:D], pT[0:CTX, u, :], V[0:CTX, b, :],
                                  start=True, stop=True).then_inc(o_ready, 1)

                each_pair(pe, scores, body)

            @block.scalar
            def _(act):
                def exponentials(i):
                    for u in range(2):
                        act.wait_ge(max_done, after(2 * i + (u + 1)))
                        act.wait_ge(pt_ready, after(2 * i + (u - 1)))
                        act.activation(pr[:, u, :], k.ps[:, u, 0:CTX], ACT.Exp, bias=neg[:, u:u + 1],
                                       accum_out=rs[:, bass.ds(2 * i + u, 1)]).then_inc(exp_done, 1)

                def copies(i):
                    for u in range(2):
                        act.wait_ge(pt_ready, after(2 * i + (u + 1)))
                        act.wait_ge(o_ready, after(2 * i + (u - 1)))
                        act.activation(pT[0:CTX, u, :], k.ps[0:CTX, 2 + u, 0:P], ACT.Copy).then_inc(pt_copied, 1)

                exponentials(0)
                with act.Fori(0, T // 2 - 1) as i:
                    copies(i)
                    exponentials(i + 1)
                copies(T // 2 - 1)

            @block.vector
            def _(dve):
                def maxima(i):
                    for u in range(2):
                        dve.wait_ge(s_ready, after(2 * i + (u + 1)))
                        dve.tensor_reduce(neg[:, u:u + 1], k.ps[:, u, 0:CTX], AX.X, ALU.max,
                                          negate=True).then_inc(max_done, 1)

                def sums(i):
                    for u in range(2):
                        dve.wait_ge(o_ready, after(2 * i + (u + 1)))
                        dve.reciprocal(inv[:, u:u + 1], rs[:, bass.ds(2 * i + u, 1)]).then_inc(inverse_done, 1)
                        dve.wait_ge(inverse_done, after(2 * i + (u + 1)))
                        row = k.x[:, 2 * i + u, :]
                        dve.scalar_tensor_tensor(out=row, in0=k.ps[:, 4 + u, 0:D], scalar=inv[:, u:u + 1], in1=row,
                                                 op0=ALU.mult, op1=ALU.add).then_inc(o_done, 1)

                maxima(0)
                with dve.Fori(0, T // 2 - 1) as i:
                    maxima(i + 1)
                    sums(i)
                sums(T // 2 - 1)



LH = 8
LD = 64
LW = LH * LD


HALF = D // 2


def keep_halves(dve, x, h):
    for b in range(BATCH):
        dve.memset(h[0:1, b * TB, HALF:D], 0.0)
    dve.tensor_copy(h[:, :, 0:HALF], x[:, :, 0:HALF])


def move_halves(sp, x, h, moved):
    sp.dma_start(h[1:P, :, HALF:D], x[0:P - 1, :, HALF:D]).then_inc(moved, 16)
    for b in range(BATCH):
        sp.dma_start(h[0:1, b * TB + 1:(b + 1) * TB, HALF:D],
                     x[P - 1:P, b * TB:(b + 1) * TB - 1, HALF:D]).then_inc(moved, 16)


def shift_rows(nc, k, x, h):
    with stage(nc, "moved") as (block, moved):
        @block.vector
        def _(dve):
            keep_halves(dve, x, h)

        @block.sync
        def _(sp):
            move_halves(sp, x, h, moved)
            sp.wait_ge(moved, after(16 * (1 + BATCH)))


def build_mask(pool, step, mask, ident16, ident):
    step(pool.memset(mask[:, :, :, :], 0.0))
    for j in range(2):
        m = mask[:, 0, j, 0:P]
        step(pool.affine_select(out=m, in_=m, compare_op=ALU.is_ge, fill=NEG, base=0,
                                pattern=[[1, P]], channel_multiplier=-1))
        m = mask[:, :, j, P:2 * P]
        step(pool.affine_select(out=m, in_=m, compare_op=ALU.is_ge, fill=NEG, base=0,
                                pattern=[[0, 2], [-1, P]], channel_multiplier=1))
        step(pool.memset(mask[:, 1, j, 0:P], NEG))
    pool.tensor_copy(ident16[:, :], ident)


def local_qkv(nc, k, a, layer, y, h, ws, bb, ab, QT, KT, V, mask, ident16):
    with ExitStack() as held:
        sb = tiles(nc, held)
        cosT = sb("cosT", [P, TB, 2, LD])
        sinT = sb("sinT", [P, TB, 2, LD])
        qks = sb("qks", [P, 2, LD])
        qkw = sb("qkw", [P, 2, LD])
        with stage(nc, "tables_loaded", "moved", "mask_step") as (block, tables_loaded, moved, mask_step):
            @block.gpsimd
            def _(pool):
                build_mask(pool, Chain(pool, mask_step), mask, ident16, k.ident[:, :])

            @block.scalar
            def _(act):
                move_halves(act, y, h, moved)
                act.wait_ge(moved, after(16 * (1 + BATCH)))

            @block.sync
            def _(sp):
                sp.dma_start(cosT[:, :, :, :], a["rotary_cos"]).then_inc(tables_loaded, 16)
                sp.dma_start(sinT[:, :, :, :], a["rotary_sin"]).then_inc(tables_loaded, 16)
                for j, n in enumerate(("L2_ffn_q_scale", "L2_ffn_k_scale")):
                    v = a[n][layer:layer + 1, :]
                    sp.dma_start(qks[:, j, :], v.to_broadcast([P, LD])).then_inc(tables_loaded, 16)
                    for m in range(2):
                        sp.dma_start(qkw[:, j, m * LD // 2:(m + 1) * LD // 2],
                                     v[:, (1 - m) * LD // 2:(2 - m) * LD // 2].to_broadcast([P, LD // 2])
                                     ).then_inc(tables_loaded, 16)
                sp.wait_ge(tables_loaded, after(16 * 8))

            @block.vector
            def _(dve):
                keep_halves(dve, y, h)
                dve.memset(KT[:, :, 0:P], 0.0)
                dve.memset(V[:, :, 0, :], 0.0)
                dve.wait_ge(tables_loaded, after(16 * 8))
                for tab, sc in ((cosT, qks), (sinT, qkw)):
                    dve.tensor_tensor(tab[:, :, :, :], tab[:, :, :, :],
                                      sc[:, :, :].unsqueeze(1).to_broadcast([P, TB, 2, LD]), ALU.mult)

        xn = sb("xn", [P, GT, D])
        xT = sb("xT", [P, KD, GN])
        sq = sb("sq", [P, 2 * LH, LD])
        qk = sb("qk", [P, 2, 2, LW])
        ss = sb("ss", [P, 2, 2 * LH])
        root = sb("root", [P, 2, 2 * LH])
        rn = sb("rn", [P, 2, 2 * LH])
        psT = k.ps[:, 0:2, :]
        CH = 6
        heads = lambda ap: ap.rearrange("p b (h w) -> p b h w", w=LD)
        with stage(nc, "w_loaded", "normed", "turned", "copied", "qk_ready", "qk_out", "v_ready", "v_out", "squared",
                   "products", "summed", "ss_ready", "root_ready", "chain", "rotated", "qkt_ready", "qkt_out") as (
                block, w_loaded, normed, turned, copied, qk_ready, qk_out, v_ready, v_out, squared,
                products, summed, ss_ready, root_ready, chain, rotated, qkt_ready, qkt_out):
            @block.sync
            def _(sp):
                sp.dma_start(ws[:, :, :], turned_weights(a["L2_ffn_wqkv"][layer])).then_inc(w_loaded, 16)

            def each_tile(eng, group, tile, lagging):
                def body(g, first, last):
                    for u in range(GT):
                        tile(g, u)
                        if u == GT - 1 and not last:
                            group(g + 1)
                        if u >= 2 or not first:
                            lagging(g, u - 2)
                group(0)
                body(0, True, False)
                with eng.Fori(1, G - 1) as g:
                    body(g, False, False)
                body(G - 1, False, True)
                lagging(G - 1, GT - 2)
                lagging(G - 1, GT - 1)

            @block.tensor
            def _(pe):
                def group(g):
                    turn_group(pe, g, k, xn, psT, normed, turned, copied, 1)

                def tile(g, u):
                    if u == 0:
                        pe.wait_ge(w_loaded, after(16))
                        pe.wait_ge(copied, after((g + 1) * 2))
                    pe.wait_ge(qk_out, after(g * GT + (u - 1)))
                    for j in range(3):
                        if j == 2:
                            pe.wait_ge(v_out, after(g * GT + u))
                        out = k.ps[:, 6, :] if j == 2 else k.ps[:, 2 + 2 * (u % 2) + j, :]
                        for c in range(KD):
                            mm = pe.matmul(out, xT[:, c, u * P:(u + 1) * P], ws[:, c, j * LW:(j + 1) * LW],
                                           start=(c == 0), stop=(c == KD - 1))
                        if j:
                            mm.then_inc(qk_ready if j == 1 else v_ready, 1)

                def turn_qk(g, u):
                    for j in range(2):
                        pe.wait_ge(rotated, after(g * GT + (u + 1)))
                        pe.wait_ge(qkt_out, after(g * 2 * GT + (2 * u + j)))
                        flat = ab[:, u % 4, :, :].rearrange("p h w -> p (h w)")
                        for c in range(4):
                            mm = pe.transpose(k.ps[:, 7, c * P:(c + 1) * P],
                                              flat[:, (4 * j + c) * P:(4 * j + c + 1) * P], k.ident[:, :])
                        mm.then_inc(qkt_ready, 1)

                each_tile(pe, group, tile, turn_qk)

            @block.scalar
            def _(act):
                def group(g):
                    copy_group(act, g, [xT], psT, [None], turned, copied, v_ready, GT)

                def roots(g, u):
                    act.wait_ge(ss_ready, after(g * GT + (u + 1)))
                    act.activation(root[:, u % 2, :], ss[:, u % 2, :], ACT.Sqrt).then_inc(root_ready, 1)

                def tile(g, u):
                    act.wait_ge(qk_ready, after(g * GT + (u + 1)))
                    act.wait_ge(products, after(g * GT + (u - 1)))
                    act.activation(qk[:, u % 2, :, :], k.ps[:, 2 + 2 * (u % 2):4 + 2 * (u % 2), :],
                                   ACT.Copy).then_inc(qk_out, 1)
                    act.wait_ge(qk_out, after(g * GT + (u + 1)))
                    act.wait_ge(ss_ready, after(g * GT + u))
                    act.activation(sq[:, :, :].rearrange("p h w -> p (h w)"),
                                   qk[:, u % 2, :, :].rearrange("p b n -> p (b n)"), ACT.Square).then_inc(squared, 1)
                    if u or not (isinstance(g, int) and g == 0):
                        roots(g, u - 1)
                    act.wait_ge(v_ready, after(g * GT + (u + 1)))
                    act.activation(V[:, :, bass.ds(g * GT + u + 1, 1), :].rearrange("p a t n -> p (a t) n"),
                                   k.ps[:, 6, :].rearrange("p (a n) -> p a n", a=4), ACT.Copy).then_inc(v_out, 1)

                def copy_qk(g, u):
                    if isinstance(g, int) and (g, u) == (G - 1, GT - 2):
                        roots(G - 1, GT - 1)
                    for j, dst in enumerate((QT, KT)):
                        act.wait_ge(qkt_ready, after(g * 2 * GT + (2 * u + j + 1)))
                        at = (g * GT + u + 1) * P
                        act.activation(dst[:, :, bass.ds(at, P)], k.ps[:, 7, :].rearrange("p (c n) -> p c n", c=4),
                                       ACT.Copy).then_inc(qkt_out, 1)

                each_tile(act, group, tile, copy_qk)

            @block.vector
            def _(dve):
                H = LD // 2
                two = lambda ap: ap.rearrange("p (b h) w -> p b h w", b=2)

                def rotate(t):
                    i = t % TB
                    A, B = ab[:, t % 4, :, :], bb[:, :, :]
                    dve.wait_ge(qk_out, after(t + 1))
                    dve.wait_ge(qkt_ready, after(2 * (t - 3)))
                    dve.wait_ge(summed, after(t))
                    dve.tensor_tensor(two(A), heads(qk[:, t % 2, :, :]),
                                      cosT[:, i, :, :].unsqueeze(2).to_broadcast([P, 2, LH, LD]), ALU.mult)
                    for m in range(2):
                        ins = dve.tensor_tensor(
                            two(B)[:, :, :, m * H:(m + 1) * H], heads(qk[:, t % 2, :, :])[:, :, :, (1 - m) * H:(2 - m) * H],
                            sinT[:, i, :, m * H:(m + 1) * H].unsqueeze(2).to_broadcast([P, 2, LH, H]), ALU.mult)
                    ins.then_inc(products, 1)
                    dve.wait_ge(squared, after(t + 1))
                    dve.tensor_reduce(ss[:, t % 2, :], sq[:, :, :], AX.X, ALU.add).then_inc(ss_ready, 1)

                def scale(t):
                    A, s, m = ab[:, t % 4, :, :], ss[:, t % 2, :], root[:, t % 2, :]
                    dve.wait_ge(root_ready, after(t + 1))
                    step = Chain(dve, chain, t * CH)
                    r0, r1 = rn[:, 0, :], rn[:, 1, :]
                    step(dve.tensor_scalar(m, m, 1e-12, None, ALU.max))
                    step(dve.reciprocal(r0, m))
                    step(dve.tensor_tensor(r0, r0, s, ALU.mult))
                    step(dve.tensor_tensor(r0, r0, m, ALU.add))
                    step(dve.tensor_scalar(r0, r0, 0.5, 1e-12, ALU.mult, ALU.max))
                    step(dve.reciprocal(r1, r0))
                    assert step.n == CH
                    dve.wait_ge(summed, after(t + 1))
                    dve.tensor_tensor(A, A, r1.unsqueeze(2).to_broadcast([P, 2 * LH, LD]), ALU.mult).then_inc(rotated, 1)

                normalise_group(dve, 0, xn, h, None, turned, normed)
                for t in range(T):
                    rotate(t)
                    if t:
                        scale(t - 1)
                    if t % GT == 1 and t // GT + 1 < G:
                        normalise_group(dve, t // GT + 1, xn, h, None, turned, normed)
                scale(T - 1)

            @block.gpsimd
            def _(pool):
                with pool.Fori(0, G) as g:
                    for u in range(GT):
                        pool.wait_ge(products, after(g * GT + (u + 1)))
                        A, B = ab[:, u % 4, :, :], bb[:, :, :]
                        pool.tensor_tensor(A, A, B, ALU.add).then_inc(summed, 1)


def local_attention(nc, k, QT, KT, V, O, mask, ident16):
    HB = P // LD
    with ExitStack() as held:
        sb = tiles(nc, held)
        qz = sb("qz", [P, 2, 4, HB, P])
        pr = sb("pr", [P, 2, 4, 2 * P])
        pT = sb("pT", [P, 2, 8, P])
        neg, rs, inv = sb("neg", [P, 4, 4]), sb("rs", [P, 4, 4]), sb("inv", [P, 2, 4])
        with stage(nc) as (block,):
            @block.vector
            def _(dve):
                dve.memset(qz[:, 0, :, :, :], 0.0)

            @block.gpsimd
            def _(pool):
                pool.memset(qz[:, 1, :, :, :], 0.0)
        N4 = 4
        with stage(nc, "q_staged", "s_ready", "max_done", "exp_done", "near_turned", "near_copied", "far_turned",
                   "far_copied", "o_ready", "inverse_done", "o_done") as (
                block, q_staged, s_ready, max_done, exp_done, near_turned, near_copied, far_turned,
                far_copied, o_ready, inverse_done, o_done):
            @block.gpsimd
            def _(pool):
                with pool.Fori(0, T // 2) as i:
                    for u in range(2):
                        pool.wait_ge(s_ready, after(i * N4 + (2 * u - 2)))
                        for e in range(HB):
                            r = slice(e * LD, (e + 1) * LD)
                            pool.tensor_copy(qz[r, u, :, e, :], QT[r, :, bass.ds((2 * i + u + 1) * P, P)]
                                             ).then_inc(q_staged, 1)
                            pool.wait_ge(q_staged, after(2 * HB * i + (HB * u + e + 1)))

            @block.tensor
            def _(pe):
                def scores(i, c, first=False):
                    u, half = c // 2 % 2, c % 2
                    pe.wait_ge(q_staged, after(2 * HB * i + HB * (c // 2 + 1)))
                    pe.wait_ge(exp_done, after(i * N4 + (c - 1)))
                    for m in range(2):
                        bank = k.ps[:, 2 * (c % 2) + m, :]
                        pe.matmul(bank, ident16[:, :], mask[:, int(first), :, :].rearrange("p b n -> p (b n)"),
                                  start=True, stop=False)
                        for e in range(HB):
                            blk = 2 * half + m
                            mm = pe.matmul(bank[:, e * 2 * P:(e + 1) * 2 * P], qz[:, u, blk, e, :],
                                           KT[:, blk, bass.ds((2 * i + c // 2) * P, 2 * P)], start=False, stop=(e == 1))
                    mm.then_inc(s_ready, 1)

                def turn(i, c):
                    pe.wait_ge(exp_done, after(i * N4 + (c + 1)))
                    flat = pr[:, c % 2, :, :].rearrange("p h n -> p (h n)")
                    for bank, out, turned in ((4, near_copied, near_turned), (5, far_copied, far_turned)):
                        pe.wait_ge(out, after(i * N4 + c))
                        for m in range(4):
                            at = ((bank - 4) * 4 + m) * P
                            mm = pe.transpose(k.ps[:, bank, m * P:(m + 1) * P], flat[:, at:at + P], k.ident[:, :])
                        mm.then_inc(turned, 1)

                def values(i, c):
                    u, half = c // 2, c % 2
                    pe.wait_ge(near_copied, after(i * N4 + (c + 1)))
                    pe.wait_ge(far_copied, after(i * N4 + (c + 1)))
                    pe.wait_ge(o_done, after(i * N4 + (c - 1)))
                    for hh in range(4):
                        h = 4 * half + hh
                        for w in range(2):
                            mm = pe.matmul(k.ps[:, 6 + c % 2, hh * LD:(hh + 1) * LD], pT[:, c % 2, 2 * hh + w, :],
                                           V[:, h // HB, bass.ds(2 * i + u + w, 1), h % HB * LD:(h % HB + 1) * LD].rearrange(
                                               "p t n -> p (t n)"), start=(w == 0), stop=(w == 1))
                    mm.then_inc(o_ready, 1)

                def before(b, i):
                    scores(i, 0, first=True)
                    scores(i, 1, first=True)

                def body(b, i, last):
                    for c in range(N4):
                        if c + 2 < N4 or not last:
                            scores(i, c + 2)
                        turn(i, c)
                        if c:
                            values(i, c - 1)
                    values(i, N4 - 1)

                each_pair(pe, before, body)

            @block.scalar
            def _(act):
                def exps(i, c):
                    act.wait_ge(max_done, after(i * N4 + (c + 1)))
                    act.wait_ge(far_turned, after(i * N4 + (c - 1)))
                    act.wait_ge(o_done, after(i * N4 + (c - 3)))
                    for hh in range(4):
                        ins = act.activation(pr[:, c % 2, hh, :], k.ps[:, 2 * (c % 2) + hh // 2,
                                                                     hh % 2 * 2 * P:(hh % 2 + 1) * 2 * P],
                                             ACT.Exp, bias=neg[:, c % 4, hh:hh + 1], accum_out=rs[:, c % 4, hh:hh + 1])
                    ins.then_inc(exp_done, 1)

                def copy_near(i, c):
                    act.wait_ge(near_turned, after(i * N4 + (c + 1)))
                    act.wait_ge(o_ready, after(i * N4 + (c - 1)))
                    act.activation(pT[:, c % 2, 0:4, :].rearrange("p a n -> p (a n)"), k.ps[:, 4, :],
                                   ACT.Copy).then_inc(near_copied, 1)

                def body(b, i, last):
                    for c in range(N4):
                        if c + 1 < N4 or not last:
                            exps(i, c + 1)
                        copy_near(i, c)

                each_pair(act, lambda b, i: exps(i, 0), body)

            @block.vector
            def _(dve):
                def maxima(i, c):
                    dve.wait_ge(s_ready, after(i * N4 + (c + 1)))
                    dve.tensor_reduce(neg[:, c % 4, :], k.ps[:, 2 * (c % 2):2 * (c % 2) + 2, :].rearrange(
                        "p b (h n) -> p (b h) n", h=2), AX.X, ALU.max, negate=True).then_inc(max_done, 1)

                def copy_far(i, c):
                    dve.wait_ge(far_turned, after(i * N4 + (c + 1)))
                    dve.wait_ge(o_ready, after(i * N4 + (c - 1)))
                    dve.tensor_copy(pT[:, c % 2, 4:8, :].rearrange("p a n -> p (a n)"), k.ps[:, 5, :]
                                    ).then_inc(far_copied, 1)

                def normal(i, c):
                    u, half = c // 2, c % 2
                    dve.wait_ge(o_ready, after(i * N4 + (c + 1)))
                    dve.reciprocal(inv[:, c % 2, :], rs[:, c, :]).then_inc(inverse_done, 1)
                    dve.wait_ge(inverse_done, after(i * N4 + (c + 1)))
                    dve.tensor_tensor(
                        O[:, 2 * half:2 * half + 2, bass.ds(2 * i + u, 1), :].rearrange(
                            "p a t (h w) -> p (a t) h w", w=LD),
                        k.ps[:, 6 + c % 2, 0:4 * LD].rearrange("p (a h w) -> p a h w", a=2, w=LD),
                        inv[:, c % 2, :].rearrange("p (a h) -> p a h", a=2).unsqueeze(3).to_broadcast([P, 2, 2, LD]),
                        ALU.mult).then_inc(o_done, 1)

                def before(b, i):
                    maxima(i, 0)
                    maxima(i, 1)

                def body(b, i, last):
                    for c in range(N4):
                        if c + 2 < N4 or not last:
                            maxima(i, c + 2)
                        copy_far(i, c)
                        if c:
                            normal(i, c - 1)
                    normal(i, N4 - 1)

                each_pair(dve, before, body)


def layer2_ffn(nc, k, a):
    with ExitStack() as held:
        y = tiles(nc, held)("y_rows", [P, T, D])
        kept = nc.dram_tensor("kept_x", (P, T * D), F32).ap()
        layer_norm_rows(nc, k, k.x, y, None, keep=kept)
        for layer in range(2):
            with ExitStack() as outer:
                O = tiles(nc, outer)("O", [P, 4, T, P])
                with ExitStack() as inner:
                    sb = tiles(nc, inner)
                    QT, KT = sb("QT", [P, 4, TOK + P]), sb("KT", [P, 4, TOK + P])
                    V = sb("V", [P, 4, T + 1, P])
                    flat = O[:, :, :, :].rearrange("p a t n -> p (a t n)")
                    h = flat[:, 0:T * D].rearrange("p (t d) -> p t d", d=D)
                    ws = flat[:, T * D:T * D + KD * 3 * LW].rearrange("p (c n) -> p c n", c=KD)
                    bb = flat[:, T * D + KD * 3 * LW:T * D + KD * 3 * LW + 2 * LW].rearrange("p (h w) -> p h w", w=LD)
                    ab = k.x[:, :, :].rearrange("p (j t) d -> p j (t d)", j=4).rearrange("p j (h w) -> p j h w", w=LD)
                    mask = sb("mask", [P, 2, 2, 2 * P], BF16)
                    ident16 = sb("ident16", [P, P], BF16)
                    local_qkv(nc, k, a, layer, y, h, ws, bb, ab, QT, KT, V, mask, ident16)
                    local_attention(nc, k, QT, KT, V, O, mask, ident16)
                out_project(nc, k, O, a["L2_ffn_wo"][layer], None, y)
            with ExitStack() as inner:
                h = tiles(nc, inner)("h", [P, T, D])
                shift_rows(nc, k, y, h)
                C = f"L2_ffn_{layer}_"
                ffn(nc, k, h, y, a["L2_ffn_w1"][layer], a["L2_ffn_w2"][layer],
                    (k.col(C + "ln_g"), k.col(C + "ln_b")), k.col(C + "b1"), a["L2_ffn_b2"][layer:layer + 1, :], glu=True,
                    meanwhile=(k.x[:, :, :].rearrange("p t d -> p (t d)"), kept) if layer == 1 else None)
        add_rows(nc, k, y)



E = 8


def layer0_ffn(nc, k, a):
    NT = 4
    NF = 2
    with ExitStack() as held:
        sb = tiles(nc, held)
        norm = sb("norm", [P, 11, T])
        xn = sb("xn", [P, GT, D])
        xT = sb("xT", [P, KD, GN])
        bias_cols = k.col("L0_ffn_gate_up_proj_bias")
        gu = [sb(f"gu{e}", [P, KD, 4 * P]) for e in range(2)]
        dn = [sb(f"dn{e}", [P, NF, D]) for e in range(2)]
        gate, up, sig = (sb(n, [P, NF, GN]) for n in ("gate", "up", "sig"))
        inter = sb("inter", [P, 2, NF, GN])
        idx, idf = sb("idx", [P, NT, 2], I32), sb("idf", [P, NT, 2])
        rw = sb("rw", [P, NT, E])
        pick = sb("pick", [P, 2, NT, E])
        weight = sb("weight", [P, NT, E])
        weightT = sb("weightT", [E, NT, P])
        bd = sb("bd", [E, D])
        psT = k.ps[:, 0:2, :]
        with stage(nc, "loaded", "normed", "turned", "copied", "h_ready", "picked", "weights_turned",
                   "weights_copied", "y_ready", "norm_step") as (
                block, loaded, normed, turned, copied, h_ready, picked, weights_turned, weights_copied, y_ready,
                norm_step):
            @block.sync
            def _(sp):
                sp.dma_start(idx[:, :, :], a["L0_ffn_router_indices"].rearrange("(t p) k -> p t k", p=P)
                             ).then_inc(loaded, 16)
                sp.dma_start(rw[:, :, :], a["L0_ffn_routing_weights"].rearrange("(t p) e -> p t e", p=P)
                             ).then_inc(loaded, 16)
                sp.dma_start(bd[:, :], a["L0_ffn_down_proj_bias"]).then_inc(loaded, 16)
                sp.wait_ge(loaded, after(48))

            @block.vector
            def _(dve):
                row_norms(dve, Chain(dve, norm_step), k.x, norm, 0, NT)
                normalise_group(dve, 0, xn, k.x, norm, turned, normed)
                step = Chain(dve, picked)
                dve.wait_ge(loaded, after(48))
                step(dve.tensor_copy(idf[:, :, :], idx[:, :, :]))
                for j in range(2):
                    ins = dve.tensor_tensor(pick[:, j], idf[:, :, j:j + 1].to_broadcast([P, NT, E]),
                                            k.eidx[:, :].unsqueeze(1).to_broadcast([P, NT, E]), ALU.is_equal)
                    step(ins)
                step(dve.tensor_tensor(pick[:, 0], pick[:, 0], pick[:, 1], ALU.add))
                step(dve.tensor_tensor(weight[:, :, :], pick[:, 0], rw[:, :, :], ALU.mult))
                dve.wait_ge(weights_turned, after(1))
                dve.tensor_copy(weightT[:, :, :].rearrange("p t n -> p (t n)"), k.ps[0:E, 2, :]).then_inc(weights_copied, 1)
                for t in range(NT):
                    dve.wait_ge(y_ready, after(t + 1))
                    dve.tensor_tensor(k.x[:, t, :], k.x[:, t, :], k.ps[:, 3 + t, 0:D], ALU.add)

            @block.tensor
            def _(pe):
                turn_group(pe, 0, k, xn, psT, normed, turned, copied, 1)
                pe.wait_ge(picked, after(5))
                for t in range(NT):
                    mm = pe.transpose(k.ps[0:E, 2, t * P:(t + 1) * P], weight[:, t, :], k.ident[:, :])
                mm.then_inc(weights_turned, 1)
                pe.wait_ge(weights_copied, after(1))
                pe.wait_ge(loaded, after(48))
                for t in range(NT):
                    pe.matmul(k.ps[:, 3 + t, 0:D], weightT[:, t, :], bd[:, :], start=True, stop=True).then_inc(y_ready, 1)

            @block.scalar
            def _(act):
                copy_group(act, 0, [xT], psT, [None], turned, copied, h_ready, 1)

        with stage(nc, "first_loaded", "second_loaded", "h_ready", "h_read", "gate_ready", "up_ready", "sig_ready",
                   "prod_ready", "inter_done", "y_ready", "y_added") as (
                block, first_loaded, second_loaded, h_ready, h_read, gate_ready, up_ready, sig_ready,
                prod_ready, inter_done, y_ready, y_added):
            w_loaded = (first_loaded, second_loaded)

            @block.sync
            def _(sp):
                with sp.Fori(0, E // 2) as i:
                    for e in range(2):
                        sp.wait_ge(y_ready, after(2 * NT * i))
                        sp.dma_start(gu[e][:, :, :], a["L0_ffn_gate_up_proj"][bass.ds(2 * i + e, 1)].rearrange(
                            "e (c p) f -> p (e c) f", p=P)).then_inc(w_loaded[e], 16)
                        sp.dma_start(dn[e][:, :, :], a["L0_ffn_down_proj"][bass.ds(2 * i + e, 1)].rearrange(
                            "e (c p) f -> p (e c) f", p=P)).then_inc(w_loaded[e], 16)

            @block.tensor
            def _(pe):
                def hidden(i, e):
                    pe.wait_ge(w_loaded[e], after(32 * (i + 1)))
                    for f in range(NF):
                        pe.wait_ge(h_read, after(2 * NF * i + (NF * e + f - 1)))
                        for half in range(2):
                            for c in range(KD):
                                at = (NF * half + f) * P
                                mm = pe.matmul(k.ps[:, 2 * f + half, :], gu[e][:, c, at:at + P], xT[:, c, :],
                                               start=(c == 0), stop=(c == KD - 1))
                        mm.then_inc(h_ready, 1)

                def down(i, e):
                    pe.wait_ge(inter_done, after(2 * NF * i + NF * (e + 1)))
                    for t in range(NT):
                        pe.wait_ge(y_added, after(2 * NT * i + (NT * e + t - 3)))
                        for f in range(NF):
                            mm = pe.matmul(k.ps[:, 4 + t, 0:D], inter[:, e, f, t * P:(t + 1) * P], dn[e][:, f, :],
                                           start=(f == 0), stop=(f == NF - 1))
                        mm.then_inc(y_ready, 1)

                with pe.Fori(0, E // 2) as i:
                    hidden(i, 0)
                    hidden(i, 1)
                    down(i, 0)
                    down(i, 1)

            @block.vector
            def _(dve):
                def gates(i, e):
                    dve.wait_ge(inter_done, after(2 * NF * i + NF * e))
                    for f in range(NF):
                        n = 2 * NF * i + NF * e + f
                        col = lambda half: bias_cols[:, bass.ds((2 * i + e) * 4 + NF * half + f, 1)]
                        dve.wait_ge(h_ready, after(n + 1))
                        dve.tensor_scalar(gate[:, f, :], k.ps[:, 2 * f, :], col(0), 7.0, ALU.add,
                                          ALU.min).then_inc(gate_ready, 1)
                        dve.tensor_scalar(up[:, f, :], k.ps[:, 2 * f + 1, :], col(1), 7.0, ALU.add,
                                          ALU.min).then_inc(h_read, 1)
                        dve.wait_ge(h_read, after(n + 1))
                        dve.tensor_scalar(up[:, f, :], up[:, f, :], -7.0, 1.0, ALU.max, ALU.add).then_inc(up_ready, 1)
                    for f in range(NF):
                        n = 2 * NF * i + NF * e + f
                        dve.wait_ge(sig_ready, after(n + 1))
                        dve.wait_ge(prod_ready, after(n + 1))
                        dve.tensor_tensor(inter[:, e, f, :], up[:, f, :], sig[:, f, :], ALU.mult).then_inc(inter_done, 1)

                with dve.Fori(0, E // 2) as i:
                    gates(i, 0)
                    gates(i, 1)
                    for e in range(2):
                        for t in range(NT):
                            dve.wait_ge(y_ready, after(2 * NT * i + (NT * e + t + 1)))
                            row = k.x[:, t, :]
                            dve.scalar_tensor_tensor(out=row, in0=k.ps[:, 4 + t, 0:D],
                                                     scalar=weight[:, t, bass.ds(2 * i + e, 1)], in1=row,
                                                     op0=ALU.mult, op1=ALU.add).then_inc(y_added, 1)

            @block.gpsimd
            def _(pool):
                with pool.Fori(0, E // 2) as i:
                    for m in range(2 * NF):
                        pool.wait_ge(up_ready, after(2 * NF * i + (m + 1)))
                        u = up[:, m % NF, :]
                        pool.tensor_tensor(u, u, gate[:, m % NF, :], ALU.mult).then_inc(prod_ready, 1)

            @block.scalar
            def _(act):
                with act.Fori(0, E // 2) as i:
                    for m in range(2 * NF):
                        act.wait_ge(gate_ready, after(2 * NF * i + (m + 1)))
                        act.wait_ge(inter_done, after(2 * NF * i + (m - 1)))
                        act.activation(sig[:, m % NF, :], gate[:, m % NF, :], ACT.Sigmoid,
                                       scale=1.702).then_inc(sig_ready, 1)



def route(nc, k, rows, wg, cap, top, slots, gather_at, scatter_at, weights, sent, zeros):
    with ExitStack() as held:
        sb = tiles(nc, held)
        wgs = sb("wgs", [P, KD, E])
        xn = sb("xn", [P, GT, D])
        xT = sb("xT", [P, KD, GN])
        psT = k.ps[:, 0:2, :]
        with stage(nc, "w_loaded", "normed", "turned", "copied", "logits_ready", "zeroed", "filled") as (
                block, w_loaded, normed, turned, copied, logits_ready, zeroed, filled):
            @block.gpsimd
            def _(pool):
                pool.memset(zeros[:, :], 0.0).then_inc(zeroed, 1)

            @block.sync
            def _(sp):
                sp.dma_start(wgs[:, :, :], turned_weights(wg)).then_inc(w_loaded, 16)
                width = zeros.shape[1]
                n = slots * D // P // width
                sp.wait_ge(zeroed, after(1))
                for j in range(n):
                    sp.dma_start(sent[0:slots, :].rearrange("(p r) d -> p (r d)", p=P)[:, j * width:(j + 1) * width],
                                 zeros[:, :]).then_inc(filled, 16)
                sp.wait_ge(filled, after(16 * n))

            @block.vector
            def _(dve):
                with dve.Fori(0, G) as g:
                    normalise_group(dve, g, xn, rows, None, turned, normed)

            @block.scalar
            def _(act):
                with act.Fori(0, G) as g:
                    copy_group(act, g, [xT], psT, [None], turned, copied, logits_ready, GT)

            @block.tensor
            def _(pe):
                pe.wait_ge(w_loaded, after(16))
                with pe.Fori(0, G) as g:
                    turn_group(pe, g, k, xn, psT, normed, turned, copied, 1)
                    pe.wait_ge(copied, after((g + 1) * 2))
                    for u in range(GT):
                        for c in range(KD):
                            mm = pe.matmul(k.ps[:, 2, bass.ds((g * GT + u) * E, E)], xT[:, c, u * P:(u + 1) * P],
                                           wgs[:, c, :], start=(c == 0), stop=(c == KD - 1))
                        mm.then_inc(logits_ready, 1)

        lg = sb("lg", [P, T, E])
        less = sb("less", [P, T, E])
        cand = sb("cand", [P, T, E])
        oh = sb("oh", [P, top, T, E])
        best, first = sb("best", [P, 2, T]), sb("first", [P, 2, T])
        e8 = sb("e8", [P, E])
        gate = sb("gate", [P, 2, T])
        dif, den = sb("dif", [P, T]), sb("den", [P, T])
        total = sb("total", [P, E])
        all_total = sb("all_total", [P, T, E])
        spare = sb("spare", [P, top, T])
        rank, keep, slot = (sb(n, [P, T]) for n in ("rank", "keep", "slot"))
        wide = lambda v: v.unsqueeze(2).to_broadcast([P, T, E])
        experts = lambda v: v.unsqueeze(1).to_broadcast([P, T, E])
        flat = lambda v: v.rearrange("p t e -> p (t e)")
        with stage(nc, "dve_step", "exp_asked", "exp_done", "chosen", "ranked", "spare_made") as (
                block, dve_step, exp_asked, exp_done, chosen, ranked, spare_made):
            @block.gpsimd
            def _(pool):
                pool.iota(spare[:, :, :], pattern=[[TOK, top], [P, T]], base=slots, channel_multiplier=1,
                          allow_small_or_imprecise_dtypes=True).then_inc(spare_made, 1)

            @block.vector
            def _(dve):
                step = Chain(dve, dve_step)

                def first_best(values, j):
                    step(dve.tensor_reduce(best[:, j, :], values, AX.X, ALU.max))
                    step(dve.tensor_tensor(cand[:, :, :], values, wide(best[:, j, :]), ALU.is_equal))
                    step(dve.tensor_tensor(cand[:, :, :], cand[:, :, :], experts(e8[:, :]), ALU.mult))
                    step(dve.tensor_reduce(first[:, j, :], cand[:, :, :], AX.X, ALU.min))
                    step(dve.tensor_tensor(oh[:, j], experts(e8[:, :]), wide(first[:, j, :]), ALU.is_equal))

                step(dve.tensor_scalar(e8[:, :], k.eidx[:, :], -8.0, None, ALU.add))
                step(dve.tensor_copy(flat(lg[:, :, :]), k.ps[:, 2, 0:T * E]))
                if top == 2:
                    first_best(lg[:, :, :], 0)
                    step(dve.scalar_tensor_tensor(out=less[:, :, :], in0=oh[:, 0], scalar=NEG, in1=lg[:, :, :],
                                                  op0=ALU.mult, op1=ALU.add))
                    first_best(less[:, :, :], 1)
                    dve.tensor_tensor(dif[:, :], best[:, 1, :], best[:, 0, :], ALU.subtract).then_inc(exp_asked, 1)
                    step(dve.tensor_reduce(total[:, :], oh[:, 0].rearrange("p t e -> p e t"), AX.X, ALU.add))
                    dve.tensor_copy(all_total[:, :, :], experts(total[:, :])).then_inc(chosen, 1)
                    dve.wait_ge(exp_done, after(1))
                    step(dve.tensor_scalar(den[:, :], gate[:, 1, :], 1.0, None, ALU.add))
                    step(dve.reciprocal(gate[:, 0, :], den[:, :]))
                    step(dve.tensor_tensor(gate[:, 1, :], gate[:, 1, :], gate[:, 0, :], ALU.mult))
                else:
                    step(dve.tensor_reduce(best[:, 0, :], lg[:, :, :], AX.X, ALU.max))
                    dve.tensor_tensor(lg[:, :, :], lg[:, :, :], wide(best[:, 0, :]), ALU.subtract).then_inc(exp_asked, 1)
                    dve.wait_ge(exp_done, after(1))
                    step(dve.tensor_reduce(den[:, :], less[:, :, :], AX.X, ALU.add))
                    step(dve.reciprocal(dif[:, :], den[:, :]))
                    step(dve.tensor_tensor(less[:, :, :], less[:, :, :], wide(dif[:, :]), ALU.mult))
                    first_best(less[:, :, :], 0)
                    step(dve.tensor_copy(gate[:, 0, :], best[:, 0, :]))
                    dve.tensor_copy(den[:, :], best[:, 0, :]).then_inc(chosen, 1)
                dve.wait_ge(spare_made, after(1))
                for j in range(top):
                    dve.wait_ge(ranked, after(j + 1))
                    step(dve.tensor_tensor(flat(cand[:, :, :]), k.ps[:, 3 + j, 0:T * E], flat(oh[:, j]), ALU.mult))
                    step(dve.tensor_reduce(rank[:, :], cand[:, :, :], AX.X, ALU.add))
                    step(dve.tensor_scalar(keep[:, :], rank[:, :], float(cap), None, ALU.is_lt))
                    step(dve.tensor_tensor(weights[:, j, :], gate[:, j, :], keep[:, :], ALU.mult))
                    step(dve.tensor_scalar(slot[:, :], first[:, j, :], 8.0, float(cap), ALU.add, ALU.mult))
                    step(dve.tensor_tensor(slot[:, :], slot[:, :], rank[:, :], ALU.add))
                    step(dve.tensor_tensor(slot[:, :], slot[:, :], keep[:, :], ALU.mult))
                    step(dve.tensor_copy(gather_at[:, j, :], slot[:, :]))
                    step(dve.tensor_scalar(keep[:, :], keep[:, :], -1.0, 1.0, ALU.mult, ALU.add))
                    step(dve.tensor_tensor(keep[:, :], keep[:, :], spare[:, j, :], ALU.mult))
                    step(dve.tensor_tensor(slot[:, :], slot[:, :], keep[:, :], ALU.add))
                    step(dve.tensor_copy(scatter_at[:, j, :], slot[:, :]))

            @block.scalar
            def _(act):
                act.wait_ge(exp_asked, after(1))
                if top == 2:
                    act.activation(gate[:, 1, :], dif[:, :], ACT.Exp).then_inc(exp_done, 1)
                else:
                    act.activation(less[:, :, :], lg[:, :, :], ACT.Exp).then_inc(exp_done, 1)

            @block.tensor
            def _(pe):
                pe.wait_ge(chosen, after(1))
                for j in range(top):
                    mine = flat(oh[:, j])
                    out = k.ps[:, 3 + j, :]
                    pe.matmul(out[:, 0:T * E], k.upper[:, :], mine, start=True, stop=False)
                    if j:
                        pe.matmul(out[:, 0:T * E], k.ones[:, :], flat(all_total[:, :, :]), start=False, stop=False)
                    for s in range(1, T):
                        mm = pe.matmul(out[:, s * E:T * E], k.ones[:, :], mine[:, 0:(T - s) * E], start=False,
                                       stop=(s == T - 1))
                    mm.then_inc(ranked, 1)


def run_experts(nc, k, sent, made, w1, w2, cap, b1, b2):
    NU = cap // P
    parts = 1 if cap <= 512 else 2
    CN = cap // parts
    NB = w2.shape[1] // P
    HN = parts * NB
    BANKS, RING = 3, 4
    pairs = [(u, min(2, NU - u)) for u in range(0, NU, 2)]
    NPR = len(pairs)
    W = NB * P // 2
    pieces = [(0, c, slice(m * W, (m + 1) * W)) for c in range(KD) for m in range(2)]
    W1P = len(pieces)
    pieces += [(1, slice(j, j + 2), slice(0, D)) for j in range(0, NB, 2)]
    NP = len(pieces)
    with ExitStack() as held:
        sb = tiles(nc, held)
        raw = [(sb(f"w1s{e}", [P, KD, NB * P]), sb(f"w2s{e}", [P, NB, D])) for e in range(2)]
        high = [(sb(f"w1h{e}", [P, KD, NB * P], F32R), sb(f"w2h{e}", [P, NB, D], F32R)) for e in range(2)]
        low = [(sb(f"w1l{e}", [P, KD, NB * P], F32R), sb(f"w2l{e}", [P, NB, D], F32R)) for e in range(2)]
        xs = [sb(f"xs{e}", [P, NU, D]) for e in range(2)]
        b2s = [sb(f"b2s{e}", [P, D]) for e in range(2)] if b2 is not None else None
        xT, xh, xl = (sb(n, [P, KD, cap], t) for n, t in (("xT", F32), ("xh", F32R), ("xl", F32R)))
        hw = sb("hw", [P, RING, CN])
        hh, hl = sb("hh", [P, NB, cap], F32R), sb("hl", [P, NB, cap], F32R)
        ys = [sb(f"ys{e}", [P, NU, D]) for e in range(2)]
        with stage(nc, "even_w_loaded", "odd_w_loaded", "even_x_loaded", "odd_x_loaded", "even_b_loaded", "odd_b_loaded", "w_high", "w_low",
                   "turned", "copied", "x_high", "x_split", "h_ready", "h_done", "h_high", "h_split", "y_ready",
                   "y_copied", "stored") as (
                block, even_w_loaded, odd_w_loaded, even_x_loaded, odd_x_loaded, even_b_loaded, odd_b_loaded, w_high, w_low,
                turned, copied, x_high, x_split, h_ready, h_done, h_high, h_split, y_ready, y_copied, stored):
            w_loaded = (even_w_loaded, odd_w_loaded)
            x_loaded, b_loaded = (even_x_loaded, odd_x_loaded), (even_b_loaded, odd_b_loaded)

            def each_expert(eng, body):
                with eng.Fori(0, E // 2 - 1) as i:
                    for e in range(2):
                        body(i, e, 2 * i + e, False)
                for e in range(2):
                    body(E // 2 - 1, e, E - 2 + e, e == 1)

            @block.sync
            def _(sp):
                def load_rows(n, e):
                    sp.dma_start(xs[e][:, :, :], sent[bass.ds(n * cap, cap), :].rearrange(
                        "(p u) d -> p u d", u=NU)).then_inc(x_loaded[e], 16)

                def load_weights(n, e):
                    for w, src in zip(raw[e], (w1, w2)):
                        sp.dma_start(w[:, :, :], src[bass.ds(n, 1)].rearrange("e (c p) f -> p (e c) f", p=P)
                                     ).then_inc(w_loaded[e], 16)

                def load_bias(n, e):
                    if b2 is not None:
                        sp.dma_start(b2s[e][:, :], b2[bass.ds(n, 1), :].to_broadcast([P, D])).then_inc(b_loaded[e], 16)

                def store(n, e):
                    sp.wait_ge(y_copied, after(NU * (n + 1)))
                    sp.dma_start(made[bass.ds(n * cap, cap), :].rearrange("(p u) d -> p u d", u=NU),
                                 ys[e][:, :, :]).then_inc(stored, 16)

                for e in range(2):
                    load_rows(e, e)
                    load_weights(e, e)
                    load_bias(e, e)
                with sp.Fori(0, E // 2 - 1) as i:
                    for e in range(2):
                        n = 2 * i + e
                        sp.wait_ge(w_low, after(NP * (n + 1)))
                        load_weights(n + 2, e)
                        sp.wait_ge(h_ready, after(HN * (n + 1)))
                        load_rows(n + 2, e)
                        store(n, e)
                        load_bias(n + 2, e)
                for e in range(2):
                    store(E - 2 + e, e)
                sp.wait_ge(stored, after(16 * E))

            @block.tensor
            def _(pe):
                def turn(n, e):
                    for j, (u, m) in enumerate(pairs):
                        pe.wait_ge(copied, after(NPR * n + slot_free(j, NPR, 2)))
                        for v in range(m):
                            for c in range(KD):
                                mm = pe.transpose(k.ps[:, j % 2, (c * m + v) * P:(c * m + v + 1) * P],
                                                  xs[e][:, u + v, c * P:(c + 1) * P], k.ident[:, :])
                        mm.then_inc(turned, 1)

                def body(i, e, n, last):
                    pe.wait_ge(w_low, after(NP * n + W1P))
                    pe.wait_ge(x_split, after(n + 1))
                    for m in range(HN):
                        at, j = m // NB * CN, m % NB
                        pe.wait_ge(h_done, after(HN * n + slot_free(m, HN, BANKS)))
                        for c in range(KD):
                            b = slice(j * P, (j + 1) * P)
                            mm = product(pe, k.ps[:, 2 + m % BANKS, 0:CN], (high[e][0][:, c, b], low[e][0][:, c, b]),
                                         (xh[:, c, at:at + CN], xl[:, c, at:at + CN]),
                                         start=(c == 0), stop=(c == KD - 1))
                        mm.then_inc(h_ready, 1)
                    if not last:
                        pe.wait_ge(x_loaded[1 - e], after(16 * (i + 1 + e)))
                        turn(n + 1, 1 - e)
                    pe.wait_ge(w_low, after(NP * (n + 1)))
                    pe.wait_ge(h_split, after(HN * (n + 1)))
                    for u in range(NU):
                        pe.wait_ge(y_copied, after(NU * n + slot_free(u, NU, 3)))
                        for j in range(NB):
                            b = slice(u * P, (u + 1) * P)
                            mm = product(pe, k.ps[:, 5 + u % 3, 0:D], (hh[:, j, b], hl[:, j, b]),
                                         (high[e][1][:, j, :], low[e][1][:, j, :]), start=(j == 0), stop=(j == NB - 1))
                        mm.then_inc(y_ready, 1)

                pe.wait_ge(x_loaded[0], after(16))
                turn(0, 0)
                each_expert(pe, body)

            @block.scalar
            def _(act):
                def high_piece(q, e):
                    w, a, b = pieces[q]
                    act.activation(high[e][w][:, a, b], raw[e][w][:, a, b], ACT.Copy).then_inc(w_high, 1)

                def body(i, e, n, last):
                    for m in range(HN):
                        j = m % NB
                        act.wait_ge(h_ready, after(HN * n + (m + 1)))
                        act.wait_ge(h_split, after(HN * n + (m - RING + 1)))
                        bias = 0.0 if b1 is None else b1[:, bass.ds(n * NB + j, 1)]
                        act.activation(hw[:, m % RING, :], k.ps[:, 2 + m % BANKS, 0:CN],
                                       ACT.Gelu if b1 is None else ACT.Relu, bias=bias).then_inc(h_done, 1)
                        if m < NP and not last:
                            if m == 0:
                                act.wait_ge(w_loaded[1 - e], after(32 * (i + 1 + e)))
                                act.wait_ge(y_ready, after(NU * n))
                            high_piece(m, 1 - e)

                act.wait_ge(w_loaded[0], after(32))
                for q in range(NP):
                    high_piece(q, 0)
                each_expert(act, body)

            @block.gpsimd
            def _(pool):
                def low_pieces(n, e):
                    for q, (w, a, b) in enumerate(pieces):
                        pool.wait_ge(w_high, after(NP * n + (q + 1)))
                        low_part(pool, low[e][w][:, a, b], raw[e][w][:, a, b], high[e][w][:, a, b]).then_inc(w_low, 1)

                low_pieces(0, 0)
                each_expert(pool, lambda i, e, n, last: None if last else low_pieces(n + 1, 1 - e))

            @block.vector
            def _(dve):
                def split_x(n):
                    for j, (u, m) in enumerate(pairs):
                        dve.wait_ge(turned, after(NPR * n + (j + 1)))
                        if j == 0:
                            dve.wait_ge(h_ready, after(HN * n))
                        dve.tensor_copy(xT[:, :, u * P:(u + m) * P], k.ps[:, j % 2, 0:KD * m * P].rearrange(
                            "p (c n) -> p c n", c=KD)).then_inc(copied, 1)
                    dve.wait_ge(copied, after(NPR * (n + 1)))
                    dve.tensor_copy(xh[:, :, :], xT[:, :, :]).then_inc(x_high, 1)
                    dve.wait_ge(x_high, after(n + 1))
                    low_part(dve, xl[:, :, :], xT[:, :, :], xh[:, :, :]).then_inc(x_split, 1)

                def body(i, e, n, last):
                    dve.wait_ge(y_ready, after(NU * n))
                    for m in range(HN):
                        at, j = m // NB * CN, m % NB
                        h, whole = hh[:, j, at:at + CN], hw[:, m % RING, :]
                        dve.wait_ge(h_done, after(HN * n + (m + 1)))
                        dve.tensor_copy(h, whole).then_inc(h_high, 1)
                        dve.wait_ge(h_high, after(HN * n + (m + 1)))
                        low_part(dve, hl[:, j, at:at + CN], whole, h).then_inc(h_split, 1)
                    if not last:
                        split_x(n + 1)
                    dve.wait_ge(stored, after(16 * 2 * i))
                    if b2 is not None:
                        dve.wait_ge(b_loaded[e], after(16 * (i + 1)))
                    for u in range(NU):
                        dve.wait_ge(y_ready, after(NU * n + (u + 1)))
                        psY = k.ps[:, 5 + u % 3, 0:D]
                        if b2 is None:
                            dve.tensor_copy(ys[e][:, u, :], psY).then_inc(y_copied, 1)
                        else:
                            dve.tensor_tensor(ys[e][:, u, :], psY, b2s[e][:, :], ALU.add).then_inc(y_copied, 1)

                split_x(0)
                each_expert(dve, body)


def mixture(nc, k, wg, w1, w2, cap, top, b1=None, b2=None):
    slots = E * cap
    ID = nc.next_id()
    sent = nc.dram_tensor(f"sent_{ID}", (slots + top * TOK, D), F32).ap()
    made = nc.dram_tensor(f"made_{ID}", (slots, D), F32).ap()
    rows_sent, *rows_fetched = k.mixture_sems[top]
    with ExitStack() as held:
        sb = tiles(nc, held)
        gather_at, scatter_at = (sb(n, [P, top, T], U32) for n in ("gather_at", "scatter_at"))
        weights = sb("weights", [P, top, T])
        with ExitStack() as inner:
            sb2 = tiles(nc, inner)
            rows = sb2("rows", [P, T, D])
            zeros = sb2("zeros", [P, 2048])
            layer_norm_rows(nc, k, k.x, rows, None)
            route(nc, k, rows, wg, cap, top, slots, gather_at, scatter_at, weights, sent, zeros)
            with stage(nc) as (block,):
                @block.gpsimd
                def _(pool):
                    for j in range(top):
                        for t in range(T):
                            pool.indirect_dma_start(
                                sent, bass.IndirectOffsetOnAxis(ap=scatter_at[:, j, t:t + 1], axis=0),
                                rows[:, t, :], None).then_inc(rows_sent, 16)
                    pool.wait_ge(rows_sent, 16 * top * T)
        run_experts(nc, k, sent, made, w1, w2, cap, b1, b2)
        back = sb("back", [P, top, T, D])
        with stage(nc, "added") as (block, added):
            @block.gpsimd
            def _(pool):
                for t in range(T):
                    for j in range(top):
                        pool.indirect_dma_start(
                            back[:, j, t, :], None, made,
                            bass.IndirectOffsetOnAxis(ap=gather_at[:, j, t:t + 1], axis=0)).then_inc(rows_fetched[t // GT], 16)

            @block.vector
            def _(dve):
                for g in range(G):
                    dve.wait_ge(rows_fetched[g], 16 * top * GT)
                    for j in range(top):
                        if j:
                            dve.wait_ge(added, after(g + 1))
                        for u in range(GT):
                            t = g * GT + u
                            row = k.x[:, t, :]
                            ins = dve.scalar_tensor_tensor(out=row, in0=back[:, j, t, :], scalar=weights[:, j, t:t + 1], in1=row,
                                                           op0=ALU.mult, op1=ALU.add)
                        if j == 0:
                            ins.then_inc(added, 1)


def layer1_ffn(nc, k, a):
    w1, w2 = a["L1_ffn_c_fc"], a["L1_ffn_c_proj"]
    cap = 2 * TOK * 5 // 4 // E
    cap += cap % 2
    mixture(nc, k, a["L1_ffn_w_g"], w1, w2, cap, 2)


def layer3_ffn(nc, k, a):
    mixture(nc, k, a["L3_ffn_wg"], a["L3_ffn_w1"], a["L3_ffn_w2"], TOK // E, 1, k.col("L3_ffn_b1"), a["L3_ffn_b2"])


LAYERS = [layer0_attention, layer0_ffn, layer1_attention, layer1_ffn, layer2_attention, layer2_ffn, layer3_attention,
          layer3_ffn]

COLUMNS = [("L0_xattn_bq", 2), ("L0_xattn_bk", 2)]
COLUMNS += [("L1_xattn_" + n, w) for n, w in [
    ("a1_lnx_g", 2), ("a1_lnx_b", 2), ("a1_lny_g", 2), ("a1_lny_b", 2), ("a1_ln3_g", 2), ("a1_ln3_b", 2),
    ("a1_li2_b", 8), ("a2_lnx_g", 2), ("a2_lnx_b", 2), ("a2_lny_g", 1), ("a2_lny_b", 1), ("a2_ln3_g", 2),
    ("a2_ln3_b", 2), ("a2_li2_b", 8)]]

COLUMNS += [("L0_ffn_gate_up_proj_bias", 32), ("L3_xattn_bq", 2), ("L3_xattn_bk", 2), ("L3_ffn_b1", 64)]
COLUMNS += [(f"L2_ffn_{layer}_{n}", w) for layer in range(2) for n, w in [("ln_g", 2), ("ln_b", 2), ("b1", 12)]]


def build(nc, a, out, layers=range(8)):
    ncols = sum(n for _, n in COLUMNS)
    with ExitStack() as held:
        sb = tiles(nc, held)

        class K:
            x = sb("x_rows", [P, T, D])
            ctx = sb("ctx_rows", [P, BATCH, IMG])
            ctxT = sb("ctxT", [P, BATCH, CTX])
            cols = sb("cols_sb", [P, ncols])
            ident = sb("ident", [P, P])
            ones = sb("ones", [P, P])
            hm16 = sb("hm16", [P, 8])
            hm32 = sb("hm32", [P, 4])
            vmask = sb("vmask", [P, 5, 3])
            eidx = sb("eidx", [P, 8])
            upper = sb("upper", [P, P])
            ps = held.enter_context(nc.psum_tensor("ps", [P, 8, 512], F32))
            mixture_sems = {top: [held.enter_context(nc.semaphore(f"{n}_top{top}"))
                                  for n in ("rows_sent", *(f"rows_fetched{g}" for g in range(G)))]
                            for top in (1, 2)}

            @staticmethod
            def col(name):
                at = 0
                for n, width in COLUMNS:
                    if n == name:
                        return K.cols[:, at:at + width]
                    at += width
                raise KeyError(name)

        build_constants(nc, K, a["columns"], a["ctx_512"], a["x"])
        for n in layers:
            LAYERS[n](nc, K, a)
        with stage(nc, "stored") as (block, stored):
            @block.sync
            def _(sp):
                sp.dma_start(out.rearrange("b (t p) d -> p (b t) d", p=P), K.x[:, :, :]).then_inc(stored, 16)
                sp.wait_ge(stored, after(16))



def rotary_tables():
    f = np.float32
    half = np.arange(0, LD, 2, dtype=f)
    inv_freq = f(1.0) / f(10000.0) ** (half / f(LD))
    t = np.arange(SEQ, dtype=f)
    freqs = t[:, None] * inv_freq[None, :]
    base = (half + f(0.4 * LD)) / f(1.4 * LD)
    scale = base[None, :] ** ((t - f(SEQ // 2)) / f(P // 2))[:, None]
    cos, sin = np.cos(freqs), np.sin(freqs)
    qc, qs, kc, ks = cos * scale * f(8), sin * scale * f(8), cos / scale, sin / scale
    both = lambda q, kk, sign: np.stack([np.concatenate([sign * q, q], 1), np.concatenate([sign * kk, kk], 1)], 1)
    turn = lambda v: np.ascontiguousarray(v.reshape(TB, P, 2, LD).transpose(1, 0, 2, 3), dtype=f)
    return turn(both(qc, kc, f(1))), turn(both(qs, ks, f(-1)))


def lay_out(inputs):
    a = {n: np.ascontiguousarray(v) for n, v in inputs.items()}
    wkv = a.pop("L2_xattn_Wkv")
    a["L2_xattn_Wk"] = np.ascontiguousarray(wkv[:D].T)
    a["L2_xattn_Wv"] = np.ascontiguousarray(wkv[D:].T)
    for n in ("L2_xattn_Wq", "L2_xattn_Wo"):
        a[n] = np.ascontiguousarray(a[n].T)
    for n in ("a1_wq", "a1_wk", "a1_wv", "a2_wq", "a2_wk", "a2_wv"):
        w = a["L1_xattn_" + n]
        a["L1_xattn_" + n] = np.ascontiguousarray(w.transpose(1, 0, 2).reshape(w.shape[1], -1))
    a["rotary_cos"], a["rotary_sin"] = rotary_tables()
    for n in ("L0_ffn_gate_up_proj", "L0_ffn_gate_up_proj_bias"):
        a[n] = np.ascontiguousarray(np.concatenate([a[n][..., 0::2], a[n][..., 1::2]], axis=-1))
    of = dict(a)
    for layer in range(2):
        for n in ("ln_g", "ln_b"):
            of[f"L2_ffn_{layer}_{n}"] = a[f"L2_ffn_{n}"][layer]
        b1 = a["L2_ffn_b1"][layer].reshape(2, -1)
        of[f"L2_ffn_{layer}_b1"] = np.pad(b1, ((0, 0), (0, -b1.shape[1] % P)))
    vectors = []
    for name, n in COLUMNS:
        v = of[name].reshape(-1)
        vectors.append(v.reshape(n, P).T)
    a["columns"] = np.ascontiguousarray(np.concatenate(vectors, axis=1))
    return a


def kernel(**inputs):
    import concourse.bacc as _bacc
    from concourse.bass_utils import run_bass_kernel_spmd as _run

    arrays = lay_out(inputs)
    nc = _bacc.Bacc("TRN2", target_bir_lowering=False, num_devices=1)
    named = {f"in_{n}": v for n, v in arrays.items()}
    aps = {n: nc.dram_tensor(f"in_{n}", v.shape, mybir.dt.from_np(v.dtype), kind="ExternalInput").ap()
           for n, v in arrays.items()}
    out = nc.dram_tensor("out", (BATCH, SEQ, D), F32, kind="ExternalOutput").ap()
    build(nc, aps, out)
    r = _run(nc, [named], core_ids=[0])
    return r.results[0]["out"]
```
